# Optimizing a Trainium2 kernel written in Bass

```python
import numpy as np
import jax
import jax.numpy as jnp

def _softmax(x, axis=-1):
    return jax.nn.softmax(x, axis=axis)

def _gelu(x):
    return jax.nn.gelu(x, approximate=True)

def _silu(x):
    return jax.nn.silu(x)

def _sigmoid(x):
    return jax.nn.sigmoid(x)

def _layernorm(x, axis=-1, eps=1e-05):
    m = jnp.mean(x, axis=axis, keepdims=True)
    v = jnp.var(x, axis=axis, keepdims=True)
    return (x - m) / jnp.sqrt(v + eps)

def _scatter_add(tgt, idx, src, axis=0):
    return tgt.at[idx].add(src)

def _segment_sum(src, seg, n):
    return jax.ops.segment_sum(src, seg, n)
kernel_name = 'mk_gnn_resnorm_d2_gnn_r8_479746'

def setup_inputs(seed: int=0):
    np.random.seed(seed)
    _w = jnp.asarray

    def _rec_inputs():
        import jax
        import jax.numpy as jnp
        _gk = jax.random.key(seed)
        x = -0.0003713 + 1 * jax.random.normal(jax.random.fold_in(_gk, 1), (6250, 128), jnp.float32)
        _s = jax.random.randint(jax.random.fold_in(_gk, 2), (100000,), 0, 6250, jnp.int32)
        _d = jax.random.randint(jax.random.fold_in(_gk, 3), (100000,), 0, 6250, jnp.int32)
        _loop = jnp.arange(6250, dtype=jnp.int32)
        src = jnp.concatenate([_s, _d, _loop])
        dst = jnp.concatenate([_d, _s, _loop])
        _o = jnp.argsort(dst, stable=True)
        src = src[_o]
        dst = dst[_o]
        edge_attr_128 = -5.16925e-05 + 1.00005 * jax.random.normal(jax.random.fold_in(_gk, 11), (206250, 128), jnp.float32)
        edge_type_8 = jax.random.randint(jax.random.fold_in(_gk, 13), (206250,), 0, 8, jnp.int32)
        return (x, src, dst, edge_attr_128, edge_type_8)
    x, src, dst, edge_attr_128, edge_type_8 = _rec_inputs()

    def _L0_gnn_setup():
        import jax, jax.numpy as jnp
        import numpy as np
        N_ENT = 12500

        def _rgcn_layer(x, W, SW, b, src, dst, rel):
            xt = jnp.einsum('nd,rde->rne', x, W)
            msg = xt[rel, src]
            agg = jax.ops.segment_sum(msg, dst, num_segments=x.shape[0])
            return jax.nn.relu(agg + x @ SW + b)
        key = jax.random.key(seed)
        ks = jax.random.split(key, 8)
        d, R, E = (128, 8, 75000)
        scale = 1.0 / np.sqrt(d)
        return {'entity_emb': jax.random.normal(ks[0], (N_ENT, d), dtype=jnp.float32), 'w1': jax.random.normal(ks[1], (R, d, d), dtype=jnp.float32) * scale, 'sl1': jax.random.normal(ks[2], (d, d), dtype=jnp.float32) * scale, 'b1': jnp.zeros((d,), dtype=jnp.float32), 'w2': jax.random.normal(ks[3], (R, d, d), dtype=jnp.float32) * scale, 'sl2': jax.random.normal(ks[4], (d, d), dtype=jnp.float32) * scale, 'b2': jnp.zeros((d,), dtype=jnp.float32), 'edge_index': jax.random.randint(ks[5], (2, E), 0, N_ENT, dtype=jnp.int64), 'edge_type': jax.random.randint(ks[6], (E,), 0, R, dtype=jnp.int64)}
    _L0_gnn_all = _L0_gnn_setup()
    _L0_gnn_in = {k: v for k, v in _L0_gnn_all.items() if k in ('w1', 'sl1', 'b1', 'w2', 'sl2', 'b2')}
    del _L0_gnn_all

    def _L1_gnn_setup():
        import jax, jax.numpy as jnp
        import numpy as np
        N, E, H, NH, HD = (6250, 100000, 128, 8, 16)

        def _layernorm(x, g, b, eps=1e-05):
            mu = jnp.mean(x, axis=-1, keepdims=True)
            var = jnp.mean(jnp.square(x - mu), axis=-1, keepdims=True)
            return (x - mu) * jax.lax.rsqrt(var + eps) * g + b
        key = jax.random.key(seed)
        ks = jax.random.split(key, 24)
        w = lambda k, shape, s=0.05: jax.random.normal(k, shape, jnp.float32) * s
        return {'x': jax.random.normal(ks[0], (N, H), jnp.float32), 'edge_index': jax.random.randint(ks[1], (2, E), 0, N, dtype=jnp.int64), 'curv': jax.random.normal(ks[2], (E, H), jnp.float32), 'Wq': w(ks[3], (H, H)), 'bq': jnp.zeros((H,), jnp.float32), 'Wk': w(ks[4], (H, H)), 'bk': jnp.zeros((H,), jnp.float32), 'Wv': w(ks[5], (H, H)), 'bv': jnp.zeros((H,), jnp.float32), 'Wo': w(ks[6], (H, H)), 'bo': jnp.zeros((H,), jnp.float32), 'Wc': w(ks[7], (H, NH)), 'bc': jnp.zeros((NH,), jnp.float32), 'W1': w(ks[8], (H, 4 * H)), 'b1': jnp.zeros((4 * H,), jnp.float32), 'W2': w(ks[9], (4 * H, H)), 'b2': jnp.zeros((H,), jnp.float32), 'g1': jnp.ones((H,), jnp.float32), 'be1': jnp.zeros((H,), jnp.float32), 'g2': jnp.ones((H,), jnp.float32), 'be2': jnp.zeros((H,), jnp.float32)}
    _L1_gnn_all = _L1_gnn_setup()
    _L1_gnn_in = {k: v for k, v in _L1_gnn_all.items() if k in ('Wq', 'bq', 'Wk', 'bk', 'Wv', 'bv', 'Wo', 'bo', 'Wc', 'bc', 'W1', 'b1', 'W2', 'b2', 'g1', 'be1', 'g2', 'be2')}
    del _L1_gnn_all
    return {'x': x, 'src': src, 'dst': dst, 'edge_attr_128': edge_attr_128, 'edge_type_8': edge_type_8, 'L0_gnn_w1': _L0_gnn_in['w1'], 'L0_gnn_sl1': _L0_gnn_in['sl1'], 'L0_gnn_b1': _L0_gnn_in['b1'], 'L0_gnn_w2': _L0_gnn_in['w2'], 'L0_gnn_sl2': _L0_gnn_in['sl2'], 'L0_gnn_b2': _L0_gnn_in['b2'], 'L1_gnn_Wq': _L1_gnn_in['Wq'], 'L1_gnn_bq': _L1_gnn_in['bq'], 'L1_gnn_Wk': _L1_gnn_in['Wk'], 'L1_gnn_bk': _L1_gnn_in['bk'], 'L1_gnn_Wv': _L1_gnn_in['Wv'], 'L1_gnn_bv': _L1_gnn_in['bv'], 'L1_gnn_Wo': _L1_gnn_in['Wo'], 'L1_gnn_bo': _L1_gnn_in['bo'], 'L1_gnn_Wc': _L1_gnn_in['Wc'], 'L1_gnn_bc': _L1_gnn_in['bc'], 'L1_gnn_W1': _L1_gnn_in['W1'], 'L1_gnn_b1': _L1_gnn_in['b1'], 'L1_gnn_W2': _L1_gnn_in['W2'], 'L1_gnn_b2': _L1_gnn_in['b2'], 'L1_gnn_g1': _L1_gnn_in['g1'], 'L1_gnn_be1': _L1_gnn_in['be1'], 'L1_gnn_g2': _L1_gnn_in['g2'], 'L1_gnn_be2': _L1_gnn_in['be2']}

def reference(x, src, dst, edge_attr_128, edge_type_8, L0_gnn_w1, L0_gnn_sl1, L0_gnn_b1, L0_gnn_w2, L0_gnn_sl2, L0_gnn_b2, L1_gnn_Wq, L1_gnn_bq, L1_gnn_Wk, L1_gnn_bk, L1_gnn_Wv, L1_gnn_bv, L1_gnn_Wo, L1_gnn_bo, L1_gnn_Wc, L1_gnn_bc, L1_gnn_W1, L1_gnn_b1, L1_gnn_W2, L1_gnn_b2, L1_gnn_g1, L1_gnn_be1, L1_gnn_g2, L1_gnn_be2):
    import jax
    import jax.numpy as jnp

    def _L0_gnn_ref(entity_emb, w1, sl1, b1, w2, sl2, b2, edge_index, edge_type):
        import jax, jax.numpy as jnp
        import numpy as np
        N_ENT = 12500

        def _rgcn_layer(x, W, SW, b, src, dst, rel):
            xt = jnp.einsum('nd,rde->rne', x, W)
            msg = xt[rel, src]
            agg = jax.ops.segment_sum(msg, dst, num_segments=x.shape[0])
            return jax.nn.relu(agg + x @ SW + b)
        src, dst = (edge_index[0], edge_index[1])
        x = _rgcn_layer(entity_emb, w1, sl1, b1, src, dst, edge_type)
        x = _rgcn_layer(x, w2, sl2, b2, src, dst, edge_type)
        return x

    def _L1_gnn_ref(x, edge_index, curv, Wq, bq, Wk, bk, Wv, bv, Wo, bo, Wc, bc, W1, b1, W2, b2, g1, be1, g2, be2):
        import jax, jax.numpy as jnp
        import numpy as np
        N, E, H, NH, HD = (6250, 100000, 128, 8, 16)

        def _layernorm(x, g, b, eps=1e-05):
            mu = jnp.mean(x, axis=-1, keepdims=True)
            var = jnp.mean(jnp.square(x - mu), axis=-1, keepdims=True)
            return (x - mu) * jax.lax.rsqrt(var + eps) * g + b
        num_nodes = x.shape[0]
        src, tgt = (edge_index[0], edge_index[1])
        x_norm = _layernorm(x, g1, be1)
        q = (x_norm @ Wq + bq).reshape(num_nodes, NH, HD)
        k = (x_norm @ Wk + bk).reshape(num_nodes, NH, HD)
        v = (x_norm @ Wv + bv).reshape(num_nodes, NH, HD)
        scores = jnp.einsum('ehd,ehd->eh', q[src], k[tgt]) / np.sqrt(HD).astype(np.float32)
        scores = scores + (curv @ Wc + bc)
        smax = jax.ops.segment_max(scores, tgt, num_segments=num_nodes)
        p = jnp.exp(scores - smax[tgt])
        ssum = jax.ops.segment_sum(p, tgt, num_segments=num_nodes)
        probs = p / ssum[tgt]
        messages = (probs[:, :, None] * v[tgt]).reshape(scores.shape[0], -1)
        out = jnp.zeros_like(x).at[src].add(messages)
        out = out @ Wo + bo
        x = x + out
        x_norm2 = _layernorm(x, g2, be2)
        ffn_out = jax.nn.relu(x_norm2 @ W1 + b1) @ W2 + b2
        return x + ffn_out
    edge_index = jnp.stack([src, dst])
    x = _layernorm(x + _L0_gnn_ref(x, L0_gnn_w1, L0_gnn_sl1, L0_gnn_b1, L0_gnn_w2, L0_gnn_sl2, L0_gnn_b2, edge_index, edge_type_8), axis=-1)
    x = _layernorm(x + _L1_gnn_ref(x, edge_index, edge_attr_128, L1_gnn_Wq, L1_gnn_bq, L1_gnn_Wk, L1_gnn_bk, L1_gnn_Wv, L1_gnn_bv, L1_gnn_Wo, L1_gnn_bo, L1_gnn_Wc, L1_gnn_bc, L1_gnn_W1, L1_gnn_b1, L1_gnn_W2, L1_gnn_b2, L1_gnn_g1, L1_gnn_be1, L1_gnn_g2, L1_gnn_be2), axis=-1)
    return x

_drawn_inputs = setup_inputs


def setup_inputs(seed=0):
    import zlib

    import numpy as np

    out = dict(_drawn_inputs(seed))
    spreads = {'L0_gnn_b1': (0.0, 0.326),
     'L0_gnn_b2': (0.0, 2.0),
     'L1_gnn_bq': (0.0, 2.0),
     'L1_gnn_bk': (0.0, 2.0),
     'L1_gnn_bv': (0.0, 0.1),
     'L1_gnn_bo': (0.0, 0.1),
     'L1_gnn_bc': (0.0, 2.0),
     'L1_gnn_b1': (0.0, 0.1),
     'L1_gnn_b2': (0.0, 0.1),
     'L1_gnn_g1': (1.0, 0.2),
     'L1_gnn_be1': (0.0, 0.51),
     'L1_gnn_g2': (1.0, 0.2),
     'L1_gnn_be2': (0.0, 0.334)}
    factors = {'edge_attr_128': 3.062, 'L1_gnn_Wc': 3.063, 'L1_gnn_Wk': 2.912}
    for name, (base, spread) in spreads.items():
        noise = np.random.default_rng([zlib.crc32(name.encode()), seed]).standard_normal(out[name].shape)
        drawn = base * np.exp(spread * noise) if base else spread * noise
        out[name] = jnp.asarray(drawn.astype(out[name].dtype))
    for name, factor in factors.items():
        out[name] = (out[name] * factor).astype(out[name].dtype)
    return out
```

```python
import concourse.bass as bass
from concourse import mybir
from contextlib import ExitStack

FP32 = mybir.dt.float32
I32 = mybir.dt.int32
ALU = mybir.AluOpType
ACT = mybir.ActivationFunctionType
AX = mybir.AxisListType

P = 128
N = 6250
E = 206250
D = 128
R = 8
H = 8
HD = D // H
FF = 4 * D
W = -(-N // P)
NT = W + W % 2
NP = NT * P
KC = -(-(E // P + W) // P)
K = KC * P
G = 4
SLOTS = 4
TURNS = K // (SLOTS * G)
PAIRS = K // (2 * G)
EP = 125
BIG = 1.0e30
REP = 2 * G
EPS = 1e-5
DUMP = P


class Memory:

    def __init__(self, nc, stack, stage):
        self.nc, self.stack, self.stage = nc, stack, stage
        self.sem_stack, self.sems = stack, []

    def sb(self, name, shape, dt=FP32):
        return self.stack.enter_context(self.nc.sbuf_tensor(self.stage + name, shape, dt))

    def ps(self, name, shape, dt=FP32):
        return self.stack.enter_context(self.nc.psum_tensor(self.stage + name, shape, dt))

    def sem(self, name):
        self.sems.append(self.sem_stack.enter_context(self.nc.semaphore(self.stage + name)))
        return self.sems[-1]


def ring_index(pool, sem, value, passed):
    pool.wait_ge(sem, value)
    pool.sem_inc(passed, 1)


def prepare_edges(nc, m, t, src, dst, rel, x, d):
    dst_i = m.sb("dst_i", [EP, E // EP], I32)
    dst_f = m.sb("dst_f", [EP, E // EP])
    below = m.sb("below", [EP, E // EP])
    limit = m.sb("limit", [P, W + 1])
    count = m.sb("count", [EP, W + 1])
    ones = m.sb("ones_col", [P, 1])
    before = m.sb("before", [P, P])
    last_w = m.sb("last_w", [W, 1])
    wend = m.sb("wend", [W, 2])
    wn = m.sb("wn", [W, 1])
    wni = m.sb("wni", [W, 1], I32)
    wtile = m.sb("wtile", [W, 2])
    wval = m.sb("wval", [W, 3])
    tile_no = m.sb("tile_no", [P, K])
    hot = m.sb("hot", [W, K])
    started = m.sb("started", [W, K])
    tval = m.sb("tval", [P, KC, 3])
    tno = m.sb("tno", [P, KC])
    raw = m.sb("raw", [P, KC])
    start = m.sb("start", [P, KC])
    start_i = m.sb("start_i", [P, KC], I32)
    win_i = m.sb("win_i", [P, KC], I32)
    lead = m.sb("lead", [P, KC])
    until = m.sb("until", [P, KC])
    rows_i = [t["nodes_a"][:, a * K:(a + 1) * K].bitcast(I32) for a in range(3)]
    rows_f = [t["nodes_b"][:, a * K:(a + 1) * K].rearrange("p (c e) -> p c e", e=P) for a in range(3)]
    rows_f += [m.sb(f"rows_f{a}", [P, KC, P])[:, :, :] for a in range(3, 6)]
    valid = m.sb("valid", [P, KC, P])
    dump = m.sb("dump", [P, P])
    first_zero = m.sb("zero_rows", [P, D])
    cnt_ps = m.ps("cnt_ps", [P, 512])
    tr_ps = [m.ps(f"tr_ps{b}", [P, 512]) for b in range(2)]
    s_dst, s_in, s_pool, s_v, s_pe, s_tab, s_tab2, s_tr, s_cp, s_pad = (
        m.sem(n) for n in ("p_dst", "p_in", "p_const", "p_vector", "p_tensor", "p_table",
                           "p_table_back", "p_transposed", "p_copied", "p_pad"))
    s_rows = t["landed"][0]
    add_landed(t, [3 * KC * 16, 0, 0, 0])
    s_cnt = m.sem("p_count")
    s_link = m.sem("p_link")
    passed = m.sem("p_passed")
    CH = [(c0, min(G, KC - c0)) for c0 in range(0, KC, G)]
    CONV, COUNTED, WEND, WN, WVAL, TVAL, START, SIX = range(1, 9)

    block = m.stack.enter_context(nc.Block())

    @block.sync
    def _(sp):
        sp.dma_start(dst_i[:, :], dst.rearrange("(p n) -> p n", p=EP)).then_inc(s_dst, 16)
        sp.dma_start(d["xpad"][0:N, :], x).then_inc(s_pad, 16)
        sp.wait_ge(s_pool, 2)
        for n0 in range(N, NP + P, P):
            n1 = min(n0 + P, NP + P)
            sp.dma_start(d["xpad"][n0:n1, :], first_zero[0:n1 - n0, :]).then_inc(s_pad, 16)
        sp.wait_ge(s_v, START)
        with nc.allow_non_contiguous_dma(reason="a few thousand words, once"):
            sp.dma_start(d["tiles"][0].rearrange("(c p) -> p c", p=P), start_i[:, :]).then_inc(s_tab, 16)
            sp.dma_start(d["tiles"][1].rearrange("(c p) -> p c", p=P), win_i[:, :]).then_inc(s_tab, 16)
        sp.wait_ge(s_tab, 32)
        sp.dma_start(t["first_edge"][:, :], d["tiles"][0:1, :]).then_inc(s_tab2, 16)
        sp.dma_start(t["window"][:, :], d["tiles"][1:2, :]).then_inc(s_tab2, 16)
        sp.wait_ge(s_tab2, 32)
        sp.wait_ge(s_pad, 16 * (1 + len(range(N, NP + P, P))))

    @block.gpsimd
    def _(pool):
        pool.memset(first_zero[:, :], 0.0).then_inc(s_pool, 1)
        pool.memset(ones[:, :], 1.0).then_inc(s_pool, 1)
        pool.memset(t["ident"][:, :], 0.0).then_inc(s_pool, 1)
        pool.memset(before[:, :], 1.0).then_inc(s_pool, 1)
        pool.memset(t["earlier"][:, :], 1.0).then_inc(s_pool, 1)
        pool.memset(last_w[:, :], 0.0).then_inc(s_pool, 1)
        pool.wait_ge(s_pool, 6)
        pool.affine_select(out=t["ident"][:, :], in_=t["ident"][:, :], compare_op=ALU.not_equal, fill=1.0,
                           base=0, pattern=[[-1, P]], channel_multiplier=1).then_inc(s_pool, 1)
        pool.affine_select(out=before[:, :], in_=before[:, :], compare_op=ALU.is_gt, fill=0.0,
                           base=0, pattern=[[1, P]], channel_multiplier=-1).then_inc(s_pool, 1)
        pool.affine_select(out=t["earlier"][:, :], in_=t["earlier"][:, :], compare_op=ALU.is_gt, fill=0.0,
                           base=0, pattern=[[-1, P]], channel_multiplier=1).then_inc(s_pool, 1)
        pool.affine_select(out=last_w[:, :], in_=last_w[:, :], compare_op=ALU.not_equal, fill=float(K * P),
                           base=-(W - 1), pattern=[[0, 1]], channel_multiplier=1).then_inc(s_pool, 1)
        f = dict(allow_small_or_imprecise_dtypes=True)
        pool.iota(limit[:, :], pattern=[[P, W + 1]], base=0, channel_multiplier=0, **f).then_inc(s_pool, 1)
        pool.iota(tile_no[:, :], pattern=[[1, K]], base=0, channel_multiplier=0, **f).then_inc(s_pool, 1)
        pool.iota(tno[:, :], pattern=[[P * P, KC]], base=0, channel_multiplier=P, **f).then_inc(s_pool, 1)
        pool.iota(t["iota"][:, :], pattern=[[1, P]], base=0, channel_multiplier=0, **f).then_inc(s_pool, 1)
        pool.iota(t["lane"][:, :], pattern=[[0, 1]], base=0, channel_multiplier=1, **f).then_inc(s_pool, 1)
        pool.iota(dump[:, :], pattern=[[1, P]], base=N, channel_multiplier=0, **f).then_inc(s_pool, 1)
        pool.iota(t["dump_row"][:, :], pattern=[[0, 1]], base=N, channel_multiplier=1, **f).then_inc(s_pool, 1)
        pool.iota(wval[:, 2:3], pattern=[[0, 1]], base=0, channel_multiplier=1, **f).then_inc(s_pool, 1)
        pool.wait_ge(s_v, START)
        for a, v in enumerate((src, dst, rel)):
            for c in range(KC):
                pool.indirect_dma_start(
                    rows_i[a][:, c * P:(c + 1) * P], None, v.rearrange("(e a) -> e a", a=1),
                    bass.IndirectOffsetOnAxis(ap=start_i[:, c:c + 1], axis=0)).then_inc(s_rows, 16)

    POOL_DONE = 18

    @block.tensor
    def _(pe):
        pe.wait_ge(s_v, COUNTED)
        pe.wait_ge(s_pool, POOL_DONE)
        for j in range(2):
            nc.tensor.matmul(cnt_ps[0:W, j:j + 1], count[:, j:j + W], ones[0:EP, :],
                             start=True, stop=True).then_inc(s_pe, 1)
        pe.wait_ge(s_v, WN)
        nc.tensor.matmul(cnt_ps[0:W, 2:3], before[0:W, 0:W], wn[:, :], start=True, stop=True).then_inc(s_pe, 1)
        pe.wait_ge(s_v, WVAL)
        for c in range(KC):
            last = nc.tensor.matmul(cnt_ps[:, 16 + 3 * c:19 + 3 * c], hot[:, c * P:(c + 1) * P], wval[:, :],
                                    start=True, stop=True)
        last.then_inc(s_pe, 1)
        pe.wait_ge(s_v, SIX)
        n = 0
        for a in range(6):
            for c0, cn in CH:
                if n >= 2:
                    pe.wait_ge(s_cp, n - 1)
                for j in range(cn):
                    last = nc.tensor.transpose(tr_ps[n % 2][:, j * P:(j + 1) * P], rows_f[a][:, c0 + j, :],
                                               t["ident"][:, :])
                last.then_inc(s_tr, 1)
                n += 1

    @block.scalar
    def _(act):
        n = 0
        for a, name in enumerate(("row", "source", "source_or_dump", "target", "reset", "run_end")):
            for c0, cn in CH:
                act.wait_ge(s_tr, n + 1)
                nc.scalar.activation(t[name][:, c0 * P:(c0 + cn) * P], tr_ps[n % 2][:, 0:cn * P],
                                     ACT.Copy).then_inc(s_cp, 1)
                n += 1

    @block.vector
    def _(v):
        v.wait_ge(s_dst, 16)
        nc.vector.tensor_copy(dst_f[:, :], dst_i[:, :]).then_inc(s_v, 1)
        v.wait_ge(s_v, CONV)
        v.wait_ge(s_pool, POOL_DONE)
        with v.Fori(0, W + 1) as w:
            nc.vector.tensor_scalar(below[:, :], dst_f[:, :], limit[0:EP, bass.ds(w, 1)], 0.0, ALU.is_lt,
                                    ALU.add, accum_out=count[:, bass.ds(w, 1)]).then_inc(s_cnt, 1)
            v.wait_ge(s_cnt, w + 1)
        nc.vector.memset(below[:, 0:1], 0.0).then_inc(s_v, 1)
        v.wait_ge(s_pe, 2)
        nc.vector.tensor_copy(wend[:, :], cnt_ps[0:W, 0:2]).then_inc(s_v, 1)
        v.wait_ge(s_v, WEND)
        n = [0]

        def link(ins):
            n[0] += 1
            ins.then_inc(s_link, 1)
            v.wait_ge(s_link, n[0])

        link(nc.vector.scalar_tensor_tensor(wn[:, :], wend[:, 1:2], float(P - 1), wend[:, 0:1],
                                            ALU.add, ALU.subtract))
        link(nc.vector.tensor_copy(wni[:, :], wn[:, :]))
        link(nc.vector.tensor_scalar(wni[:, :], wni[:, :], 7, None, ALU.arith_shift_right))
        nc.vector.tensor_copy(wn[:, :], wni[:, :]).then_inc(s_v, 1)
        v.wait_ge(s_pe, 3)
        link(nc.vector.tensor_copy(wtile[:, 0:1], cnt_ps[0:W, 2:3]))
        link(nc.vector.tensor_tensor(wtile[:, 1:2], wtile[:, 0:1], wn[:, :], ALU.add))
        link(nc.vector.tensor_tensor(wtile[:, 1:2], wtile[:, 1:2], last_w[:, :], ALU.add))
        link(nc.vector.scalar_tensor_tensor(wval[:, 0:1], wtile[:, 0:1], -float(P), wend[:, 0:1],
                                            ALU.mult, ALU.add))
        link(nc.vector.tensor_copy(wval[:, 1:2], wend[:, 1:2]))
        link(nc.vector.tensor_scalar(started[:, :], tile_no[0:W, :], wtile[:, 0:1], None, ALU.is_ge))
        nc.vector.scalar_tensor_tensor(hot[:, :], tile_no[0:W, :], wtile[:, 1:2], started[:, :],
                                       ALU.is_lt, ALU.mult).then_inc(s_v, 1)
        v.wait_ge(s_pe, 4)
        nc.vector.tensor_copy(tval[:, :, :], cnt_ps[:, 16:16 + 3 * KC].rearrange("p (c v) -> p c v", v=3))\
            .then_inc(s_v, 1)
        v.wait_ge(s_v, TVAL)
        link(nc.vector.tensor_tensor(raw[:, :], tval[:, :, 0], tno[:, :], ALU.add))
        link(nc.vector.tensor_scalar(start[:, :], raw[:, :], float(E - P), None, ALU.min))
        link(nc.vector.tensor_tensor(lead[:, :], raw[:, :], start[:, :], ALU.subtract))
        link(nc.vector.tensor_tensor(until[:, :], tval[:, :, 1], start[:, :], ALU.subtract))
        link(nc.vector.tensor_copy(win_i[:, :], tval[:, :, 2]))
        nc.vector.tensor_copy(start_i[:, :], start[:, :]).then_inc(s_v, 1)

        def over_tiles(a):
            return a.unsqueeze(1).to_broadcast([P, KC, P])

        def over_edges(a):
            return a.unsqueeze(2).to_broadcast([P, KC, P])

        pos = over_tiles(t["iota"][:, :])
        link(nc.vector.tensor_tensor(rows_f[0][:, :, :], pos, over_edges(lead[:, :]), ALU.is_ge))
        link(nc.vector.tensor_tensor(valid[:, :, :], pos, over_edges(until[:, :]), ALU.is_lt))
        link(nc.vector.tensor_tensor(valid[:, :, :], valid[:, :, :], rows_f[0][:, :, :], ALU.mult))
        v.wait_ge(s_rows, 3 * KC * 16)
        srow, drow, trow = (r[:, :].rearrange("p (c e) -> p c e", e=P) for r in rows_i)
        row, source, sod, target, reset, run_end = rows_f
        link(nc.vector.tensor_copy(source[:, :, :], srow))
        link(nc.vector.tensor_copy(target[:, :, :], drow))
        link(nc.vector.tensor_copy(row[:, :, :], trow))
        link(nc.vector.scalar_tensor_tensor(row[:, :, :], source[:, :, :], float(R), row[:, :, :],
                                            ALU.mult, ALU.add))
        link(nc.vector.tensor_scalar(lead[:, :], tval[:, :, 2], float(P), None, ALU.mult))
        link(nc.vector.tensor_tensor(target[:, :, :], target[:, :, :], over_edges(lead[:, :]), ALU.subtract))
        link(nc.vector.scalar_tensor_tensor(target[:, :, :], target[:, :, :], 1.0, valid[:, :, :],
                                            ALU.add, ALU.mult))
        link(nc.vector.tensor_scalar(target[:, :, :], target[:, :, :], -1.0, None, ALU.add))
        link(nc.vector.tensor_tensor(sod[:, :, :], source[:, :, :], over_tiles(dump[:, :]), ALU.subtract))
        link(nc.vector.tensor_tensor(sod[:, :, :], sod[:, :, :], valid[:, :, :], ALU.mult))
        link(nc.vector.tensor_tensor(sod[:, :, :], sod[:, :, :], over_tiles(dump[:, :]), ALU.add))
        link(nc.vector.memset(run_end[:, :, :], 1.0))
        link(nc.vector.tensor_tensor(run_end[:, :, 0:P - 1], target[:, :, 1:P], target[:, :, 0:P - 1],
                                     ALU.not_equal))
        link(nc.vector.memset(reset[:, :, :], -BIG))
        nc.vector.tensor_scalar(reset[:, :, 1:P], run_end[:, :, 0:P - 1], -BIG, None, ALU.mult)\
            .then_inc(s_v, 1)


def two(i, h):
    return i * 2 + h


def relation_table(nc, m, t, d, w_all, self_w, bias, first):
    wrel = m.sb("wrel", [D, R * D])
    wself = m.sb("wself", [D, D])
    bcol = m.sb("bcol", [D, 1])
    xin = [m.sb(f"xin{h}", [P, D]) for h in range(2)]
    xts = [m.sb(f"xts{h}", [D, P]) for h in range(2)]
    summed = [m.sb(f"summed{h}", [D, P]) for h in range(2)]
    xo = [m.sb(f"xo{h}", [P, R * D]) for h in range(2)]
    ps_t = [m.ps(f"ps_t{h}", [P, 512]) for h in range(2)]
    ps_x = [[m.ps(f"ps_x{h}{j}", [P, 512]) for j in range(2)] for h in range(2)]
    HALF = R * D // 2
    s_w, s_t, s_sum, s_xts, s_x, s_keep, s_oa, s_ov, s_st, s_free, s_zero = (
        m.sem(n) for n in ("r_weights", "r_transposed", "r_summed", "r_slot", "r_product", "r_kept",
                           "r_out_scalar", "r_out_vector", "r_stored", "r_free", "r_zeroed"))
    s_in = [m.sem(f"r_in{h}") for h in range(2)]
    block = m.stack.enter_context(nc.Block())

    @block.sync
    def _(sp):
        sp.dma_start(wrel[:, :].rearrange("d (r e) -> d r e", r=R), w_all.rearrange("r d e -> d r e"))\
            .then_inc(s_w, 16)
        sp.dma_start(wself[:, :], self_w).then_inc(s_w, 16)
        with nc.allow_non_contiguous_dma(reason="a bias as a column"):
            sp.dma_start(bcol[:, :], bias.rearrange("(d a) -> d a", a=1)).then_inc(s_w, 16)
        sp.wait_ge(s_w, 48)
        if first:
            sp.dma_start(xin[0][:, :], d["xpad"][0:P, :]).then_inc(s_in[0], 16)
        sp.sem_inc(s_free, 2)
        with sp.Fori(0, NT // 2) as i:
            for h in range(2):
                g = two(i, h)
                if first:
                    sp.dma_start(xin[1 - h][:, :], d["xpad"][bass.ds((g + 1) * P, P), :])\
                        .then_inc(s_in[1 - h], 16)
                sp.wait_ge(s_oa, g + 1)
                sp.wait_ge(s_ov, g + 1)
                sp.dma_start(d["xt"][bass.ds(g * P, P), :], xo[h][:, :]).then_inc(s_st, 16)
                sp.wait_ge(s_st, g * 16 + 16)
                sp.sem_inc(s_free, 1)
        if first:
            sp.wait_ge(s_in[0], (NT // 2 + 1) * 16)

    @block.tensor
    def _(pe):
        pe.wait_ge(s_w, 48)
        with pe.Fori(0, NT // 2) as i:
            for h in range(2):
                g = two(i, h)
                pe.wait_ge(s_free, g + 1)
                if first:
                    pe.wait_ge(s_in[h], i * 16 + 16)
                    nc.tensor.transpose(ps_t[h][:, 0:P], xin[h][:, :], t["ident"][:, :]).then_inc(s_t, 1)
                else:
                    nc.tensor.matmul(ps_t[h][:, 0:P], wself[:, :], t["nodes_a"][:, bass.ds(g * P, P)],
                                     start=True, stop=True).then_inc(s_t, 1)
                pe.wait_ge(s_xts, g + 1)
                for j in range(2):
                    last = nc.tensor.matmul(ps_x[h][j][:, :], xts[h][:, :], wrel[:, j * HALF:(j + 1) * HALF],
                                            start=True, stop=True)
                last.then_inc(s_x, 1)

    @block.scalar
    def _(act):
        act.wait_ge(s_w, 48)
        with act.Fori(0, NT // 2) as i:
            for h in range(2):
                g = two(i, h)
                if first:
                    act.wait_ge(s_t, g + 1)
                    nc.scalar.activation(xts[h][:, :], ps_t[h][:, 0:P], ACT.Copy).then_inc(s_xts, 1)
                else:
                    act.wait_ge(s_sum, g + 1)
                    nc.scalar.activation(xts[h][:, :], summed[h][:, :], ACT.Relu, bias=bcol[:, :])\
                        .then_inc(s_xts, 1)
                act.wait_ge(s_x, g + 1)
                nc.scalar.activation(xo[h][:, 0:HALF], ps_x[h][0][:, :], ACT.Copy).then_inc(s_oa, 1)

    @block.vector
    def _(v):
        if first:
            nc.vector.memset(t["nodes_b"][:, :], 0.0).then_inc(s_zero, 1)
        with v.Fori(0, NT // 2) as i:
            for h in range(2):
                g = two(i, h)
                if first:
                    v.wait_ge(s_xts, g + 1)
                    nc.vector.tensor_copy(t["nodes_a"][:, bass.ds(g * P, P)], xts[h][:, :])\
                        .then_inc(s_keep, 1)
                else:
                    v.wait_ge(s_t, g + 1)
                    nc.vector.tensor_tensor(summed[h][:, :], ps_t[h][:, 0:P],
                                            t["nodes_b"][:, bass.ds(g * P, P)], ALU.add).then_inc(s_sum, 1)
                    v.wait_ge(s_xts, g + 1)
                    nc.vector.tensor_copy(t["nodes_a"][:, bass.ds(g * P, P)], xts[h][:, :])\
                        .then_inc(s_keep, 1)
                    nc.vector.tensor_scalar(t["nodes_b"][:, bass.ds(g * P, P)], summed[h][:, :], 0.0, None,
                                            ALU.mult).then_inc(s_zero, 1)
                v.wait_ge(s_x, g + 1)
                nc.vector.tensor_copy(xo[h][:, HALF:2 * HALF], ps_x[h][1][:, :]).then_inc(s_ov, 1)


def aggregate(nc, m, t, d, zero_sums):
    index = [m.sb(f"index{q}", [P, G], I32) for q in range(SLOTS)]
    msg = [m.sb(f"msg{q}", [P, G, D]) for q in range(SLOTS)]
    hot = [m.sb(f"hot{q}", [P, G, P]) for q in range(2)]
    zero = m.sb("zero", [P, 10 * D]) if zero_sums else None
    ps = [m.ps(f"ps_agg{q}", [D, G, P]) for q in range(2)]
    s_index, s_hot, s_freed, s_acc, s_read, passed, s_z, s_zd = (
        m.sem(n) for n in ("a_index", "a_hot", "a_msg_free", "a_added", "a_ps_read",
                           "a_passed", "a_zero", "a_zeroed"))
    s_msg = t["landed"]
    at = add_landed(t, [TURNS * G * 16] * SLOTS)
    block = m.stack.enter_context(nc.Block())
    xt = d["xt"].rearrange("n (r e) -> (n r) e", r=R)

    if zero_sums:
        @block.sync
        def _(sp):
            sp.wait_ge(s_z, 1)
            n = 0
            for r in range(REP):
                for a in range(NP // (10 * P)):
                    sp.dma_start(d["sums"][r][a * 10 * P:(a + 1) * 10 * P, :].rearrange("(p j) e -> p (j e)", p=P),
                                 zero[:, :]).then_inc(s_zd, 16)
                    n += 1
            sp.wait_ge(s_zd, 16 * n)

    @block.scalar
    def _(act):
        with act.Fori(0, TURNS) as i:
            for q in range(SLOTS):
                g = i * SLOTS + q
                act.wait_ge(s_freed, g + 1)
                nc.scalar.activation(index[q][:, :], t["row"][:, bass.ds(g * G, G)], ACT.Copy)\
                    .then_inc(s_index, 1)

    @block.gpsimd
    def _(pool):
        with pool.Fori(0, TURNS) as i:
            for q in range(SLOTS):
                g = i * SLOTS + q
                ring_index(pool, s_index, g + 1, passed)
                for j in range(G):
                    pool.indirect_dma_start(msg[q][:, j, :], None, xt,
                                            bass.IndirectOffsetOnAxis(ap=index[q][:, j:j + 1], axis=0))\
                        .then_inc(s_msg[q], 16)

    @block.tensor
    def _(pe):
        pe.sem_inc(s_freed, SLOTS)
        with pe.Fori(0, TURNS) as i:
            for q in range(SLOTS):
                g = i * SLOTS + q
                pe.wait_ge(s_hot, g + 1)
                pe.wait_ge(s_read, g + 1)
                pe.wait_ge(s_msg[q], i * (16 * G) + (16 * G + at[q]))
                for j in range(G):
                    last = nc.tensor.matmul(ps[q % 2][:, j, :], msg[q][:, j, :], hot[q % 2][:, j, :],
                                            start=True, stop=True)
                last.then_inc(s_freed, 1)

    @block.vector
    def _(v):
        v.sem_inc(s_read, 2)
        if zero_sums:
            nc.vector.memset(zero[:, :], 0.0).then_inc(s_z, 1)
        with v.Fori(0, TURNS) as i:
            for q in range(SLOTS):
                g = i * SLOTS + q
                v.wait_ge(s_freed, g + SLOTS - 1)
                nc.vector.tensor_tensor(
                    hot[q % 2][:, :, :], t["iota"][:, :].unsqueeze(1).to_broadcast([P, G, P]),
                    t["target"][:, bass.ds(g * G, G)].unsqueeze(2).to_broadcast([P, G, P]),
                    ALU.is_equal).then_inc(s_hot, 1)
                w = [v.value_load(t["window"][0:1, bass.ds(g * G + j, 1)], min_val=0, max_val=W - 1)
                     for j in range(G)]
                v.wait_ge(s_freed, g + SLOTS + 1)
                for j in range(G):
                    into = t["nodes_b"][:, bass.ds(w[j] * P, P)]
                    nc.vector.tensor_tensor(into, into, ps[q % 2][:, j, :], ALU.add).then_inc(s_acc, 1)
                    v.wait_ge(s_acc, g * G + j + 1)
                v.sem_inc(s_read, 1)


class Steps:

    def __init__(self, engine, sem, base, stood=None):
        self.engine, self.sem, self.base, self.stood, self.n = engine, sem, base, stood, 0

    def stand(self):
        self.engine.sem_inc(self.stood, 1)

    def __call__(self, instruction):
        self.n += 1
        instruction.then_inc(self.sem, 1)
        self.engine.wait_ge(self.sem, self.base + self.n)


def normalize(nc, v, step, out, in_, stats, moments, s_var, s_std, turn):
    step(nc.vector.bn_stats(stats, in_))
    step.stand()
    nc.vector.bn_aggr(moments, stats).then_inc(s_var, 1)
    v.wait_ge(s_std, turn)
    step(nc.vector.reciprocal(moments[:, 1:2], moments[:, 1:2]))
    return nc.vector.tensor_scalar(out, in_, moments[:, 0:1], moments[:, 1:2], ALU.subtract, ALU.mult)


def deviation(nc, act, moments, eps, s_var, s_std, turn):
    act.wait_ge(s_var, turn)
    nc.scalar.activation(moments[:, 1:2], moments[:, 1:2], ACT.Sqrt, bias=eps).then_inc(s_std, 1)


def add_landed(t, counts):
    before = list(t["landed_at"])
    t["landed_at"] = [a + b for a, b in zip(before, counts)]
    return before


def rows_of(v):
    return v.partition_broadcast(P)


def project(nc, m, t, d, self_w, bias, wq, wk, wv, bq, bk, bv, g1, be1):
    wself = m.sb("wself", [D, D])
    wqkv = m.sb("wqkv", [D, 3 * D])
    bcol = m.sb("bcol", [D, 1])
    bqkv = m.sb("bqkv", [P, 3 * D])
    gain = m.sb("gain", [P, D])
    shift = m.sb("shift", [P, D])
    two_of = lambda n, shape: [m.sb(f"{n}{h}", shape) for h in range(2)]
    xin, summed, ht, y, xl, n1, n1t, qkv = (two_of(n, [P, D]) for n in (
        "xin", "summed", "ht", "y", "xl", "n1", "n1t", "qo"))
    stats, moments = two_of("stats", [P, 6]), two_of("moments", [P, 2])
    ps_a, ps_b, ps_c, ps_d = ([m.ps(f"{n}{h}", [P, 512]) for h in range(2)] for n in (
        "ps_self", "ps_rows", "ps_normed", "ps_qkv"))
    s_w, s_self, s_sum, s_ht, s_rows, s_norm, s_nt, s_n1t, s_qkv, s_out, s_step, s_st, s_free = (
        m.sem(n) for n in ("q_weights", "q_self", "q_summed", "q_relu", "q_rows", "q_normed",
                           "q_normed_t", "q_slot", "q_product", "q_out", "q_step", "q_stored", "q_free"))
    s_in = [m.sem(f"q_in{h}") for h in range(2)]
    s_stood = m.sem("q_stood")
    s_var, s_std, s_eps = m.sem("q_variance"), m.sem("q_deviation"), m.sem("q_eps")
    eps = m.sb("eps", [P, 1])
    STEPS = 10
    block = m.stack.enter_context(nc.Block())

    @block.sync
    def _(sp):
        n = 0
        for out, in_ in ((wself[:, :], self_w), (wqkv[:, 0:D], wq), (wqkv[:, D:2 * D], wk),
                         (wqkv[:, 2 * D:3 * D], wv), (bqkv[:, 0:D], rows_of(bq)),
                         (bqkv[:, D:2 * D], rows_of(bk)), (bqkv[:, 2 * D:3 * D], rows_of(bv)),
                         (gain[:, :], rows_of(g1)), (shift[:, :], rows_of(be1))):
            sp.dma_start(out, in_).then_inc(s_w, 16)
            n += 1
        with nc.allow_non_contiguous_dma(reason="a bias as a column"):
            sp.dma_start(bcol[:, :], bias.rearrange("(d a) -> d a", a=1)).then_inc(s_w, 16)
        sp.wait_ge(s_w, 16 * (n + 1))
        sp.dma_start(xin[0][:, :], d["xpad"][0:P, :]).then_inc(s_in[0], 16)
        sp.sem_inc(s_free, 2)
        with sp.Fori(0, NT // 2) as i:
            for h in range(2):
                g = two(i, h)
                sp.dma_start(xin[1 - h][:, :], d["xpad"][bass.ds((g + 1) * P, P), :]).then_inc(s_in[1 - h], 16)
                sp.wait_ge(s_out, g + 1)
                sp.dma_start(d["q"][bass.ds(g * P, P), :], qkv[h][:, :]).then_inc(s_st, 16)
                sp.dma_start(d["xl"][bass.ds(g * P, P), :], xl[h][:, :]).then_inc(s_st, 16)
                sp.wait_ge(s_st, g * 32 + 32)
                sp.sem_inc(s_free, 1)
        sp.wait_ge(s_in[0], (NT // 2 + 1) * 16)

    @block.tensor
    def _(pe):
        pe.wait_ge(s_w, 160)
        with pe.Fori(0, NT // 2) as i:
            for h in range(2):
                g = two(i, h)
                pe.wait_ge(s_free, g + 1)
                nc.tensor.matmul(ps_a[h][:, 0:P], wself[:, :], t["nodes_a"][:, bass.ds(g * P, P)],
                                 start=True, stop=True).then_inc(s_self, 1)
                pe.wait_ge(s_ht, g + 1)
                nc.tensor.transpose(ps_b[h][:, 0:D], ht[h][:, :], t["ident"][:, :]).then_inc(s_rows, 1)
                pe.wait_ge(s_norm, g + 1)
                nc.tensor.transpose(ps_c[h][:, 0:P], n1[h][:, :], t["ident"][:, :]).then_inc(s_nt, 1)
                pe.wait_ge(s_n1t, g + 1)
                nc.tensor.matmul(ps_d[h][:, 0:3 * D], n1t[h][:, :], wqkv[:, :], start=True, stop=True)\
                    .then_inc(s_qkv, 1)

    @block.gpsimd
    def _(pool):
        pool.memset(eps[:, :], EPS).then_inc(s_eps, 1)

    @block.scalar
    def _(act):
        act.wait_ge(s_eps, 1)
        act.wait_ge(s_w, 160)
        with act.Fori(0, NT // 2) as i:
            for h in range(2):
                g = two(i, h)
                act.wait_ge(s_sum, g + 1)
                nc.scalar.activation(ht[h][:, :], summed[h][:, :], ACT.Relu, bias=bcol[:, :]).then_inc(s_ht, 1)
                for a in range(2):
                    deviation(nc, act, moments[h], eps[:, :], s_var, s_std, g * 2 + 1 + a)
                act.wait_ge(s_nt, g + 1)
                nc.scalar.activation(n1t[h][:, :], ps_c[h][:, 0:P], ACT.Copy).then_inc(s_n1t, 1)

    @block.vector
    def _(v):
        v.wait_ge(s_w, 160)
        with v.Fori(0, NT // 2) as i:
            for h in range(2):
                g = two(i, h)
                step = Steps(v, s_step, g * STEPS, s_stood)
                v.wait_ge(s_self, g + 1)
                nc.vector.tensor_tensor(summed[h][:, :], ps_a[h][:, 0:P], t["nodes_b"][:, bass.ds(g * P, P)],
                                        ALU.add).then_inc(s_sum, 1)
                v.wait_ge(s_in[h], i * 16 + 16)
                v.wait_ge(s_rows, g + 1)
                step(nc.vector.tensor_tensor(y[h][:, :], ps_b[h][:, 0:D], xin[h][:, :], ALU.add))
                step(normalize(nc, v, step, xl[h][:, :], y[h][:, :], stats[h][:, :], moments[h][:, :],
                               s_var, s_std, g * 2 + 1))
                step(normalize(nc, v, step, n1[h][:, :], xl[h][:, :], stats[h][:, :], moments[h][:, :],
                               s_var, s_std, g * 2 + 2))
                step(nc.vector.tensor_tensor(n1[h][:, :], n1[h][:, :], gain[:, :], ALU.mult))
                nc.vector.tensor_tensor(n1[h][:, :], n1[h][:, :], shift[:, :], ALU.add).then_inc(s_norm, 1)
                v.wait_ge(s_qkv, g + 1)
                step(nc.vector.tensor_tensor(qkv[h][:, :], ps_d[h][:, 0:D], bqkv[:, 0:D], ALU.add))
                step(nc.vector.tensor_scalar(qkv[h][:, :], qkv[h][:, :], HD ** -0.5, None, ALU.mult))
                nc.vector.tensor_tensor(t["nodes_a"][:, bass.ds(g * P, P)], ps_d[h][:, D:2 * D],
                                        bqkv[:, D:2 * D], ALU.add)
                nc.vector.tensor_tensor(t["nodes_b"][:, bass.ds(g * P, P)], ps_d[h][:, 2 * D:3 * D],
                                        bqkv[:, 2 * D:3 * D], ALU.add).then_inc(s_out, 1)
                assert step.n == STEPS


def score(nc, m, t, d, curv, wc, bc):
    slots = lambda n, k, shape, dt=FP32: [m.sb(f"{n}{q}", shape, dt) for q in range(k)]
    index = slots("index", SLOTS, [P, G], I32)
    qrow = slots("qrow", SLOTS, [P, G, D])
    cur = slots("cur", SLOTS, [P, G, D])
    tgt = slots("tgt", 2, [P, G])
    of_node = slots("of_node", 2, [P, G * P])
    cur_t = slots("cur_t", 2, [D, G * P])
    prod = slots("prod", 2, [P, G * D])
    qk = slots("qk", 2, [P, G * H])
    wc_sb = m.sb("wc_sb", [D, H])
    bc_sb = m.sb("bc_sb", [1, H])
    ones = m.sb("ones_row", [1, P])
    ps_t, ps_c, ps_k, ps_s = ([m.ps(f"{n}{h}", [P, 512]) for h in range(2)] for n in (
        "ps_tgt", "ps_cur", "ps_key", "ps_score"))
    s_w, s_index, s_tgt, s_freed, s_pt, s_pc, s_node, s_ct, s_k, s_s, s_prod, s_qk, s_out, passed, s_one = (
        m.sem(n) for n in ("s_weights", "s_index", "s_target", "s_slot_free", "s_target_t", "s_curv_t",
                           "s_of_node", "s_curv_slot", "s_key", "s_curv_score", "s_products", "s_qk",
                           "s_scores", "s_passed", "s_ones"))
    s_q = t["landed"]
    at = add_landed(t, [TURNS * G * 16] * SLOTS)
    s_c = [m.sem(f"s_c{q}") for q in range(SLOTS)]
    block = m.stack.enter_context(nc.Block())

    @block.sync
    def _(sp):
        sp.dma_start(wc_sb[:, :], wc).then_inc(s_w, 16)
        sp.dma_start(bc_sb[:, :], bc.rearrange("(a h) -> a h", a=1)).then_inc(s_w, 16)
        with sp.Fori(0, TURNS) as i:
            for q in range(SLOTS):
                g = i * SLOTS + q
                first = [sp.value_load(t["first_edge"][0:1, bass.ds(g * G + j, 1)], min_val=0, max_val=E - P)
                         for j in range(G)]
                sp.wait_ge(s_freed, g + 1)
                for j in range(G):
                    sp.dma_start(cur[q][:, j, :], curv[bass.ds(first[j], P), :]).then_inc(s_c[q], 16)

    @block.gpsimd
    def _(pool):
        with pool.Fori(0, TURNS) as i:
            for q in range(SLOTS):
                g = i * SLOTS + q
                ring_index(pool, s_index, g + 1, passed)
                for j in range(G):
                    pool.indirect_dma_start(qrow[q][:, j, :], None, d["q"],
                                            bass.IndirectOffsetOnAxis(ap=index[q][:, j:j + 1], axis=0))\
                        .then_inc(s_q[q], 16)

    @block.scalar
    def _(act):
        nc.scalar.activation(ones[:, :], t["ident"][0:1, :], ACT.Copy, bias=1.0, scale=0.0).then_inc(s_one, 1)
        with act.Fori(0, TURNS) as i:
            for q in range(SLOTS):
                g = i * SLOTS + q
                h = q % 2
                act.wait_ge(s_freed, g + 1)
                nc.scalar.activation(index[q][:, :], t["source"][:, bass.ds(g * G, G)], ACT.Copy)\
                    .then_inc(s_index, 1)
                nc.scalar.activation(tgt[h][:, :], t["target"][:, bass.ds(g * G, G)], ACT.Copy)\
                    .then_inc(s_tgt, 1)
                act.wait_ge(s_pc, g + 1)
                nc.scalar.activation(cur_t[h][:, :], ps_c[h][:, :], ACT.Copy).then_inc(s_ct, 1)

    @block.tensor
    def _(pe):
        pe.wait_ge(s_w, 32)
        pe.wait_ge(s_one, 1)
        with pe.Fori(0, TURNS) as i:
            for q in range(SLOTS):
                g = i * SLOTS + q
                h = q % 2
                w = [pe.value_load(t["window"][0:1, bass.ds(g * G + j, 1)], min_val=0, max_val=W - 1)
                     for j in range(G)]
                pe.wait_ge(s_tgt, g + 1)
                for j in range(G):
                    last = nc.tensor.transpose(ps_t[h][:, j * P:(j + 1) * P],
                                               tgt[h][:, j:j + 1].to_broadcast([P, P]), t["ident"][:, :])
                last.then_inc(s_pt, 1)
                pe.wait_ge(s_c[q], i * (16 * G) + 16 * G)
                for j in range(G):
                    last = nc.tensor.transpose(ps_c[h][:, j * P:(j + 1) * P], cur[q][:, j, :], t["ident"][:, :])
                last.then_inc(s_pc, 1)
                pe.wait_ge(s_node, g + 1)
                for j in range(G):
                    last = nc.tensor.matmul(ps_k[h][:, j * D:(j + 1) * D], of_node[h][:, j * P:(j + 1) * P],
                                            t["nodes_a"][:, bass.ds(w[j] * P, P)], start=True, stop=True)
                last.then_inc(s_k, 1)
                pe.wait_ge(s_ct, g + 1)
                for j in range(G):
                    into = ps_s[h][:, j * H:(j + 1) * H]
                    nc.tensor.matmul(into, cur_t[h][:, j * P:(j + 1) * P], wc_sb[:, :], start=True, stop=False)
                    last = nc.tensor.matmul(into, ones[:, :], bc_sb[:, :], start=False, stop=True)
                last.then_inc(s_s, 1)

    @block.vector
    def _(v):
        v.sem_inc(s_freed, SLOTS)
        with v.Fori(0, TURNS) as i:
            for q in range(SLOTS):
                g = i * SLOTS + q
                h = q % 2
                v.wait_ge(s_pt, g + 1)
                nc.vector.tensor_scalar(of_node[h][:, :], ps_t[h][:, :], t["lane"][:, :], None, ALU.is_equal)\
                    .then_inc(s_node, 1)
                v.wait_ge(s_k, g + 1)
                v.wait_ge(s_q[q], i * (16 * G) + (16 * G + at[q]))
                nc.vector.tensor_tensor(prod[h][:, :], ps_k[h][:, :], qrow[q][:, :, :].rearrange("p j e -> p (j e)"),
                                        ALU.mult).then_inc(s_prod, 1)
                v.wait_ge(s_prod, g + 1)
                nc.vector.tensor_reduce(qk[h][:, :], prod[h][:, :].rearrange("p (a e) -> p a e", e=HD),
                                        AX.X, ALU.add).then_inc(s_qk, 1)
                v.wait_ge(s_qk, g + 1)
                v.wait_ge(s_s, g + 1)
                nc.vector.tensor_tensor(t["scores"][:, bass.ds(g * (G * H), G * H)], qk[h][:, :],
                                        ps_s[h][:, 0:G * H], ALU.add).then_inc(s_freed, 1)


MB = 16
XB = 8


def maxima(nc, m, t):
    slots = lambda n, shape: [m.sb(f"{n}{q}", shape) for q in range(2)]
    sc, rs, rs_t, run, hot, me, tm, pen = (slots(n, shape) for n, shape in (
        ("sc", [P, MB * H]), ("rs", [P, MB, H]), ("rs_t", [P, P]), ("run", [P, P]), ("hot", [P, MB, P]),
        ("me", [P, MB, H + 1]), ("tm", [P, MB, H]), ("pen", [P, MB])))
    ps_s, ps_r, ps_b, ps_e = ([m.ps(f"{n}{h}", [P, 512]) for h in range(2)] for n in (
        "ps_sc", "ps_rs", "ps_back", "ps_max"))
    s_slot, s_st, s_rt, s_rst, s_run, s_back, s_hot, s_me, s_e, s_pen, s_tm, s_acc, s_step = (
        m.sem(n) for n in ("m_slots", "m_scores_t", "m_reset_t", "m_reset_slot", "m_run_max", "m_back",
                           "m_hot", "m_ends", "m_product", "m_penalty", "m_tile_max", "m_added", "m_zero"))
    block = m.stack.enter_context(nc.Block())
    assert MB * H == P

    @block.scalar
    def _(act):
        with act.Fori(0, K // MB // 2) as i:
            for h in range(2):
                b = two(i, h)
                act.wait_ge(s_e, b + 1)
                nc.scalar.activation(sc[h][:, :], t["scores"][:, bass.ds(b * P, P)], ACT.Copy).then_inc(s_slot, 1)
                nc.scalar.activation(rs[h][:, :, :], t["reset"][:, bass.ds(b * MB, MB)].unsqueeze(2)
                                     .to_broadcast([P, MB, H]), ACT.Copy).then_inc(s_slot, 1)
                act.wait_ge(s_rt, b + 1)
                nc.scalar.activation(rs_t[h][:, :], ps_r[h][:, 0:P], ACT.Copy).then_inc(s_rst, 1)

    @block.tensor
    def _(pe):
        pe.sem_inc(s_e, 2)
        with pe.Fori(0, K // MB // 2) as i:
            for h in range(2):
                b = two(i, h)
                pe.wait_ge(s_slot, b * 2 + 2)
                nc.tensor.transpose(ps_s[h][:, 0:P], sc[h][:, :], t["ident"][:, :]).then_inc(s_st, 1)
                nc.tensor.transpose(ps_r[h][:, 0:P], rs[h][:, :, :].rearrange("p a b -> p (a b)"),
                                    t["ident"][:, :]).then_inc(s_rt, 1)
                pe.wait_ge(s_run, b + 1)
                nc.tensor.transpose(ps_b[h][:, 0:P], run[h][:, :], t["ident"][:, :]).then_inc(s_back, 1)
                pe.wait_ge(s_me, b + 1)
                for j in range(MB):
                    last = nc.tensor.matmul(ps_e[h][:, j * (H + 1):(j + 1) * (H + 1)], hot[h][:, j, :],
                                            me[h][:, j, :], start=True, stop=True)
                last.then_inc(s_e, 1)

    @block.vector
    def _(v):
        nc.vector.memset(t["node_max"][:, :], -BIG).then_inc(s_step, 1)
        v.wait_ge(s_step, 1)
        with v.Fori(0, K // MB // 2) as i:
            for h in range(2):
                b = two(i, h)
                w = [v.value_load(t["window"][0:1, bass.ds(b * MB + j, 1)], min_val=0, max_val=W - 1)
                     for j in range(MB)]
                nc.vector.tensor_tensor(
                    hot[h][:, :, :], t["iota"][:, :].unsqueeze(1).to_broadcast([P, MB, P]),
                    t["target"][:, bass.ds(b * MB, MB)].unsqueeze(2).to_broadcast([P, MB, P]),
                    ALU.is_equal).then_inc(s_hot, 1)
                v.wait_ge(s_st, b + 1)
                v.wait_ge(s_rst, b + 1)
                nc.vector.tensor_tensor_scan(run[h][:, :], rs_t[h][:, :], ps_s[h][:, 0:P], -BIG, ALU.add,
                                             ALU.max).then_inc(s_run, 1)
                v.wait_ge(s_back, b + 1)
                ends = t["run_end"][:, bass.ds(b * MB, MB)].unsqueeze(2)
                nc.vector.tensor_tensor(me[h][:, :, 0:H], ps_b[h][:, 0:P].rearrange("p (j a) -> p j a", a=H),
                                        ends.to_broadcast([P, MB, H]), ALU.mult)
                nc.vector.tensor_copy(me[h][:, :, H:H + 1], ends).then_inc(s_me, 1)
                v.wait_ge(s_e, b + 3)
                got = ps_e[h][:, 0:MB * (H + 1)].rearrange("p (j a) -> p j a", a=H + 1)
                nc.vector.tensor_scalar(pen[h][:, :].unsqueeze(2), got[:, :, H:H + 1], BIG, -BIG, ALU.mult,
                                        ALU.add).then_inc(s_pen, 1)
                v.wait_ge(s_pen, b + 1)
                nc.vector.tensor_tensor(tm[h][:, :, :], got[:, :, 0:H],
                                        pen[h][:, :].unsqueeze(2).to_broadcast([P, MB, H]), ALU.add)\
                    .then_inc(s_tm, 1)
                v.wait_ge(s_tm, b + 1)
                for j in range(MB):
                    into = t["node_max"][:, bass.ds(w[j] * H, H)]
                    nc.vector.tensor_tensor(into, into, tm[h][:, j, :], ALU.max).then_inc(s_acc, 1)
                    v.wait_ge(s_acc, b * MB + j + 1)


def exponentials(nc, m, t):
    slots = lambda n, shape: [m.sb(f"{n}{q}", shape) for q in range(2)]
    tgt, of_node, hot, diff = (slots(n, shape) for n, shape in (
        ("tgt", [P, XB]), ("of_node", [P, XB * P]), ("hot", [P, XB, P]), ("diff", [P, XB * H])))
    ps_t = [[m.ps(f"ps_tgt{h}{a}", [P, 512]) for a in range(2)] for h in range(2)]
    ps_m, ps_u = ([m.ps(f"{n}{h}", [P, 512]) for h in range(2)] for n in ("ps_nmax", "ps_sum"))
    s_tgt, s_pt, s_hot, s_node, s_m, s_diff, s_exp, s_u, s_acc, s_z = (
        m.sem(n) for n in ("e_target", "e_target_t", "e_hot", "e_of_node", "e_max", "e_diff", "e_exp",
                           "e_product", "e_added", "e_zero"))
    block = m.stack.enter_context(nc.Block())
    TB = XB // G

    @block.scalar
    def _(act):
        with act.Fori(0, K // XB // 2) as i:
            for h in range(2):
                b = two(i, h)
                act.wait_ge(s_u, b + 1)
                nc.scalar.activation(tgt[h][:, :], t["target"][:, bass.ds(b * XB, XB)], ACT.Copy)\
                    .then_inc(s_tgt, 1)
                act.wait_ge(s_diff, b + 1)
                nc.scalar.activation(t["scores"][:, bass.ds(b * (XB * H), XB * H)], diff[h][:, :], ACT.Exp)\
                    .then_inc(s_exp, 1)

    @block.tensor
    def _(pe):
        pe.sem_inc(s_u, 2)
        with pe.Fori(0, K // XB // 2) as i:
            for h in range(2):
                b = two(i, h)
                w = [pe.value_load(t["window"][0:1, bass.ds(b * XB + j, 1)], min_val=0, max_val=W - 1)
                     for j in range(XB)]
                pe.wait_ge(s_tgt, b + 1)
                for j in range(XB):
                    last = nc.tensor.transpose(ps_t[h][j // G][:, j % G * P:(j % G + 1) * P],
                                               tgt[h][:, j:j + 1].to_broadcast([P, P]), t["ident"][:, :])
                last.then_inc(s_pt, 1)
                pe.wait_ge(s_node, b * TB + TB)
                for j in range(XB):
                    last = nc.tensor.matmul(ps_m[h][:, j * H:(j + 1) * H], of_node[h][:, j * P:(j + 1) * P],
                                            t["node_max"][:, bass.ds(w[j] * H, H)], start=True, stop=True)
                last.then_inc(s_m, 1)
                pe.wait_ge(s_exp, b + 1)
                pe.wait_ge(s_hot, b + 1)
                for j in range(XB):
                    last = nc.tensor.matmul(ps_u[h][:, j * H:(j + 1) * H], hot[h][:, j, :],
                                            t["scores"][:, bass.ds(b * (XB * H) + j * H, H)],
                                            start=True, stop=True)
                last.then_inc(s_u, 1)

    @block.vector
    def _(v):
        nc.vector.memset(t["node_sum"][:, :], 0.0).then_inc(s_z, 1)
        v.wait_ge(s_z, 1)
        with v.Fori(0, K // XB // 2) as i:
            for h in range(2):
                b = two(i, h)
                w = [v.value_load(t["window"][0:1, bass.ds(b * XB + j, 1)], min_val=0, max_val=W - 1)
                     for j in range(XB)]
                nc.vector.tensor_tensor(
                    hot[h][:, :, :], t["iota"][:, :].unsqueeze(1).to_broadcast([P, XB, P]),
                    t["target"][:, bass.ds(b * XB, XB)].unsqueeze(2).to_broadcast([P, XB, P]),
                    ALU.is_equal).then_inc(s_hot, 1)
                v.wait_ge(s_pt, b + 1)
                for a in range(TB):
                    nc.vector.tensor_scalar(of_node[h][:, a * 512:(a + 1) * 512], ps_t[h][a][:, :],
                                            t["lane"][:, :], None, ALU.is_equal).then_inc(s_node, 1)
                v.wait_ge(s_m, b + 1)
                nc.vector.tensor_tensor(diff[h][:, :], t["scores"][:, bass.ds(b * (XB * H), XB * H)],
                                        ps_m[h][:, 0:XB * H], ALU.subtract).then_inc(s_diff, 1)
                v.wait_ge(s_u, b + 3)
                for j in range(XB):
                    into = t["node_sum"][:, bass.ds(w[j] * H, H)]
                    nc.vector.tensor_tensor(into, into, ps_u[h][:, j * H:(j + 1) * H], ALU.add).then_inc(s_acc, 1)
                    v.wait_ge(s_acc, b * XB + j + 1)


def scatter(nc, m, t, d):
    slots = lambda n, k, shape, dt=FP32: [m.sb(f"{n}{q}", shape, dt) for q in range(k)]
    index = slots("index", SLOTS, [P, G], I32)
    total = slots("total", SLOTS, [P, G, D])
    tgt = slots("tgt", 2, [P, G])
    srcs = slots("srcs", 2, [P, G])
    of_node = slots("of_node", 2, [P, G * P])
    same = slots("same", 2, [P, G, P])
    dup = slots("dup", 2, [P, G, P])
    dups = slots("dups", 2, [P, G])
    away = slots("away", 2, [P, G])
    msg = slots("msg", 2, [P, G * D])
    inverse = m.sb("inverse", [P, W * H])
    ps_t, ps_q, ps_v, ps_o = ([m.ps(f"{n}{h}", [P, 512]) for h in range(2)] for n in (
        "ps_tgt", "ps_src", "ps_val", "ps_tot"))
    s_inv, s_tgt, s_pt, s_ps, s_node, s_same, s_dup, s_dups, s_away, s_away2, s_index, s_v, s_msg, s_o, s_tot, s_free = (
        m.sem(n) for n in ("c_inverse", "c_slots", "c_target_t", "c_source_t", "c_of_node", "c_same", "c_dup",
                           "c_dups", "c_away", "c_away2", "c_index", "c_values", "c_msg", "c_product",
                           "c_total", "c_total_free"))
    s_sc = t["landed"]
    at = add_landed(t, [TURNS * 2 * G * 16] * 2 + [0, 0])
    passed = m.sem("c_passed")
    s_read = m.sem("c_total_read")
    block = m.stack.enter_context(nc.Block())

    @block.scalar
    def _(act):
        with act.Fori(0, TURNS) as i:
            for q in range(SLOTS):
                g = i * SLOTS + q
                h = q % 2
                act.wait_ge(s_o, g + 1)
                nc.scalar.activation(tgt[h][:, :], t["target"][:, bass.ds(g * G, G)], ACT.Copy).then_inc(s_tgt, 1)
                nc.scalar.activation(srcs[h][:, :], t["source_or_dump"][:, bass.ds(g * G, G)], ACT.Copy)\
                    .then_inc(s_tgt, 1)
                act.wait_ge(s_free, g + 1)
                act.wait_ge(s_o, g + 3)
                nc.scalar.activation(total[q][:, :, :].rearrange("p j e -> p (j e)"), ps_o[h][:, :], ACT.Copy)\
                    .then_inc(s_tot, 1)
                act.wait_ge(s_tot, g + 1)
                act.sem_inc(s_read, 1)

    @block.gpsimd
    def _(pool):
        pool.sem_inc(s_free, SLOTS)
        pool.sem_inc(s_read, 2)

        def turn(i, first):
            for q in range(SLOTS):
                g = i * SLOTS + q
                h = q % 2
                pool.wait_ge(s_index, g + 1)
                ring_index(pool, s_tot, g + 1, passed)
                for j in range(G):
                    pool.indirect_dma_start(d["sums"][h * G + j],
                                            bass.IndirectOffsetOnAxis(ap=index[q][:, j:j + 1], axis=0),
                                            total[q][:, j, :], None, compute_op=ALU.add).then_inc(s_sc[h], 16)
                if not (first and q == 0):
                    n = i * (2 * 16 * G) + ((q + 1) // 2 * 16 * G + at[1 - h])
                    ring_index(pool, s_sc[1 - h], n, s_free)

        turn(0, True)
        with pool.Fori(1, TURNS) as i:
            turn(i, False)
        for h in range(2):
            pool.wait_ge(s_sc[h], TURNS * 2 * 16 * G + at[h])

    @block.tensor
    def _(pe):
        pe.sem_inc(s_o, 2)
        with pe.Fori(0, TURNS) as i:
            for q in range(SLOTS):
                g = i * SLOTS + q
                h = q % 2
                w = [pe.value_load(t["window"][0:1, bass.ds(g * G + j, 1)], min_val=0, max_val=W - 1)
                     for j in range(G)]
                pe.wait_ge(s_tgt, g * 2 + 2)
                for j in range(G):
                    last = nc.tensor.transpose(ps_t[h][:, j * P:(j + 1) * P],
                                               tgt[h][:, j:j + 1].to_broadcast([P, P]), t["ident"][:, :])
                last.then_inc(s_pt, 1)
                for j in range(G):
                    last = nc.tensor.transpose(ps_q[h][:, j * P:(j + 1) * P],
                                               srcs[h][:, j:j + 1].to_broadcast([P, P]), t["ident"][:, :])
                last.then_inc(s_ps, 1)
                pe.wait_ge(s_node, g + 1)
                for j in range(G):
                    last = nc.tensor.matmul(ps_v[h][:, j * D:(j + 1) * D], of_node[h][:, j * P:(j + 1) * P],
                                            t["nodes_b"][:, bass.ds(w[j] * P, P)], start=True, stop=True)
                last.then_inc(s_v, 1)
                pe.wait_ge(s_msg, g + 1)
                pe.wait_ge(s_same, g + 1)
                pe.wait_ge(s_read, g + 1)
                for j in range(G):
                    last = nc.tensor.matmul(ps_o[h][:, j * D:(j + 1) * D], same[h][:, j, :],
                                            msg[h][:, j * D:(j + 1) * D], start=True, stop=True)
                last.then_inc(s_o, 1)

    @block.vector
    def _(v):
        nc.vector.tensor_scalar(inverse[:, :], t["node_sum"][:, :], 0.5, None, ALU.max).then_inc(s_inv, 1)
        v.wait_ge(s_inv, 1)
        nc.vector.reciprocal(inverse[:, :], inverse[:, :]).then_inc(s_inv, 1)
        v.wait_ge(s_inv, 2)
        by_head = t["nodes_b"][:, 0:W * P].rearrange("p (a e) -> p a e", e=HD)
        nc.vector.tensor_tensor(by_head, by_head, inverse[:, :].unsqueeze(2).to_broadcast([P, W * H, HD]),
                                ALU.mult).then_inc(s_inv, 1)
        v.wait_ge(s_inv, 3)
        with v.Fori(0, TURNS) as i:
            for q in range(SLOTS):
                g = i * SLOTS + q
                h = q % 2
                v.wait_ge(s_pt, g + 1)
                nc.vector.tensor_scalar(of_node[h][:, :], ps_t[h][:, :], t["lane"][:, :], None, ALU.is_equal)\
                    .then_inc(s_node, 1)
                v.wait_ge(s_ps, g + 1)
                nc.vector.tensor_tensor(same[h][:, :, :], ps_q[h][:, :].rearrange("p (j e) -> p j e", e=P),
                                        srcs[h][:, :].unsqueeze(2).to_broadcast([P, G, P]), ALU.is_equal)\
                    .then_inc(s_same, 1)
                v.wait_ge(s_v, g + 1)
                nc.vector.tensor_tensor(
                    msg[h][:, :].rearrange("p (a e) -> p a e", e=HD),
                    ps_v[h][:, :].rearrange("p (a e) -> p a e", e=HD),
                    t["scores"][:, bass.ds(g * (G * H), G * H)].unsqueeze(2).to_broadcast([P, G * H, HD]),
                    ALU.mult).then_inc(s_msg, 1)
                v.wait_ge(s_same, g + 1)
                nc.vector.tensor_tensor(dup[h][:, :, :], same[h][:, :, :],
                                        t["earlier"][:, :].unsqueeze(1).to_broadcast([P, G, P]), ALU.mult)\
                    .then_inc(s_dup, 1)
                v.wait_ge(s_dup, g + 1)
                nc.vector.tensor_reduce(dups[h][:, :], dup[h][:, :, :], AX.X, ALU.add).then_inc(s_dups, 1)
                nc.vector.tensor_scalar(away[h][:, :], srcs[h][:, :], -1.0, t["dump_row"][:, :], ALU.mult,
                                        ALU.add).then_inc(s_away, 1)
                v.wait_ge(s_dups, g + 1)
                v.wait_ge(s_away, g + 1)
                nc.vector.scalar_tensor_tensor(away[h][:, :], dups[h][:, :], 1.0, away[h][:, :], ALU.min,
                                               ALU.mult).then_inc(s_away2, 1)
                v.wait_ge(s_away2, g + 1)
                v.wait_ge(s_free, g + 1)
                nc.vector.tensor_tensor(index[q][:, :], away[h][:, :], srcs[h][:, :], ALU.add).then_inc(s_index, 1)


def finish(nc, m, t, d, wo, bo, g2, be2, wf1, bf1, wf2, bf2, out):
    NF = FF // P
    wo_sb = m.sb("wo_sb", [D, D])
    w1_sb = m.sb("w1_sb", [D, FF])
    w2_sb = m.sb("w2_sb", [P, NF, D])
    b1_sb = m.sb("b1_sb", [P, NF])
    bo_sb, b2_sb, gain, shift = (m.sb(n, [P, D]) for n in ("bo_sb", "b2_sb", "gain", "shift"))
    two_of = lambda n, shape: [m.sb(f"{n}{h}", shape) for h in range(2)]
    parts = two_of("parts", [P, REP, D])
    xl, o, ot, x1, n2, n2t, y, yo = (two_of(n, [P, D]) for n in ("xl", "o", "ot", "x1", "n2", "n2t", "y", "yo"))
    hid = two_of("hid", [P, NF, P])
    stats, moments = two_of("stats", [P, 6]), two_of("moments", [P, 2])
    ps_n = [m.ps(f"ps_node{h}", [P, 512]) for h in range(2)]
    ps_f = [m.ps(f"ps_hid{h}", [P, 512]) for h in range(2)]
    s_w, s_o, s_ot, s_otc, s_att, s_n2, s_nt, s_n2t, s_f, s_hid, s_y, s_out, s_step, s_st, s_free, s_copy = (
        m.sem(n) for n in ("f_weights", "f_sum", "f_sum_t", "f_sum_slot", "f_attention", "f_normed",
                           "f_normed_t", "f_slot", "f_hidden", "f_relu", "f_ffn", "f_out", "f_step",
                           "f_stored", "f_free", "f_copied"))
    s_in = [m.sem(f"f_in{h}") for h in range(2)]
    s_stood = m.sem("f_stood")
    s_var, s_std, s_eps = m.sem("f_variance"), m.sem("f_deviation"), m.sem("f_eps")
    eps = m.sb("eps", [P, 1])
    STEPS = 11
    NIN = 16 * (REP + 1)
    block = m.stack.enter_context(nc.Block())

    @block.sync
    def _(sp):
        n = 0
        for to, of in ((wo_sb[:, :], wo), (w1_sb[:, :], wf1), (w2_sb[:, :, :], wf2.rearrange("(c p) e -> p c e", p=P)),
                       (bo_sb[:, :], rows_of(bo)), (b2_sb[:, :], rows_of(bf2)),
                       (gain[:, :], rows_of(g2)), (shift[:, :], rows_of(be2))):
            sp.dma_start(to, of).then_inc(s_w, 16)
            n += 1
        with nc.allow_non_contiguous_dma(reason="a bias as columns"):
            sp.dma_start(b1_sb[:, :], bf1.rearrange("(c p) -> p c", p=P)).then_inc(s_w, 16)
        sp.wait_ge(s_w, 16 * (n + 1))

        def load(h, rows):
            sp.dma_start(xl[h][:, :], d["xl"][rows, :]).then_inc(s_in[h], 16)
            for r in range(REP):
                sp.dma_start(parts[h][:, r, :], d["sums"][r][rows, :]).then_inc(s_in[h], 16)

        load(0, slice(0, P))
        sp.sem_inc(s_free, 2)

        def tile(i, h, more):
            g = two(i, h)
            if more:
                load(1 - h, bass.ds((g + 1) * P, P))
            sp.wait_ge(s_out, g + 1)
            sp.dma_start(d["out"][bass.ds(g * P, P), :], yo[h][:, :]).then_inc(s_st, 16)
            sp.wait_ge(s_st, g * 16 + 16)
            sp.sem_inc(s_free, 1)

        with sp.Fori(0, NT // 2 - 1) as i:
            for h in range(2):
                tile(i, h, True)
        tile(NT // 2 - 1, 0, True)
        tile(NT // 2 - 1, 1, False)
        sp.dma_start(out, d["out"][0:N, :]).then_inc(s_copy, 16)
        sp.wait_ge(s_copy, 16)

    @block.tensor
    def _(pe):
        pe.wait_ge(s_w, 128)
        with pe.Fori(0, NT // 2) as i:
            for h in range(2):
                g = two(i, h)
                node = ps_n[h][:, 0:P]
                pe.wait_ge(s_free, g + 1)
                pe.wait_ge(s_o, g + 1)
                nc.tensor.transpose(node, o[h][:, :], t["ident"][:, :]).then_inc(s_ot, 1)
                pe.wait_ge(s_otc, g + 1)
                nc.tensor.matmul(node, ot[h][:, :], wo_sb[:, :], start=True, stop=True).then_inc(s_att, 1)
                pe.wait_ge(s_n2, g + 1)
                nc.tensor.transpose(node, n2[h][:, :], t["ident"][:, :]).then_inc(s_nt, 1)
                pe.wait_ge(s_n2t, g + 1)
                for c in range(NF):
                    last = nc.tensor.matmul(ps_f[h][:, c * P:(c + 1) * P], w1_sb[:, c * P:(c + 1) * P], n2t[h][:, :],
                                            start=True, stop=True)
                last.then_inc(s_f, 1)
                pe.wait_ge(s_hid, g * NF + NF)
                for c in range(NF):
                    last = nc.tensor.matmul(node, hid[h][:, c, :], w2_sb[:, c, :], start=(c == 0),
                                            stop=(c == NF - 1))
                last.then_inc(s_y, 1)

    @block.gpsimd
    def _(pool):
        pool.memset(eps[:, :], EPS).then_inc(s_eps, 1)

    @block.scalar
    def _(act):
        act.wait_ge(s_eps, 1)
        act.wait_ge(s_w, 128)
        with act.Fori(0, NT // 2) as i:
            for h in range(2):
                g = two(i, h)
                act.wait_ge(s_ot, g + 1)
                nc.scalar.activation(ot[h][:, :], ps_n[h][:, 0:P], ACT.Copy).then_inc(s_otc, 1)
                deviation(nc, act, moments[h], eps[:, :], s_var, s_std, g * 2 + 1)
                act.wait_ge(s_nt, g + 1)
                nc.scalar.activation(n2t[h][:, :], ps_n[h][:, 0:P], ACT.Copy).then_inc(s_n2t, 1)
                act.wait_ge(s_f, g + 1)
                for c in range(NF):
                    nc.scalar.activation(hid[h][:, c, :], ps_f[h][:, c * P:(c + 1) * P], ACT.Relu,
                                         bias=b1_sb[:, c:c + 1]).then_inc(s_hid, 1)
                deviation(nc, act, moments[h], eps[:, :], s_var, s_std, g * 2 + 2)

    @block.vector
    def _(v):
        v.wait_ge(s_w, 128)
        with v.Fori(0, NT // 2) as i:
            for h in range(2):
                g = two(i, h)
                step = Steps(v, s_step, g * STEPS, s_stood)
                v.wait_ge(s_in[h], i * NIN + NIN)
                v.wait_ge(s_free, g + 1)
                nc.vector.tensor_reduce(o[h][:, :], parts[h][:, :, :].rearrange("p r e -> p e r"), AX.X,
                                        ALU.add).then_inc(s_o, 1)
                v.wait_ge(s_att, g + 1)
                step(nc.vector.tensor_tensor(x1[h][:, :], ps_n[h][:, 0:D], bo_sb[:, :], ALU.add))
                step(nc.vector.tensor_tensor(x1[h][:, :], x1[h][:, :], xl[h][:, :], ALU.add))
                step(normalize(nc, v, step, n2[h][:, :], x1[h][:, :], stats[h][:, :], moments[h][:, :],
                               s_var, s_std, g * 2 + 1))
                step(nc.vector.tensor_tensor(n2[h][:, :], n2[h][:, :], gain[:, :], ALU.mult))
                nc.vector.tensor_tensor(n2[h][:, :], n2[h][:, :], shift[:, :], ALU.add).then_inc(s_n2, 1)
                v.wait_ge(s_y, g + 1)
                step(nc.vector.tensor_tensor(y[h][:, :], ps_n[h][:, 0:D], b2_sb[:, :], ALU.add))
                step(nc.vector.tensor_tensor(y[h][:, :], y[h][:, :], x1[h][:, :], ALU.add))
                step(nc.vector.tensor_tensor(y[h][:, :], y[h][:, :], xl[h][:, :], ALU.add))
                normalize(nc, v, step, yo[h][:, :], y[h][:, :], stats[h][:, :], moments[h][:, :],
                          s_var, s_std, g * 2 + 2).then_inc(s_out, 1)
                assert step.n == STEPS


def build(nc, x, src, dst, curv, rel, w1, sl1, b1, w2, sl2, b2, wq, bq, wk, bk, wv, bv, wo, bo, wc, bc,
          wf1, bf1, wf2, bf2, g1, be1, g2, be2, out):
    with ExitStack() as top:
        keep = Memory(nc, top, "")
        t = {
            "ident": keep.sb("ident", [P, P]), "iota": keep.sb("iota", [P, P]),
            "earlier": keep.sb("earlier", [P, P]), "lane": keep.sb("lane", [P, 1]),
            "dump_row": keep.sb("dump_row", [P, 1]),
            "row": keep.sb("row", [P, K], I32), "source": keep.sb("source", [P, K], I32),
            "source_or_dump": keep.sb("source_or_dump", [P, K]), "target": keep.sb("target", [P, K]),
            "reset": keep.sb("reset", [P, K]), "run_end": keep.sb("run_end", [P, K]),
            "window": keep.sb("window", [1, K], I32), "first_edge": keep.sb("first_edge", [1, K], I32),
            "nodes_a": keep.sb("nodes_a", [P, NP]), "nodes_b": keep.sb("nodes_b", [P, NP]),
            "landed": [keep.sem(f"landed{q}") for q in range(SLOTS)],
            "landed_at": [0] * SLOTS,
        }
        d = {
            "xpad": nc.dram_tensor("xpad", (NP + P, D), FP32).ap(),
            "tiles": nc.dram_tensor("tiles", (2, K), I32).ap(),
            "xt": nc.dram_tensor("xt", (NP, R * D), FP32).ap(),
            "q": nc.dram_tensor("q", (NP, D), FP32).ap(),
            "xl": nc.dram_tensor("xl", (NP, D), FP32).ap(),
            "out": nc.dram_tensor("out_rows", (NP, D), FP32).ap(),
            "sums": [nc.dram_tensor(f"sums{r}", (NP, D), FP32).ap() for r in range(REP)],
        }

        done = []

        def stage(f, *args):
            done.append(f)
            with ExitStack() as kept:
                with ExitStack() as s:
                    m = Memory(nc, s, f"stage{len(done)}_")
                    m.sem_stack = kept
                    f(nc, m, t, *args)
                for sem in m.sems:
                    nc.gpsimd.sem_clear(sem)
                nc.all_engine_barrier()

        stage(prepare_edges, src, dst, rel, x, d)
        stage(relation_table, d, w1, sl1, b1, True)
        stage(aggregate, d, True)
        stage(relation_table, d, w2, sl1, b1, False)
        stage(aggregate, d, False)
        stage(project, d, sl2, b2, wq, wk, wv, bq, bk, bv, g1, be1)
        t["scores"] = keep.sb("scores", [P, K * H])
        t["node_max"] = keep.sb("node_max", [P, W * H])
        t["node_sum"] = keep.sb("node_sum", [P, W * H])
        stage(score, d, curv, wc, bc)
        stage(maxima)
        stage(exponentials)
        stage(scatter, d)
        stage(finish, d, wo, bo, g2, be2, wf1, bf1, wf2, bf2, out)


_INS = ["x", "src", "dst", "edge_attr_128", "edge_type_8",
        "L0_gnn_w1", "L0_gnn_sl1", "L0_gnn_b1", "L0_gnn_w2", "L0_gnn_sl2", "L0_gnn_b2",
        "L1_gnn_Wq", "L1_gnn_bq", "L1_gnn_Wk", "L1_gnn_bk", "L1_gnn_Wv", "L1_gnn_bv",
        "L1_gnn_Wo", "L1_gnn_bo", "L1_gnn_Wc", "L1_gnn_bc", "L1_gnn_W1", "L1_gnn_b1",
        "L1_gnn_W2", "L1_gnn_b2", "L1_gnn_g1", "L1_gnn_be1", "L1_gnn_g2", "L1_gnn_be2"]


def kernel(**inputs):
    import numpy as _np
    import concourse.bacc as _bacc
    from concourse import mybir as _mybir
    from concourse.bass_utils import run_bass_kernel_spmd as _run

    nc = _bacc.Bacc("TRN2", target_bir_lowering=False, num_devices=1)
    arrays, args = {}, []
    for name in _INS:
        a = _np.ascontiguousarray(inputs[name])
        arrays[f"in_{name}_dram"] = a
        args.append(nc.dram_tensor(f"in_{name}_dram", a.shape, _mybir.dt.from_np(a.dtype), kind="ExternalInput").ap())
    args.append(nc.dram_tensor("out_0_dram", (N, D), _mybir.dt.float32, kind="ExternalOutput").ap())
    build(nc, *args)
    r = _run(nc, [arrays], core_ids=[0])
    return r.results[0]["out_0_dram"]
```

```python
import concourse.bass as bass
from concourse import mybir
from contextlib import ExitStack

FP32 = mybir.dt.float32
I32 = mybir.dt.int32
I16 = mybir.dt.int16
BF16 = mybir.dt.bfloat16
ALU = mybir.AluOpType
ACT = mybir.ActivationFunctionType
AX = mybir.AxisListType

P = 128
N = 6250
E = 206250
D = 128
R = 8
H = 8
HD = D // H
FF = 4 * D
W = -(-N // P)
NT = W + W % 2
NP = NT * P
KC = -(-(E // P + W) // P)
K = KC * P
G = 4
SLOTS = 4
TURNS = K // (SLOTS * G)
GROUPS = K // G
EP = 125
BIG = 1.0e30
REP = 2 * G
EPS = 1e-5
DUMP = P


class Memory:

    def __init__(self, nc, stack, stage):
        self.nc, self.stack, self.stage = nc, stack, stage
        self.sem_stack, self.sems = stack, []

    def sb(self, name, shape, dt=FP32):
        return self.stack.enter_context(self.nc.sbuf_tensor(self.stage + name, shape, dt))

    def ps(self, name, shape, dt=FP32):
        return self.stack.enter_context(self.nc.psum_tensor(self.stage + name, shape, dt))

    def sem(self, name):
        self.sems.append(self.sem_stack.enter_context(self.nc.semaphore(self.stage + name)))
        return self.sems[-1]


def ring_index(pool, sem, value, passed):
    pool.wait_ge(sem, value)
    pool.sem_inc(passed, 1)


def prepare_edges(nc, m, t, src, dst, rel, x, d):
    dst_i = m.sb("dst_i", [EP, E // EP], I32)
    dst_f = m.sb("dst_f", [EP, E // EP])
    below = m.sb("below", [EP, E // EP])
    limit = m.sb("limit", [P, W + 1])
    count = m.sb("count", [EP, W + 1])
    ones = m.sb("ones_col", [P, 1])
    before = m.sb("before", [P, P])
    last_w = m.sb("last_w", [W, 1])
    wend = m.sb("wend", [W, 2])
    wn = m.sb("wn", [W, 1])
    wni = m.sb("wni", [W, 1], I32)
    wtile = m.sb("wtile", [W, 2])
    wval = m.sb("wval", [W, 3])
    tile_no, hot, started = (t["nodes_a"][0:W, a * K:(a + 1) * K] for a in range(3))
    tval = m.sb("tval", [P, KC, 3])
    tno = m.sb("tno", [P, KC])
    raw = m.sb("raw", [P, KC])
    start = m.sb("start", [P, KC])
    start_i = m.sb("start_i", [P, KC], I32)
    win_i = m.sb("win_i", [P, KC], I32)
    lead = m.sb("lead", [P, KC])
    until = m.sb("until", [P, KC])
    rows_i = [t["big"][:, a * K:(a + 1) * K].bitcast(I32) for a in range(3)]
    rows_f = [t["big"][:, a * K:(a + 1) * K].rearrange("p (c e) -> p c e", e=P) for a in range(3, 9)]
    valid = t["nodes_a"][:, 0:K].rearrange("p (c e) -> p c e", e=P)
    dump = m.sb("dump", [P, P])
    first_zero = m.sb("zero_rows", [P, D])
    cnt_ps = m.ps("cnt_ps", [P, 512])
    tr_ps = [m.ps(f"tr_ps{b}", [P, 512]) for b in range(2)]
    s_dst, s_in, s_pool, s_v, s_pe, s_tab, s_tab2, s_tr, s_cp, s_pad = (
        m.sem(n) for n in ("p_dst", "p_in", "p_const", "p_vector", "p_tensor", "p_table",
                           "p_table_back", "p_transposed", "p_copied", "p_pad"))
    s_rows = t["landed"][0]
    add_landed(t, [3 * KC * 16, 0, 0, 0])
    s_cnt = m.sem("p_count")
    s_link = m.sem("p_link")
    passed = m.sem("p_passed")
    CH = [(c0, min(G, KC - c0)) for c0 in range(0, KC, G)]
    CONV, COUNTED, WEND, WN, WVAL, TVAL, START, SIX = range(1, 9)

    block = m.stack.enter_context(nc.Block())

    @block.sync
    def _(sp):
        sp.dma_start(dst_i[:, :], dst.rearrange("(p n) -> p n", p=EP)).then_inc(s_dst, 16)
        sp.dma_start(d["xpad"][0:N, :], x).then_inc(s_pad, 16)
        sp.wait_ge(s_pool, 2)
        for n0 in range(N, NP + P, P):
            n1 = min(n0 + P, NP + P)
            sp.dma_start(d["xpad"][n0:n1, :], first_zero[0:n1 - n0, :]).then_inc(s_pad, 16)
        sp.wait_ge(s_v, START)
        with nc.allow_non_contiguous_dma(reason="a few thousand words, once"):
            sp.dma_start(d["tiles"][0].rearrange("(c p) -> p c", p=P), start_i[:, :]).then_inc(s_tab, 16)
            sp.dma_start(d["tiles"][1].rearrange("(c p) -> p c", p=P), win_i[:, :]).then_inc(s_tab, 16)
        sp.wait_ge(s_tab, 32)
        sp.dma_start(t["first_edge"][:, :], d["tiles"][0:1, :]).then_inc(s_tab2, 16)
        sp.dma_start(t["window"][:, :], d["tiles"][1:2, :]).then_inc(s_tab2, 16)
        sp.wait_ge(s_tab2, 32)
        sp.wait_ge(s_pad, 16 * (1 + len(range(N, NP + P, P))))

    @block.gpsimd
    def _(pool):
        pool.memset(first_zero[:, :], 0.0).then_inc(s_pool, 1)
        pool.memset(ones[:, :], 1.0).then_inc(s_pool, 1)
        pool.memset(t["ident"][:, :], 0.0).then_inc(s_pool, 1)
        pool.memset(before[:, :], 1.0).then_inc(s_pool, 1)
        pool.memset(t["earlier"][:, :], 1.0).then_inc(s_pool, 1)
        pool.memset(last_w[:, :], 0.0).then_inc(s_pool, 1)
        pool.wait_ge(s_pool, 6)
        pool.affine_select(out=t["ident"][:, :], in_=t["ident"][:, :], compare_op=ALU.not_equal, fill=1.0,
                           base=0, pattern=[[-1, P]], channel_multiplier=1).then_inc(s_pool, 1)
        pool.affine_select(out=before[:, :], in_=before[:, :], compare_op=ALU.is_gt, fill=0.0,
                           base=0, pattern=[[1, P]], channel_multiplier=-1).then_inc(s_pool, 1)
        pool.affine_select(out=t["earlier"][:, :], in_=t["earlier"][:, :], compare_op=ALU.is_gt, fill=0.0,
                           base=0, pattern=[[-1, P]], channel_multiplier=1).then_inc(s_pool, 1)
        pool.affine_select(out=last_w[:, :], in_=last_w[:, :], compare_op=ALU.not_equal, fill=float(K * P),
                           base=-(W - 1), pattern=[[0, 1]], channel_multiplier=1).then_inc(s_pool, 1)
        f = dict(allow_small_or_imprecise_dtypes=True)
        pool.iota(limit[:, :], pattern=[[P, W + 1]], base=0, channel_multiplier=0, **f).then_inc(s_pool, 1)
        pool.iota(tile_no[:, :], pattern=[[1, K]], base=0, channel_multiplier=0, **f).then_inc(s_pool, 1)
        pool.iota(tno[:, :], pattern=[[P * P, KC]], base=0, channel_multiplier=P, **f).then_inc(s_pool, 1)
        pool.iota(t["iota"][:, :], pattern=[[1, P]], base=0, channel_multiplier=0, **f).then_inc(s_pool, 1)
        pool.iota(t["iota16"][:, :], pattern=[[1, P]], base=0, channel_multiplier=0, **f).then_inc(s_pool, 1)
        pool.iota(t["lane"][:, :], pattern=[[0, 1]], base=0, channel_multiplier=1, **f).then_inc(s_pool, 1)
        pool.iota(dump[:, :], pattern=[[1, P]], base=N, channel_multiplier=0, **f).then_inc(s_pool, 1)
        pool.iota(t["dump_row"][:, :], pattern=[[0, 1]], base=N, channel_multiplier=1, **f).then_inc(s_pool, 1)
        pool.iota(wval[:, 2:3], pattern=[[0, 1]], base=0, channel_multiplier=1, **f).then_inc(s_pool, 1)
        pool.wait_ge(s_v, START)
        for a, v in enumerate((src, dst, rel)):
            for c in range(KC):
                pool.indirect_dma_start(
                    rows_i[a][:, c * P:(c + 1) * P], None, v.rearrange("(e a) -> e a", a=1),
                    bass.IndirectOffsetOnAxis(ap=start_i[:, c:c + 1], axis=0)).then_inc(s_rows, 16)

    POOL_DONE = 19

    @block.tensor
    def _(pe):
        pe.wait_ge(s_v, COUNTED)
        pe.wait_ge(s_pool, POOL_DONE)
        for j in range(2):
            nc.tensor.matmul(cnt_ps[0:W, j:j + 1], count[:, j:j + W], ones[0:EP, :],
                             start=True, stop=True).then_inc(s_pe, 1)
        pe.wait_ge(s_v, WN)
        nc.tensor.matmul(cnt_ps[0:W, 2:3], before[0:W, 0:W], wn[:, :], start=True, stop=True).then_inc(s_pe, 1)
        pe.wait_ge(s_v, WVAL)
        for c in range(KC):
            last = nc.tensor.matmul(cnt_ps[:, 16 + 3 * c:19 + 3 * c], hot[:, c * P:(c + 1) * P], wval[:, :],
                                    start=True, stop=True)
        last.then_inc(s_pe, 1)
        pe.wait_ge(s_v, SIX)
        n = 0
        for a in range(6):
            for c0, cn in CH:
                if n >= 2:
                    pe.wait_ge(s_cp, n - 1)
                for j in range(cn):
                    last = nc.tensor.transpose(tr_ps[n % 2][:, j * P:(j + 1) * P], rows_f[a][:, c0 + j, :],
                                               t["ident"][:, :])
                last.then_inc(s_tr, 1)
                n += 1

    @block.scalar
    def _(act):
        n = 0
        for a, name in enumerate(("row", "source", "source_or_dump", "target", "reset", "run_end")):
            for c0, cn in CH:
                act.wait_ge(s_tr, n + 1)
                nc.scalar.activation(t[name][:, c0 * P:(c0 + cn) * P], tr_ps[n % 2][:, 0:cn * P],
                                     ACT.Copy).then_inc(s_cp, 1)
                n += 1

    @block.vector
    def _(v):
        v.wait_ge(s_dst, 16)
        nc.vector.tensor_copy(dst_f[:, :], dst_i[:, :]).then_inc(s_v, 1)
        v.wait_ge(s_v, CONV)
        v.wait_ge(s_pool, POOL_DONE)
        with v.Fori(0, W + 1) as w:
            nc.vector.tensor_scalar(below[:, :], dst_f[:, :], limit[0:EP, bass.ds(w, 1)], 0.0, ALU.is_lt,
                                    ALU.add, accum_out=count[:, bass.ds(w, 1)]).then_inc(s_cnt, 1)
            v.wait_ge(s_cnt, w + 1)
        nc.vector.memset(below[:, 0:1], 0.0).then_inc(s_v, 1)
        v.wait_ge(s_pe, 2)
        nc.vector.tensor_copy(wend[:, :], cnt_ps[0:W, 0:2]).then_inc(s_v, 1)
        v.wait_ge(s_v, WEND)
        n = [0]

        def link(ins):
            n[0] += 1
            ins.then_inc(s_link, 1)
            v.wait_ge(s_link, n[0])

        link(nc.vector.scalar_tensor_tensor(wn[:, :], wend[:, 1:2], float(P - 1), wend[:, 0:1],
                                            ALU.add, ALU.subtract))
        link(nc.vector.tensor_copy(wni[:, :], wn[:, :]))
        link(nc.vector.tensor_scalar(wni[:, :], wni[:, :], 7, None, ALU.arith_shift_right))
        nc.vector.tensor_copy(wn[:, :], wni[:, :]).then_inc(s_v, 1)
        v.wait_ge(s_pe, 3)
        link(nc.vector.tensor_copy(wtile[:, 0:1], cnt_ps[0:W, 2:3]))
        link(nc.vector.tensor_tensor(wtile[:, 1:2], wtile[:, 0:1], wn[:, :], ALU.add))
        link(nc.vector.tensor_tensor(wtile[:, 1:2], wtile[:, 1:2], last_w[:, :], ALU.add))
        link(nc.vector.scalar_tensor_tensor(wval[:, 0:1], wtile[:, 0:1], -float(P), wend[:, 0:1],
                                            ALU.mult, ALU.add))
        link(nc.vector.tensor_copy(wval[:, 1:2], wend[:, 1:2]))
        link(nc.vector.tensor_scalar(started[:, :], tile_no[0:W, :], wtile[:, 0:1], None, ALU.is_ge))
        nc.vector.scalar_tensor_tensor(hot[:, :], tile_no[0:W, :], wtile[:, 1:2], started[:, :],
                                       ALU.is_lt, ALU.mult).then_inc(s_v, 1)
        v.wait_ge(s_pe, 4)
        nc.vector.tensor_copy(tval[:, :, :], cnt_ps[:, 16:16 + 3 * KC].rearrange("p (c v) -> p c v", v=3))\
            .then_inc(s_v, 1)
        v.wait_ge(s_v, TVAL)
        link(nc.vector.tensor_tensor(raw[:, :], tval[:, :, 0], tno[:, :], ALU.add))
        link(nc.vector.tensor_scalar(start[:, :], raw[:, :], float(E - P), None, ALU.min))
        link(nc.vector.tensor_tensor(lead[:, :], raw[:, :], start[:, :], ALU.subtract))
        link(nc.vector.tensor_tensor(until[:, :], tval[:, :, 1], start[:, :], ALU.subtract))
        link(nc.vector.tensor_copy(win_i[:, :], tval[:, :, 2]))
        nc.vector.tensor_copy(start_i[:, :], start[:, :]).then_inc(s_v, 1)

        def over_tiles(a):
            return a.unsqueeze(1).to_broadcast([P, KC, P])

        def over_edges(a):
            return a.unsqueeze(2).to_broadcast([P, KC, P])

        pos = over_tiles(t["iota"][:, :])
        link(nc.vector.tensor_tensor(rows_f[0][:, :, :], pos, over_edges(lead[:, :]), ALU.is_ge))
        link(nc.vector.tensor_tensor(valid[:, :, :], pos, over_edges(until[:, :]), ALU.is_lt))
        link(nc.vector.tensor_tensor(valid[:, :, :], valid[:, :, :], rows_f[0][:, :, :], ALU.mult))
        v.wait_ge(s_rows, 3 * KC * 16)
        srow, drow, trow = (r[:, :].rearrange("p (c e) -> p c e", e=P) for r in rows_i)
        row, source, sod, target, reset, run_end = rows_f
        link(nc.vector.tensor_copy(source[:, :, :], srow))
        link(nc.vector.tensor_copy(target[:, :, :], drow))
        link(nc.vector.tensor_copy(row[:, :, :], trow))
        link(nc.vector.scalar_tensor_tensor(row[:, :, :], source[:, :, :], float(R), row[:, :, :],
                                            ALU.mult, ALU.add))
        link(nc.vector.tensor_scalar(lead[:, :], tval[:, :, 2], float(P), None, ALU.mult))
        link(nc.vector.tensor_tensor(target[:, :, :], target[:, :, :], over_edges(lead[:, :]), ALU.subtract))
        link(nc.vector.scalar_tensor_tensor(target[:, :, :], target[:, :, :], 1.0, valid[:, :, :],
                                            ALU.add, ALU.mult))
        link(nc.vector.tensor_scalar(target[:, :, :], target[:, :, :], -1.0, None, ALU.add))
        link(nc.vector.tensor_tensor(sod[:, :, :], source[:, :, :], over_tiles(dump[:, :]), ALU.subtract))
        link(nc.vector.tensor_tensor(sod[:, :, :], sod[:, :, :], valid[:, :, :], ALU.mult))
        link(nc.vector.tensor_tensor(sod[:, :, :], sod[:, :, :], over_tiles(dump[:, :]), ALU.add))
        link(nc.vector.memset(run_end[:, :, :], 1.0))
        link(nc.vector.tensor_tensor(run_end[:, :, 0:P - 1], target[:, :, 1:P], target[:, :, 0:P - 1],
                                     ALU.not_equal))
        link(nc.vector.memset(reset[:, :, :], -BIG))
        nc.vector.tensor_scalar(reset[:, :, 1:P], run_end[:, :, 0:P - 1], -BIG, None, ALU.mult)\
            .then_inc(s_v, 1)


def two(i, h):
    return i * 2 + h


def relation_table(nc, m, t, d, w_all, self_w, bias, first):
    wrel = m.sb("wrel", [D, R * D])
    wself = m.sb("wself", [D, D])
    bcol = m.sb("bcol", [D, 1])
    xin = [m.sb(f"xin{h}", [P, D]) for h in range(2)]
    xts = [m.sb(f"xts{h}", [D, P]) for h in range(2)]
    summed = [m.sb(f"summed{h}", [D, P]) for h in range(2)]
    xo = [m.sb(f"xo{h}", [P, R * D]) for h in range(2)]
    ps_t = [m.ps(f"ps_t{h}", [P, 512]) for h in range(2)]
    ps_x = [[m.ps(f"ps_x{h}{j}", [P, 512]) for j in range(2)] for h in range(2)]
    HALF = R * D // 2
    s_w, s_t, s_sum, s_xts, s_x, s_keep, s_oa, s_ov, s_st, s_free, s_zero = (
        m.sem(n) for n in ("r_weights", "r_transposed", "r_summed", "r_slot", "r_product", "r_kept",
                           "r_out_scalar", "r_out_vector", "r_stored", "r_free", "r_zeroed"))
    s_in = [m.sem(f"r_in{h}") for h in range(2)]
    block = m.stack.enter_context(nc.Block())

    @block.sync
    def _(sp):
        sp.dma_start(wrel[:, :].rearrange("d (r e) -> d r e", r=R), w_all.rearrange("r d e -> d r e"))\
            .then_inc(s_w, 16)
        sp.dma_start(wself[:, :], self_w).then_inc(s_w, 16)
        with nc.allow_non_contiguous_dma(reason="a bias as a column"):
            sp.dma_start(bcol[:, :], bias.rearrange("(d a) -> d a", a=1)).then_inc(s_w, 16)
        sp.wait_ge(s_w, 48)
        if first:
            sp.dma_start(xin[0][:, :], d["xpad"][0:P, :]).then_inc(s_in[0], 16)
        sp.sem_inc(s_free, 2)
        with sp.Fori(0, NT // 2) as i:
            for h in range(2):
                g = two(i, h)
                if first:
                    sp.dma_start(xin[1 - h][:, :], d["xpad"][bass.ds((g + 1) * P, P), :])\
                        .then_inc(s_in[1 - h], 16)
                sp.wait_ge(s_oa, g + 1)
                sp.wait_ge(s_ov, g + 1)
                sp.dma_start(d["xt"][bass.ds(g * P, P), :], xo[h][:, :]).then_inc(s_st, 16)
                sp.wait_ge(s_st, g * 16 + 16)
                sp.sem_inc(s_free, 1)
        if first:
            sp.wait_ge(s_in[0], (NT // 2 + 1) * 16)

    @block.tensor
    def _(pe):
        pe.wait_ge(s_w, 48)
        with pe.Fori(0, NT // 2) as i:
            for h in range(2):
                g = two(i, h)
                pe.wait_ge(s_free, g + 1)
                if first:
                    pe.wait_ge(s_in[h], i * 16 + 16)
                    nc.tensor.transpose(ps_t[h][:, 0:P], xin[h][:, :], t["ident"][:, :]).then_inc(s_t, 1)
                else:
                    nc.tensor.matmul(ps_t[h][:, 0:P], wself[:, :], t["nodes_a"][:, bass.ds(g * P, P)],
                                     start=True, stop=True).then_inc(s_t, 1)
                pe.wait_ge(s_xts, g + 1)
                for j in range(2):
                    last = nc.tensor.matmul(ps_x[h][j][:, :], xts[h][:, :], wrel[:, j * HALF:(j + 1) * HALF],
                                            start=True, stop=True)
                last.then_inc(s_x, 1)

    @block.scalar
    def _(act):
        act.wait_ge(s_w, 48)
        with act.Fori(0, NT // 2) as i:
            for h in range(2):
                g = two(i, h)
                if first:
                    act.wait_ge(s_t, g + 1)
                    nc.scalar.activation(xts[h][:, :], ps_t[h][:, 0:P], ACT.Copy).then_inc(s_xts, 1)
                else:
                    act.wait_ge(s_sum, g + 1)
                    nc.scalar.activation(xts[h][:, :], summed[h][:, :], ACT.Relu, bias=bcol[:, :])\
                        .then_inc(s_xts, 1)
                act.wait_ge(s_x, g + 1)
                nc.scalar.activation(xo[h][:, 0:HALF], ps_x[h][0][:, :], ACT.Copy).then_inc(s_oa, 1)

    @block.vector
    def _(v):
        if first:
            nc.vector.memset(t["nodes_b"], 0.0).then_inc(s_zero, 1)
        with v.Fori(0, NT // 2) as i:
            for h in range(2):
                g = two(i, h)
                if first:
                    v.wait_ge(s_xts, g + 1)
                    nc.vector.tensor_copy(t["nodes_a"][:, bass.ds(g * P, P)], xts[h][:, :])\
                        .then_inc(s_keep, 1)
                else:
                    v.wait_ge(s_t, g + 1)
                    nc.vector.tensor_tensor(summed[h][:, :], ps_t[h][:, 0:P],
                                            t["nodes_b"][:, bass.ds(g * P, P)], ALU.add).then_inc(s_sum, 1)
                    v.wait_ge(s_xts, g + 1)
                    nc.vector.tensor_copy(t["nodes_a"][:, bass.ds(g * P, P)], xts[h][:, :])\
                        .then_inc(s_keep, 1)
                    nc.vector.tensor_scalar(t["nodes_b"][:, bass.ds(g * P, P)], summed[h][:, :], 0.0, None,
                                            ALU.mult).then_inc(s_zero, 1)
                v.wait_ge(s_x, g + 1)
                nc.vector.tensor_copy(xo[h][:, HALF:2 * HALF], ps_x[h][1][:, :]).then_inc(s_ov, 1)


class Group:

    def __init__(self, i, q):
        self.i, self.q = i, q

    def at(self, k=0):
        return self.i * SLOTS + (self.q + k)

    def turn(self, k=0):
        return self.i + (self.q + k) // SLOTS

    def slot(self, k=0, n=SLOTS):
        return (self.q + k) % n

    def live(self, k=0):
        return not isinstance(self.i, int) or 0 <= self.at(k) < GROUPS


def walk(engine, body, before, after):
    for g in range(-before, SLOTS):
        body(Group(g // SLOTS, g % SLOTS))
    with engine.Fori(1, TURNS - 1) as i:
        for q in range(SLOTS):
            body(Group(i, q))
    for g in range(GROUPS - SLOTS, GROUPS + after):
        body(Group(g // SLOTS, g % SLOTS))


def aggregate(nc, m, t, d, zero_sums):
    index = [m.sb(f"index{q}", [P, G], I32) for q in range(SLOTS)]
    msg = [m.sb(f"msg{q}", [P, G, D]) for q in range(SLOTS)]
    hot = [m.sb(f"hot{q}", [P, G, P]) for q in range(2)]
    zero = m.sb("zero", [P, 10 * D]) if zero_sums else None
    ps = [m.ps(f"ps_agg{q}", [D, G, P]) for q in range(2)]
    s_index, s_hot, s_freed, s_acc, s_read, passed, s_z, s_zd = (
        m.sem(n) for n in ("a_index", "a_hot", "a_msg_free", "a_added", "a_ps_read",
                           "a_passed", "a_zero", "a_zeroed"))
    s_msg = t["landed"]
    at = add_landed(t, [TURNS * G * 16] * SLOTS)
    block = m.stack.enter_context(nc.Block())
    xt = d["xt"].rearrange("n (r e) -> (n r) e", r=R)

    if zero_sums:
        @block.sync
        def _(sp):
            sp.wait_ge(s_z, 1)
            n = 0
            for r in range(REP):
                for a in range(NP // (10 * P)):
                    sp.dma_start(d["sums"][r][a * 10 * P:(a + 1) * 10 * P, :].rearrange("(p j) e -> p (j e)", p=P),
                                 zero[:, :]).then_inc(s_zd, 16)
                    n += 1
            sp.wait_ge(s_zd, 16 * n)

    @block.scalar
    def _(act):
        with act.Fori(0, TURNS) as i:
            for q in range(SLOTS):
                g = i * SLOTS + q
                act.wait_ge(s_freed, g + 1)
                nc.scalar.activation(index[q][:, :], t["row"][:, bass.ds(g * G, G)], ACT.Copy)\
                    .then_inc(s_index, 1)

    @block.gpsimd
    def _(pool):
        with pool.Fori(0, TURNS) as i:
            for q in range(SLOTS):
                g = i * SLOTS + q
                ring_index(pool, s_index, g + 1, passed)
                for j in range(G):
                    pool.indirect_dma_start(msg[q][:, j, :], None, xt,
                                            bass.IndirectOffsetOnAxis(ap=index[q][:, j:j + 1], axis=0))\
                        .then_inc(s_msg[q], 16)

    @block.tensor
    def _(pe):
        pe.sem_inc(s_freed, SLOTS)
        with pe.Fori(0, TURNS) as i:
            for q in range(SLOTS):
                g = i * SLOTS + q
                pe.wait_ge(s_hot, g + 1)
                pe.wait_ge(s_read, g + 1)
                pe.wait_ge(s_msg[q], i * (16 * G) + (16 * G + at[q]))
                for j in range(G):
                    last = nc.tensor.matmul(ps[q % 2][:, j, :], msg[q][:, j, :], hot[q % 2][:, j, :],
                                            start=True, stop=True)
                last.then_inc(s_freed, 1)

    @block.vector
    def _(v):
        v.sem_inc(s_read, 2)
        if zero_sums:
            nc.vector.memset(zero[:, :], 0.0).then_inc(s_z, 1)

        def group(x):
            if x.live(1):
                v.wait_ge(s_freed, x.at(1) + SLOTS - 1)
                nc.vector.tensor_tensor(
                    hot[x.slot(1, 2)][:, :, :], t["iota16"][:, :].unsqueeze(1).to_broadcast([P, G, P]),
                    t["target"][:, bass.ds(x.at(1) * G, G)].unsqueeze(2).to_broadcast([P, G, P]),
                    ALU.is_equal).then_inc(s_hot, 1)
            if x.live():
                w = windows(nc, mybir.EngineType.DVE, t, x.at() * G, G)
                v.wait_ge(s_freed, x.at() + SLOTS + 1)
                for j in range(G):
                    into = t["nodes_b"][:, bass.ds(w[j] * P, P)]
                    nc.vector.tensor_tensor(into, into, ps[x.slot(0, 2)][:, j, :], ALU.add).then_inc(s_acc, 1)
                    v.wait_ge(s_acc, x.at() * G + j + 1)
                v.sem_inc(s_read, 1)

        walk(v, group, 1, 0)


def windows(nc, engine, t, tile, n):
    _, w = nc.values_load_multi_w_load_instructions(t["window"][0:1, bass.ds(tile, n)], engines=(engine,),
                                                    min_val=0, max_val=W - 1)
    return w


class Steps:

    def __init__(self, engine, sem, base, stood=None):
        self.engine, self.sem, self.base, self.stood, self.n = engine, sem, base, stood, 0

    def stand(self):
        self.engine.sem_inc(self.stood, 1)

    def __call__(self, instruction):
        self.n += 1
        instruction.then_inc(self.sem, 1)
        self.engine.wait_ge(self.sem, self.base + self.n)


def normalize(nc, v, step, out, in_, stats, moments, s_var, s_std, turn):
    step(nc.vector.bn_stats(stats, in_))
    step.stand()
    nc.vector.bn_aggr(moments, stats).then_inc(s_var, 1)
    v.wait_ge(s_std, turn)
    step(nc.vector.reciprocal(moments[:, 1:2], moments[:, 1:2]))
    return nc.vector.tensor_scalar(out, in_, moments[:, 0:1], moments[:, 1:2], ALU.subtract, ALU.mult)


def deviation(nc, act, moments, eps, s_var, s_std, turn):
    act.wait_ge(s_var, turn)
    nc.scalar.activation(moments[:, 1:2], moments[:, 1:2], ACT.Sqrt, bias=eps).then_inc(s_std, 1)


def add_landed(t, counts):
    before = list(t["landed_at"])
    t["landed_at"] = [a + b for a, b in zip(before, counts)]
    return before


def rows_of(v):
    return v.partition_broadcast(P)


def project(nc, m, t, d, self_w, bias, wq, wk, wv, bq, bk, bv, g1, be1):
    wself = m.sb("wself", [D, D])
    wqkv = m.sb("wqkv", [D, 3 * D])
    bcol = m.sb("bcol", [D, 1])
    bqkv = m.sb("bqkv", [P, 3 * D])
    gain = m.sb("gain", [P, D])
    shift = m.sb("shift", [P, D])
    two_of = lambda n, shape: [m.sb(f"{n}{h}", shape) for h in range(2)]
    xin, summed, ht, y, xl, n1, n1t, qkv = (two_of(n, [P, D]) for n in (
        "xin", "summed", "ht", "y", "xl", "n1", "n1t", "qo"))
    vo = two_of("vo", [P, D])
    stats, moments = two_of("stats", [P, 6]), two_of("moments", [P, 2])
    ps_a, ps_b, ps_c, ps_d = ([m.ps(f"{n}{h}", [P, 512]) for h in range(2)] for n in (
        "ps_self", "ps_rows", "ps_normed", "ps_qkv"))
    s_w, s_self, s_sum, s_ht, s_rows, s_norm, s_nt, s_n1t, s_qkv, s_out, s_step, s_st, s_free = (
        m.sem(n) for n in ("q_weights", "q_self", "q_summed", "q_relu", "q_rows", "q_normed",
                           "q_normed_t", "q_slot", "q_product", "q_out", "q_step", "q_stored", "q_free"))
    s_in = [m.sem(f"q_in{h}") for h in range(2)]
    s_stood = m.sem("q_stood")
    s_var, s_std, s_eps = m.sem("q_variance"), m.sem("q_deviation"), m.sem("q_eps")
    eps = m.sb("eps", [P, 1])
    STEPS = 10
    block = m.stack.enter_context(nc.Block())

    @block.sync
    def _(sp):
        n = 0
        for out, in_ in ((wself[:, :], self_w), (wqkv[:, 0:D], wq), (wqkv[:, D:2 * D], wk),
                         (wqkv[:, 2 * D:3 * D], wv), (bqkv[:, 0:D], rows_of(bq)),
                         (bqkv[:, D:2 * D], rows_of(bk)), (bqkv[:, 2 * D:3 * D], rows_of(bv)),
                         (gain[:, :], rows_of(g1)), (shift[:, :], rows_of(be1))):
            sp.dma_start(out, in_).then_inc(s_w, 16)
            n += 1
        with nc.allow_non_contiguous_dma(reason="a bias as a column"):
            sp.dma_start(bcol[:, :], bias.rearrange("(d a) -> d a", a=1)).then_inc(s_w, 16)
        sp.wait_ge(s_w, 16 * (n + 1))
        sp.dma_start(xin[0][:, :], d["xpad"][0:P, :]).then_inc(s_in[0], 16)
        sp.sem_inc(s_free, 2)
        with sp.Fori(0, NT // 2) as i:
            for h in range(2):
                g = two(i, h)
                sp.dma_start(xin[1 - h][:, :], d["xpad"][bass.ds((g + 1) * P, P), :]).then_inc(s_in[1 - h], 16)
                sp.wait_ge(s_out, g + 1)
                sp.dma_start(d["q"][bass.ds(g * P, P), :], qkv[h][:, :]).then_inc(s_st, 16)
                sp.dma_start(d["xl"][bass.ds(g * P, P), :], xl[h][:, :]).then_inc(s_st, 16)
                sp.dma_start(d["v"][bass.ds(g * P, P), :], vo[h][:, :]).then_inc(s_st, 16)
                sp.wait_ge(s_st, g * 48 + 48)
                sp.sem_inc(s_free, 1)
        sp.wait_ge(s_in[0], (NT // 2 + 1) * 16)

    @block.tensor
    def _(pe):
        pe.wait_ge(s_w, 160)
        with pe.Fori(0, NT // 2) as i:
            for h in range(2):
                g = two(i, h)
                pe.wait_ge(s_free, g + 1)
                nc.tensor.matmul(ps_a[h][:, 0:P], wself[:, :], t["nodes_a"][:, bass.ds(g * P, P)],
                                 start=True, stop=True).then_inc(s_self, 1)
                pe.wait_ge(s_ht, g + 1)
                nc.tensor.transpose(ps_b[h][:, 0:D], ht[h][:, :], t["ident"][:, :]).then_inc(s_rows, 1)
                pe.wait_ge(s_norm, g + 1)
                nc.tensor.transpose(ps_c[h][:, 0:P], n1[h][:, :], t["ident"][:, :]).then_inc(s_nt, 1)
                pe.wait_ge(s_n1t, g + 1)
                nc.tensor.matmul(ps_d[h][:, 0:3 * D], n1t[h][:, :], wqkv[:, :], start=True, stop=True)\
                    .then_inc(s_qkv, 1)

    @block.gpsimd
    def _(pool):
        pool.memset(eps[:, :], EPS).then_inc(s_eps, 1)

    @block.scalar
    def _(act):
        act.wait_ge(s_eps, 1)
        act.wait_ge(s_w, 160)
        with act.Fori(0, NT // 2) as i:
            for h in range(2):
                g = two(i, h)
                act.wait_ge(s_sum, g + 1)
                nc.scalar.activation(ht[h][:, :], summed[h][:, :], ACT.Relu, bias=bcol[:, :]).then_inc(s_ht, 1)
                for a in range(2):
                    deviation(nc, act, moments[h], eps[:, :], s_var, s_std, g * 2 + 1 + a)
                act.wait_ge(s_nt, g + 1)
                nc.scalar.activation(n1t[h][:, :], ps_c[h][:, 0:P], ACT.Copy).then_inc(s_n1t, 1)

    @block.vector
    def _(v):
        v.wait_ge(s_w, 160)
        with v.Fori(0, NT // 2) as i:
            for h in range(2):
                g = two(i, h)
                step = Steps(v, s_step, g * STEPS, s_stood)
                v.wait_ge(s_self, g + 1)
                nc.vector.tensor_tensor(summed[h][:, :], ps_a[h][:, 0:P], t["nodes_b"][:, bass.ds(g * P, P)],
                                        ALU.add).then_inc(s_sum, 1)
                v.wait_ge(s_in[h], i * 16 + 16)
                v.wait_ge(s_rows, g + 1)
                step(nc.vector.tensor_tensor(y[h][:, :], ps_b[h][:, 0:D], xin[h][:, :], ALU.add))
                step(normalize(nc, v, step, xl[h][:, :], y[h][:, :], stats[h][:, :], moments[h][:, :],
                               s_var, s_std, g * 2 + 1))
                step(normalize(nc, v, step, n1[h][:, :], xl[h][:, :], stats[h][:, :], moments[h][:, :],
                               s_var, s_std, g * 2 + 2))
                step(nc.vector.tensor_tensor(n1[h][:, :], n1[h][:, :], gain[:, :], ALU.mult))
                nc.vector.tensor_tensor(n1[h][:, :], n1[h][:, :], shift[:, :], ALU.add).then_inc(s_norm, 1)
                v.wait_ge(s_qkv, g + 1)
                step(nc.vector.tensor_tensor(qkv[h][:, :], ps_d[h][:, 0:D], bqkv[:, 0:D], ALU.add))
                step(nc.vector.tensor_scalar(qkv[h][:, :], qkv[h][:, :], HD ** -0.5, None, ALU.mult))
                nc.vector.tensor_tensor(t["nodes_a"][:, bass.ds(g * P, P)], ps_d[h][:, D:2 * D],
                                        bqkv[:, D:2 * D], ALU.add)
                nc.vector.tensor_tensor(vo[h][:, :], ps_d[h][:, 2 * D:3 * D],
                                        bqkv[:, 2 * D:3 * D], ALU.add).then_inc(s_out, 1)
                assert step.n == STEPS


def score(nc, m, t, d, curv, wc, bc):
    slots = lambda n, k, shape, dt=FP32: [m.sb(f"{n}{q}", shape, dt) for q in range(k)]
    GH = G * H
    index = slots("index", SLOTS, [P, G], I32)
    qrow = slots("qrow", SLOTS, [P, G * D])
    cur = slots("cur", SLOTS, [P, G, D])
    tgt = slots("tgt", 2, [P, G])
    far = slots("far", 2, [P, G * P])
    of_node = slots("of_node", 2, [P, G * P])
    cur_t = slots("cur_t", 2, [D, G * P])
    prod = slots("prod", 1, [P, G * D]) * 2
    qk = slots("qk", 2, [P, GH])
    sc = slots("sc", 2, [P, GH])
    rs = slots("rs", 2, [P, G, H])
    sc_t = slots("sc_t", 2, [GH, P])
    rs_t = slots("rs_t", 2, [GH, P + 1])
    run = slots("run", 2, [GH, P])
    top = slots("top", 2, [GH, P])
    less = slots("less", 2, [GH, P])
    ex = slots("ex", 2, [GH, P])
    hot = slots("hot", 2, [P, G, P])
    ends = slots("ends", 2, [P, G, 2 * H + 1])
    pen = slots("pen", 2, [P, G])
    wc_sb = m.sb("wc_sb", [D, H])
    bias = m.sb("bias", [GH, 1])
    minus = m.sb("minus_lane", [P, 1])
    ps_t, ps_c, ps_s, ps_m, ps_b, ps_e = (m.ps(n, [P, 512]) for n in (
        "ps_tgt", "ps_cur", "ps_score", "ps_runs", "ps_back", "ps_ends"))
    ps_k = [m.ps(f"ps_key{h}", [P, 512]) for h in range(2)]
    (s_w, s_index, s_slot, s_freed, s_pt, s_pc, s_far, s_node, s_ct, s_k, s_s, s_prod, s_qk, s_sc, passed,
     s_pm, s_sct, s_rst, s_run, s_top, s_less, s_ex, s_back, s_copies, s_ends, s_hot, s_e, s_pen, s_out,
     s_edge, s_minus) = (
        m.sem("s_" + n) for n in (
            "weights", "index", "slots", "slot_free", "target_t", "curv_t", "far", "of_node", "curv_slot",
            "key", "curv_score", "products", "qk", "scores", "passed", "runs_t", "scores_slot",
            "reset_slot", "run", "top", "less", "exp", "back", "end_copies", "ends", "hot", "sums",
            "penalty", "out", "edge", "minus"))
    s_passed_pe = m.sem("s_passed_pe")
    s_c = [m.sem(f"s_c{q}") for q in range(SLOTS)]
    s_st = [m.sem(f"s_st{h}") for h in range(2)]
    s_q = t["landed"]
    at = add_landed(t, [TURNS * G * 16] * SLOTS)
    block = m.stack.enter_context(nc.Block())

    @block.sync
    def _(sp):
        sp.dma_start(wc_sb[:, :], wc).then_inc(s_w, 16)
        with nc.allow_non_contiguous_dma(reason="a bias as a column"):
            for j in range(G):
                sp.dma_start(bias[j * H:(j + 1) * H, :], bc.rearrange("(h a) -> h a", a=1)).then_inc(s_w, 16)
        with sp.Fori(0, TURNS) as i:
            for q in range(SLOTS):
                g = i * SLOTS + q
                _, first = nc.values_load_multi_w_load_instructions(
                    t["first_edge"][0:1, bass.ds(g * G, G)], engines=(mybir.EngineType.SP,), min_val=0,
                    max_val=E - P)
                sp.wait_ge(s_freed, g + 1)
                for j in range(G):
                    sp.dma_start(cur[q][:, j, :], curv[bass.ds(first[j], P), :]).then_inc(s_c[q], 16)

    @block.gpsimd
    def _(pool):
        pool.memset(rs_t[0][:, P:P + 1], -BIG).then_inc(s_edge, 1)
        pool.memset(rs_t[1][:, P:P + 1], -BIG).then_inc(s_edge, 1)
        with pool.Fori(0, TURNS) as i:
            for q in range(SLOTS):
                g = i * SLOTS + q
                ring_index(pool, s_index, g + 1, passed)
                for j in range(G):
                    pool.indirect_dma_start(qrow[q][:, j * D:(j + 1) * D], None, d["q"],
                                            bass.IndirectOffsetOnAxis(ap=index[q][:, j:j + 1], axis=0))\
                        .then_inc(s_q[q], 16)

    @block.scalar
    def _(act):
        act.wait_ge(s_w, 16 * (G + 1))
        nc.scalar.activation(minus[:, :], t["lane"][:, :], ACT.Copy, scale=-1.0).then_inc(s_minus, 1)
        act.wait_ge(s_minus, 1)

        def group(x):
            if x.live(2):
                act.wait_ge(s_freed, x.at(2) + 1)
                nc.scalar.activation(index[x.slot(2)][:, :], t["source"][:, bass.ds(x.at(2) * G, G)],
                                     ACT.Copy).then_inc(s_index, 1)
            if x.live(1):
                nc.scalar.activation(tgt[x.slot(1, 2)][:, :], t["target"][:, bass.ds(x.at(1) * G, G)],
                                     ACT.Copy).then_inc(s_slot, 1)
            if x.live(-1):
                h = x.slot(-1, 2)
                act.wait_ge(s_pm, x.at(-1) + 1)
                nc.scalar.activation(sc_t[h][:, :], ps_m[0:GH, 0:P], ACT.Identity, bias=bias[:, :])\
                    .then_inc(s_sct, 1)
                nc.scalar.activation(rs_t[h][:, 0:P], ps_m[0:GH, P:2 * P], ACT.Copy).then_inc(s_rst, 1)
            if x.live(1):
                h = x.slot(1, 2)
                act.wait_ge(s_pt, x.at(1) + 1)
                nc.scalar.activation(far[h][:, :], ps_t[:, :], ACT.Abs, bias=minus[:, :]).then_inc(s_far, 1)
                act.wait_ge(s_far, x.at(1) + 1)
                nc.scalar.activation(of_node[h][:, :], far[h][:, :], ACT.Relu, bias=1.0, scale=-1.0)\
                    .then_inc(s_node, 1)
                act.wait_ge(s_pc, x.at(1) + 1)
                nc.scalar.activation(cur_t[h][:, :], ps_c[:, :], ACT.Copy).then_inc(s_ct, 1)
            if x.live(-1):
                h = x.slot(-1, 2)
                act.wait_ge(s_less, x.at(-1) + 1)
                if x.live(-3):
                    act.wait_ge(s_st[h], (x.i * 2 + (x.q - 3) // 2) * 16 + 16)
                nc.scalar.activation(ex[h][:, :], less[h][:, :], ACT.Exp).then_inc(s_ex, 1)
                act.wait_ge(s_ex, x.at(-1) + 1)
                act.dma_start(d["exp"][bass.ds(x.at(-1) * GH, GH), :], ex[h][:, :]).then_inc(s_st[h], 16)

        walk(act, group, 2, 1)
        for h in range(2):
            act.wait_ge(s_st[h], GROUPS // 2 * 16)

    @block.tensor
    def _(pe):
        pe.wait_ge(s_w, 16 * (G + 1))

        def group(x):
            if x.live(-2):
                h = x.slot(-2, 2)
                pe.wait_ge(s_ex, x.at(-2) + 1)
                if x.live(-3):
                    pe.wait_ge(s_ends, x.at(-3) + 1)
                pe.sem_inc(s_passed_pe, 1)
                nc.tensor.transpose(ps_b[:, 0:GH], ex[h][:, :], t["ident"][0:GH, 0:GH])
                nc.tensor.transpose(ps_b[:, GH:2 * GH], top[h][:, :], t["ident"][0:GH, 0:GH])\
                    .then_inc(s_back, 1)
            if x.live(-1):
                h = x.slot(-1, 2)
                pe.wait_ge(s_sc, x.at(-1) * 2 + 2)
                if x.live(-2):
                    pe.wait_ge(s_rst, x.at(-2) + 1)
                nc.tensor.transpose(ps_m[0:GH, 0:P], sc[h][:, :], t["ident"][:, :])
                nc.tensor.transpose(ps_m[0:GH, P:2 * P], rs[h][:, :, :].rearrange("p a b -> p (a b)"),
                                    t["ident"][:, :]).then_inc(s_pm, 1)
            if x.live(1):
                h = x.slot(1, 2)
                pe.wait_ge(s_slot, x.at(1) + 1)
                if x.live():
                    pe.wait_ge(s_far, x.at() + 1)
                for j in range(G):
                    last = nc.tensor.transpose(ps_t[:, j * P:(j + 1) * P],
                                               tgt[h][:, j:j + 1].to_broadcast([P, P]), t["ident"][:, :])
                last.then_inc(s_pt, 1)
                pe.wait_ge(s_c[x.slot(1)], x.turn(1) * (16 * G) + 16 * G)
                if x.live():
                    pe.wait_ge(s_ct, x.at() + 1)
                for j in range(G):
                    last = nc.tensor.transpose(ps_c[:, j * P:(j + 1) * P], cur[x.slot(1)][:, j, :],
                                               t["ident"][:, :])
                last.then_inc(s_pc, 1)
            if x.live():
                h = x.slot(0, 2)
                w = windows(nc, mybir.EngineType.PE, t, x.at() * G, G)
                pe.wait_ge(s_node, x.at() + 1)
                for j in range(G):
                    last = nc.tensor.matmul(ps_k[h][:, j * D:(j + 1) * D], of_node[h][:, j * P:(j + 1) * P],
                                            t["nodes_a"][:, bass.ds(w[j] * P, P)], start=True, stop=True)
                last.then_inc(s_k, 1)
                pe.wait_ge(s_ct, x.at() + 1)
                if x.live(-1):
                    pe.wait_ge(s_sc, x.at(-1) * 2 + 2)
                for j in range(G):
                    last = nc.tensor.matmul(ps_s[:, j * H:(j + 1) * H], cur_t[h][:, j * P:(j + 1) * P],
                                            wc_sb[:, :], start=True, stop=True)
                last.then_inc(s_s, 1)
            if x.live(-2):
                h = x.slot(-2, 2)
                pe.wait_ge(s_hot, x.at(-2) + 1)
                pe.wait_ge(s_ends, x.at(-2) + 1)
                if x.live(-3):
                    pe.wait_ge(s_out, x.at(-3) * 2 + 2)
                for j in range(G):
                    last = nc.tensor.matmul(ps_e[:, j * (2 * H + 1):(j + 1) * (2 * H + 1)], hot[h][:, j, :],
                                            ends[h][:, j, :], start=True, stop=True)
                last.then_inc(s_e, 1)

        walk(pe, group, 1, 2)

    @block.vector
    def _(v):
        v.sem_inc(s_freed, SLOTS)
        v.wait_ge(s_edge, 2)

        def group(x):
            if x.live(-2):
                h = x.slot(-2, 2)
                run_end = t["run_end"][:, bass.ds(x.at(-2) * G, G)].unsqueeze(2)
                if x.live(-4):
                    v.wait_ge(s_e, x.at(-4) + 1)
                v.wait_ge(s_back, x.at(-2) + 1)
                nc.vector.tensor_copy(ends[h][:, :, 2 * H:2 * H + 1], run_end).then_inc(s_copies, 1)
                nc.vector.tensor_copy(ends[h][:, :, H:2 * H],
                                      ps_b[:, 0:GH].rearrange("p (j a) -> p j a", a=H)).then_inc(s_copies, 1)
                nc.vector.tensor_tensor(ends[h][:, :, 0:H], ps_b[:, GH:2 * GH].rearrange("p (j a) -> p j a", a=H),
                                        run_end.to_broadcast([P, G, H]), ALU.mult).then_inc(s_ends, 1)
            if x.live(-1):
                h = x.slot(-1, 2)
                v.wait_ge(s_sct, x.at(-1) + 1)
                v.wait_ge(s_rst, x.at(-1) + 1)
                nc.vector.tensor_tensor_scan(run[h][:, :], rs_t[h][:, 0:P], sc_t[h][:, :], -BIG, ALU.add,
                                             ALU.max).then_inc(s_run, 1)
                v.wait_ge(s_run, x.at(-1) + 1)
                nc.vector.tensor_tensor_scan(top[h][:, ::-1], rs_t[h][:, P:0:-1], run[h][:, ::-1], -BIG,
                                             ALU.add, ALU.max).then_inc(s_top, 1)
                v.wait_ge(s_top, x.at(-1) + 1)
                nc.vector.tensor_tensor(less[h][:, :], sc_t[h][:, :], top[h][:, :], ALU.subtract)\
                    .then_inc(s_less, 1)
            if x.live(-2):
                h = x.slot(-2, 2)
                nc.vector.tensor_tensor(
                    hot[h][:, :, :], t["iota16"][:, :].unsqueeze(1).to_broadcast([P, G, P]),
                    t["target"][:, bass.ds(x.at(-2) * G, G)].unsqueeze(2).to_broadcast([P, G, P]),
                    ALU.is_equal).then_inc(s_hot, 1)
            if x.live():
                h, q = x.slot(0, 2), x.slot()
                if x.live(-2):
                    v.wait_ge(s_pm, x.at(-2) + 1)
                nc.vector.tensor_copy(rs[h][:, :, :], t["reset"][:, bass.ds(x.at() * G, G)].unsqueeze(2)
                                      .to_broadcast([P, G, H])).then_inc(s_sc, 1)
                v.wait_ge(s_k, x.at() + 1)
                v.wait_ge(s_q[q], x.turn() * (16 * G) + (16 * G + at[q]))
                if x.live(-1):
                    v.wait_ge(s_qk, x.at(-1) + 1)
                nc.vector.tensor_tensor(prod[h][:, :], ps_k[h][:, :], qrow[q][:, :], ALU.mult).then_inc(s_prod, 1)
                v.wait_ge(s_prod, x.at() + 1)
                nc.vector.tensor_reduce(qk[h][:, :], prod[h][:, :].rearrange("p (a e) -> p a e", e=HD),
                                        AX.X, ALU.add).then_inc(s_qk, 1)
                v.wait_ge(s_qk, x.at() + 1)
                v.wait_ge(s_s, x.at() + 1)
                nc.vector.tensor_tensor(sc[h][:, :], qk[h][:, :], ps_s[:, 0:GH], ALU.add).then_inc(s_sc, 1)
                v.sem_inc(s_freed, 1)
            if x.live(-2):
                h = x.slot(-2, 2)
                v.wait_ge(s_e, x.at(-2) + 1)
                got = ps_e[:, 0:G * (2 * H + 1)].rearrange("p (j a) -> p j a", a=2 * H + 1)
                at_tile = bass.ds(x.at(-2) * GH, GH)
                nc.vector.tensor_copy(t["run_sum"][:, at_tile].rearrange("p (j a) -> p j a", a=H),
                                      got[:, :, H:2 * H]).then_inc(s_out, 1)
                nc.vector.tensor_scalar(pen[h][:, :].unsqueeze(2), got[:, :, 2 * H:2 * H + 1], BIG, -BIG,
                                        ALU.mult, ALU.add).then_inc(s_pen, 1)
                v.wait_ge(s_pen, x.at(-2) + 1)
                nc.vector.tensor_tensor(t["run_max"][:, at_tile].rearrange("p (j a) -> p j a", a=H),
                                        got[:, :, 0:H], pen[h][:, :].unsqueeze(2).to_broadcast([P, G, H]),
                                        ALU.add).then_inc(s_out, 1)

        walk(v, group, 0, 2)


def combine(nc, m, t):
    row = m.sb("row_f", [1, K])
    ones = m.sb("ones", [1, P])
    win = m.sb("win", [P, K])
    reset = m.sb("reset", [P, K + 1])
    go_on = m.sb("go_on", [P, K + 1])
    work = [m.sb(f"work{a}", [P, K]) for a in range(2)]
    ps = [m.ps(f"ps_win{c}", [P, 512]) for c in range(4)]
    s_v, s_pe, s_exp = m.sem("b_step"), m.sem("b_windows"), m.sem("b_exp")
    block = m.stack.enter_context(nc.Block())
    QK = K // 4
    n = [0]

    @block.tensor
    def _(pe):
        pe.wait_ge(s_v, 2)
        for c in range(4):
            last = nc.tensor.matmul(ps[c][:, 0:QK], ones[:, :], row[:, c * QK:(c + 1) * QK], start=True, stop=True)
        last.then_inc(s_pe, 1)

    exps = []

    @block.vector
    def _(v):
        def link(ins):
            n[0] += 1
            ins.then_inc(s_v, 1)
            v.wait_ge(s_v, n[0])

        link(nc.vector.tensor_copy(row[:, :], t["window"][:, :]))
        link(nc.vector.memset(ones[:, :], 1.0))
        v.wait_ge(s_pe, 1)
        for c in range(4):
            link(nc.vector.tensor_copy(win[:, c * QK:(c + 1) * QK], ps[c][:, 0:QK]))
        link(nc.vector.memset(go_on[:, :], 0.0))
        link(nc.vector.tensor_tensor(go_on[:, 1:K], win[:, 1:K], win[:, 0:K - 1], ALU.is_equal))
        link(nc.vector.tensor_scalar(reset[:, :], go_on[:, :], BIG, -BIG, ALU.mult, ALU.add))
        mx = t["run_max"].rearrange("p (k a) -> p k a", a=H)
        sm = t["run_sum"].rearrange("p (k a) -> p k a", a=H)
        a, b = work
        for h in range(H):
            link(nc.vector.tensor_tensor_scan(a[:, :], reset[:, 0:K], mx[:, :, h], -BIG, ALU.add, ALU.max))
            link(nc.vector.tensor_tensor_scan(b[:, ::-1], reset[:, K:0:-1], a[:, ::-1], -BIG, ALU.add, ALU.max))
            link(nc.vector.tensor_tensor(a[:, :], mx[:, :, h], b[:, :], ALU.subtract))
            exps.append(n[0])
            v.wait_ge(s_exp, h + 1)
            link(nc.vector.tensor_tensor(a[:, :], sm[:, :, h], mx[:, :, h], ALU.mult))
            link(nc.vector.tensor_tensor_scan(b[:, :], go_on[:, 0:K], a[:, :], 0.0, ALU.mult, ALU.add))
            link(nc.vector.tensor_tensor_scan(a[:, ::-1], go_on[:, K:0:-1], b[:, ::-1], 0.0, ALU.mult, ALU.max))
            link(nc.vector.tensor_scalar(a[:, :], a[:, :], 0.5, None, ALU.max))
            link(nc.vector.reciprocal(b[:, :], a[:, :]))
            link(nc.vector.tensor_tensor(mx[:, :, h], mx[:, :, h], b[:, :], ALU.mult))

    @block.scalar
    def _(act):
        mx = t["run_max"].rearrange("p (k a) -> p k a", a=H)
        first, per = 2 + 4 + 3 + 3, 9
        for h in range(H):
            act.wait_ge(s_v, first + h * per)
            nc.scalar.activation(mx[:, :, h], work[0][:, :], ACT.Exp).then_inc(s_exp, 1)


def scatter(nc, m, t, d):
    slots = lambda n, k, shape, dt=FP32: [m.sb(f"{n}{q}", shape, dt) for q in range(k)]
    GH = G * H
    index = slots("index", SLOTS, [P, G], I32)
    total = slots("total", SLOTS, [P, G * D])
    ex = slots("ex", SLOTS, [GH, P])
    tgt = slots("tgt", 2, [P, G])
    srcs = slots("srcs", 2, [P, G])
    far = slots("far", 2, [P, G * P])
    of_node = slots("of_node", 2, [P, G * P])
    pe_slot = slots("pexp", 2, [P, GH])
    prob = slots("prob", 2, [P, GH])
    same = slots("same", 2, [P, G, P])
    dup = slots("dup", 1, [P, G, P]) * 2
    dups = slots("dups", 2, [P, G])
    away = slots("away", 2, [P, G])
    away2 = slots("away2", 2, [P, G])
    msg = slots("msg", 2, [P, G * D])
    minus = m.sb("minus_lane", [P, 1])
    values = t["nodes_b"]
    ps_t, ps_q, ps_p, ps_f = (m.ps(n, [P, 512]) for n in ("ps_tgt", "ps_src", "ps_exp", "ps_factor"))
    ps_v, ps_o = ([m.ps(f"{n}{h}", [P, 512]) for h in range(2)] for n in ("ps_val", "ps_tot"))
    (s_val, s_slot, s_pt, s_ps, s_far, s_node, s_pexp, s_same, s_dup, s_dups, s_away, s_away2, s_index, s_f,
     s_v, s_prob, s_msg, s_o, s_tot, s_free, passed, s_minus) = (
        m.sem("c_" + n) for n in (
            "v_table", "slots", "target_t", "source_t", "far", "of_node", "exp_slot", "same", "dup", "dups",
            "away", "away2", "index", "factor", "values", "prob", "msg", "product", "total", "total_free",
            "passed", "minus"))
    s_ex = [m.sem(f"c_exp{q}") for q in range(SLOTS)]
    s_sc = t["landed"]
    at = add_landed(t, [TURNS * 2 * G * 16] * 2 + [0, 0])
    block = m.stack.enter_context(nc.Block())

    @block.sync
    def _(sp):
        sp.dma_start(values.rearrange("p (a e) -> p a e", e=D), d["v"].rearrange("(a p) e -> p a e", p=P))\
            .then_inc(s_val, 16)

        def group(x):
            q = x.slot()
            if x.live(-SLOTS):
                sp.wait_ge(s_ps, x.at(-SLOTS) + 1)
            sp.dma_start(ex[q][:, :], d["exp"][bass.ds(x.at() * GH, GH), :]).then_inc(s_ex[q], 16)

        walk(sp, group, 0, 0)

    @block.scalar
    def _(act):
        nc.scalar.activation(minus[:, :], t["lane"][:, :], ACT.Copy, scale=-1.0).then_inc(s_minus, 1)
        act.wait_ge(s_minus, 1)

        def group(x):
            if x.live(1):
                h = x.slot(1, 2)
                if x.live(-1):
                    act.wait_ge(s_index, x.at(-1) + 1)
                nc.scalar.activation(tgt[h][:, :], t["target"][:, bass.ds(x.at(1) * G, G)], ACT.Copy)\
                    .then_inc(s_slot, 1)
                nc.scalar.activation(srcs[h][:, :], t["source_or_dump"][:, bass.ds(x.at(1) * G, G)],
                                     ACT.Copy).then_inc(s_slot, 1)
                act.wait_ge(s_pt, x.at(1) + 1)
                nc.scalar.activation(far[h][:, :], ps_t[:, :], ACT.Abs, bias=minus[:, :]).then_inc(s_far, 1)
                act.wait_ge(s_far, x.at(1) + 1)
                if x.live(-1):
                    act.wait_ge(s_v, x.at(-1) + 1)
                nc.scalar.activation(of_node[h][:, :], far[h][:, :], ACT.Relu, bias=1.0, scale=-1.0)\
                    .then_inc(s_node, 1)
                act.wait_ge(s_ps, x.at(1) + 1)
                if x.live(-1):
                    act.wait_ge(s_prob, x.at(-1) + 1)
                nc.scalar.activation(pe_slot[h][:, :], ps_p[:, 0:GH], ACT.Copy).then_inc(s_pexp, 1)
            if x.live():
                h, q = x.slot(0, 2), x.slot()
                act.wait_ge(s_free, x.at() + 1)
                act.wait_ge(s_o, x.at() + 1)
                nc.scalar.activation(total[q][:, :], ps_o[h][:, :], ACT.Copy).then_inc(s_tot, 1)

        walk(act, group, 1, 0)

    @block.gpsimd
    def _(pool):
        pool.sem_inc(s_free, SLOTS)

        def group(x):
            h, q = x.slot(0, 2), x.slot()
            pool.wait_ge(s_index, x.at() + 1)
            ring_index(pool, s_tot, x.at() + 1, passed)
            for j in range(G):
                pool.indirect_dma_start(d["sums"][h * G + j],
                                        bass.IndirectOffsetOnAxis(ap=index[q][:, j:j + 1], axis=0),
                                        total[q][:, j * D:(j + 1) * D], None, compute_op=ALU.add)\
                    .then_inc(s_sc[h], 16)
            if x.live(-1):
                n = (x.i * 2 + (x.q - 1) // 2) * (16 * G) + (16 * G + at[1 - h])
                ring_index(pool, s_sc[1 - h], n, s_free)

        walk(pool, group, 0, 0)
        for h in range(2):
            pool.wait_ge(s_sc[h], TURNS * 2 * 16 * G + at[h])

    @block.tensor
    def _(pe):
        pe.wait_ge(s_val, 16)

        def group(x):
            if x.live():
                h = x.slot(0, 2)
                w = windows(nc, mybir.EngineType.PE, t, x.at() * G, G)
                pe.wait_ge(s_node, x.at() + 1)
                if x.live(-1):
                    pe.wait_ge(s_prob, x.at(-1) + 1)
                for j in range(G):
                    last = nc.tensor.matmul(ps_f[:, j * H:(j + 1) * H], of_node[h][:, j * P:(j + 1) * P],
                                            t["run_max"][:, bass.ds(x.at() * GH + j * H, H)],
                                            start=True, stop=True)
                last.then_inc(s_f, 1)
                for j in range(G):
                    last = nc.tensor.matmul(ps_v[h][:, j * D:(j + 1) * D], of_node[h][:, j * P:(j + 1) * P],
                                            values[:, bass.ds(w[j] * P, P)], start=True, stop=True)
                last.then_inc(s_v, 1)
            if x.live(1):
                h = x.slot(1, 2)
                pe.wait_ge(s_slot, x.at(1) * 2 + 2)
                if x.live():
                    pe.wait_ge(s_far, x.at() + 1)
                for j in range(G):
                    last = nc.tensor.transpose(ps_t[:, j * P:(j + 1) * P],
                                               tgt[h][:, j:j + 1].to_broadcast([P, P]), t["ident"][:, :])
                last.then_inc(s_pt, 1)
                if x.live():
                    pe.wait_ge(s_same, x.at() + 1)
                    pe.wait_ge(s_pexp, x.at() + 1)
                pe.wait_ge(s_ex[x.slot(1)], x.turn(1) * 16 + 16)
                for j in range(G):
                    nc.tensor.transpose(ps_q[:, j * P:(j + 1) * P],
                                        srcs[h][:, j:j + 1].to_broadcast([P, P]), t["ident"][:, :])
                nc.tensor.transpose(ps_p[:, 0:GH], ex[x.slot(1)][:, :], t["ident"][0:GH, 0:GH]).then_inc(s_ps, 1)
            if x.live():
                h = x.slot(0, 2)
                pe.wait_ge(s_msg, x.at() + 1)
                pe.wait_ge(s_same, x.at() + 1)
                if x.live(-2):
                    pe.wait_ge(s_tot, x.at(-2) + 1)
                for j in range(G):
                    last = nc.tensor.matmul(ps_o[h][:, j * D:(j + 1) * D], same[h][:, j, :],
                                            msg[h][:, j * D:(j + 1) * D], start=True, stop=True)
                last.then_inc(s_o, 1)

        walk(pe, group, 1, 0)

    @block.vector
    def _(v):
        def group(x):
            if x.live():
                h = x.slot(0, 2)
                v.wait_ge(s_pexp, x.at() + 1)
                v.wait_ge(s_f, x.at() + 1)
                nc.vector.tensor_tensor(prob[h][:, :], ps_f[:, 0:GH], pe_slot[h][:, :], ALU.mult)\
                    .then_inc(s_prob, 1)
                v.wait_ge(s_prob, x.at() + 1)
                v.wait_ge(s_v, x.at() + 1)
                if x.live(-2):
                    v.wait_ge(s_o, x.at(-2) + 1)
                nc.vector.tensor_tensor(
                    msg[h][:, :].rearrange("p (a e) -> p a e", e=HD),
                    ps_v[h][:, :].rearrange("p (a e) -> p a e", e=HD),
                    prob[h][:, :].unsqueeze(2).to_broadcast([P, GH, HD]), ALU.mult).then_inc(s_msg, 1)
            if x.live(1):
                h = x.slot(1, 2)
                v.wait_ge(s_ps, x.at(1) + 1)
                if x.live(-1):
                    v.wait_ge(s_o, x.at(-1) + 1)
                nc.vector.tensor_tensor(same[h][:, :, :], ps_q[:, :].rearrange("p (j e) -> p j e", e=P),
                                        srcs[h][:, :].unsqueeze(2).to_broadcast([P, G, P]), ALU.is_equal)\
                    .then_inc(s_same, 1)
                v.wait_ge(s_same, x.at(1) + 1)
                nc.vector.tensor_tensor(dup[h][:, :, :], same[h][:, :, :],
                                        t["earlier"][:, :].unsqueeze(1).to_broadcast([P, G, P]), ALU.mult)\
                    .then_inc(s_dup, 1)
                nc.vector.tensor_scalar(away[h][:, :], srcs[h][:, :], -1.0, t["dump_row"][:, :], ALU.mult,
                                        ALU.add).then_inc(s_away, 1)
                v.wait_ge(s_dup, x.at(1) + 1)
                nc.vector.tensor_reduce(dups[h][:, :], dup[h][:, :, :], AX.X, ALU.add).then_inc(s_dups, 1)
                v.wait_ge(s_dups, x.at(1) + 1)
                v.wait_ge(s_away, x.at(1) + 1)
                nc.vector.scalar_tensor_tensor(away2[h][:, :], dups[h][:, :], 1.0, away[h][:, :], ALU.min,
                                               ALU.mult).then_inc(s_away2, 1)
                v.wait_ge(s_away2, x.at(1) + 1)
                if x.live(1 - SLOTS):
                    v.wait_ge(s_free, x.at(1) + 1)
                nc.vector.tensor_tensor(index[x.slot(1)][:, :], away2[h][:, :], srcs[h][:, :], ALU.add)\
                    .then_inc(s_index, 1)

        walk(v, group, 1, 0)


def finish(nc, m, t, d, wo, bo, g2, be2, wf1, bf1, wf2, bf2, out):
    NF = FF // P
    wo_sb = m.sb("wo_sb", [D, D])
    w1_sb = m.sb("w1_sb", [D, FF])
    w2_sb = m.sb("w2_sb", [P, NF, D])
    b1_sb = m.sb("b1_sb", [P, NF])
    bo_sb, b2_sb, gain, shift = (m.sb(n, [P, D]) for n in ("bo_sb", "b2_sb", "gain", "shift"))
    two_of = lambda n, shape: [m.sb(f"{n}{h}", shape) for h in range(2)]
    parts = two_of("parts", [P, REP, D])
    xl, o, ot, x1, n2, n2t, y, yo = (two_of(n, [P, D]) for n in ("xl", "o", "ot", "x1", "n2", "n2t", "y", "yo"))
    hid = two_of("hid", [P, NF, P])
    stats, moments = two_of("stats", [P, 6]), two_of("moments", [P, 2])
    ps_n = [m.ps(f"ps_node{h}", [P, 512]) for h in range(2)]
    ps_f = [m.ps(f"ps_hid{h}", [P, 512]) for h in range(2)]
    s_w, s_o, s_ot, s_otc, s_att, s_n2, s_nt, s_n2t, s_f, s_hid, s_y, s_out, s_step, s_st, s_free, s_copy = (
        m.sem(n) for n in ("f_weights", "f_sum", "f_sum_t", "f_sum_slot", "f_attention", "f_normed",
                           "f_normed_t", "f_slot", "f_hidden", "f_relu", "f_ffn", "f_out", "f_step",
                           "f_stored", "f_free", "f_copied"))
    s_in = [m.sem(f"f_in{h}") for h in range(2)]
    s_stood = m.sem("f_stood")
    s_var, s_std, s_eps = m.sem("f_variance"), m.sem("f_deviation"), m.sem("f_eps")
    eps = m.sb("eps", [P, 1])
    STEPS = 11
    NIN = 16 * (REP + 1)
    block = m.stack.enter_context(nc.Block())

    @block.sync
    def _(sp):
        n = 0
        for to, of in ((wo_sb[:, :], wo), (w1_sb[:, :], wf1), (w2_sb[:, :, :], wf2.rearrange("(c p) e -> p c e", p=P)),
                       (bo_sb[:, :], rows_of(bo)), (b2_sb[:, :], rows_of(bf2)),
                       (gain[:, :], rows_of(g2)), (shift[:, :], rows_of(be2))):
            sp.dma_start(to, of).then_inc(s_w, 16)
            n += 1
        with nc.allow_non_contiguous_dma(reason="a bias as columns"):
            sp.dma_start(b1_sb[:, :], bf1.rearrange("(c p) -> p c", p=P)).then_inc(s_w, 16)
        sp.wait_ge(s_w, 16 * (n + 1))

        def load(h, rows):
            sp.dma_start(xl[h][:, :], d["xl"][rows, :]).then_inc(s_in[h], 16)
            for r in range(REP):
                sp.dma_start(parts[h][:, r, :], d["sums"][r][rows, :]).then_inc(s_in[h], 16)

        load(0, slice(0, P))
        sp.sem_inc(s_free, 2)

        def tile(i, h, more):
            g = two(i, h)
            if more:
                load(1 - h, bass.ds((g + 1) * P, P))
            sp.wait_ge(s_out, g + 1)
            sp.dma_start(d["out"][bass.ds(g * P, P), :], yo[h][:, :]).then_inc(s_st, 16)
            sp.wait_ge(s_st, g * 16 + 16)
            sp.sem_inc(s_free, 1)

        with sp.Fori(0, NT // 2 - 1) as i:
            for h in range(2):
                tile(i, h, True)
        tile(NT // 2 - 1, 0, True)
        tile(NT // 2 - 1, 1, False)
        sp.dma_start(out, d["out"][0:N, :]).then_inc(s_copy, 16)
        sp.wait_ge(s_copy, 16)

    @block.tensor
    def _(pe):
        pe.wait_ge(s_w, 128)
        with pe.Fori(0, NT // 2) as i:
            for h in range(2):
                g = two(i, h)
                node = ps_n[h][:, 0:P]
                pe.wait_ge(s_free, g + 1)
                pe.wait_ge(s_o, g + 1)
                nc.tensor.transpose(node, o[h][:, :], t["ident"][:, :]).then_inc(s_ot, 1)
                pe.wait_ge(s_otc, g + 1)
                nc.tensor.matmul(node, ot[h][:, :], wo_sb[:, :], start=True, stop=True).then_inc(s_att, 1)
                pe.wait_ge(s_n2, g + 1)
                nc.tensor.transpose(node, n2[h][:, :], t["ident"][:, :]).then_inc(s_nt, 1)
                pe.wait_ge(s_n2t, g + 1)
                for c in range(NF):
                    last = nc.tensor.matmul(ps_f[h][:, c * P:(c + 1) * P], w1_sb[:, c * P:(c + 1) * P], n2t[h][:, :],
                                            start=True, stop=True)
                last.then_inc(s_f, 1)
                pe.wait_ge(s_hid, g * NF + NF)
                for c in range(NF):
                    last = nc.tensor.matmul(node, hid[h][:, c, :], w2_sb[:, c, :], start=(c == 0),
                                            stop=(c == NF - 1))
                last.then_inc(s_y, 1)

    @block.gpsimd
    def _(pool):
        pool.memset(eps[:, :], EPS).then_inc(s_eps, 1)

    @block.scalar
    def _(act):
        act.wait_ge(s_eps, 1)
        act.wait_ge(s_w, 128)
        with act.Fori(0, NT // 2) as i:
            for h in range(2):
                g = two(i, h)
                act.wait_ge(s_ot, g + 1)
                nc.scalar.activation(ot[h][:, :], ps_n[h][:, 0:P], ACT.Copy).then_inc(s_otc, 1)
                deviation(nc, act, moments[h], eps[:, :], s_var, s_std, g * 2 + 1)
                act.wait_ge(s_nt, g + 1)
                nc.scalar.activation(n2t[h][:, :], ps_n[h][:, 0:P], ACT.Copy).then_inc(s_n2t, 1)
                act.wait_ge(s_f, g + 1)
                for c in range(NF):
                    nc.scalar.activation(hid[h][:, c, :], ps_f[h][:, c * P:(c + 1) * P], ACT.Relu,
                                         bias=b1_sb[:, c:c + 1]).then_inc(s_hid, 1)
                deviation(nc, act, moments[h], eps[:, :], s_var, s_std, g * 2 + 2)

    @block.vector
    def _(v):
        v.wait_ge(s_w, 128)
        with v.Fori(0, NT // 2) as i:
            for h in range(2):
                g = two(i, h)
                step = Steps(v, s_step, g * STEPS, s_stood)
                v.wait_ge(s_in[h], i * NIN + NIN)
                v.wait_ge(s_free, g + 1)
                nc.vector.tensor_reduce(o[h][:, :], parts[h][:, :, :].rearrange("p r e -> p e r"), AX.X,
                                        ALU.add).then_inc(s_o, 1)
                v.wait_ge(s_att, g + 1)
                step(nc.vector.tensor_tensor(x1[h][:, :], ps_n[h][:, 0:D], bo_sb[:, :], ALU.add))
                step(nc.vector.tensor_tensor(x1[h][:, :], x1[h][:, :], xl[h][:, :], ALU.add))
                step(normalize(nc, v, step, n2[h][:, :], x1[h][:, :], stats[h][:, :], moments[h][:, :],
                               s_var, s_std, g * 2 + 1))
                step(nc.vector.tensor_tensor(n2[h][:, :], n2[h][:, :], gain[:, :], ALU.mult))
                nc.vector.tensor_tensor(n2[h][:, :], n2[h][:, :], shift[:, :], ALU.add).then_inc(s_n2, 1)
                v.wait_ge(s_y, g + 1)
                step(nc.vector.tensor_tensor(y[h][:, :], ps_n[h][:, 0:D], b2_sb[:, :], ALU.add))
                step(nc.vector.tensor_tensor(y[h][:, :], y[h][:, :], x1[h][:, :], ALU.add))
                step(nc.vector.tensor_tensor(y[h][:, :], y[h][:, :], xl[h][:, :], ALU.add))
                normalize(nc, v, step, yo[h][:, :], y[h][:, :], stats[h][:, :], moments[h][:, :],
                          s_var, s_std, g * 2 + 2).then_inc(s_out, 1)
                assert step.n == STEPS


def build(nc, x, src, dst, curv, rel, w1, sl1, b1, w2, sl2, b2, wq, bq, wk, bk, wv, bv, wo, bo, wc, bc,
          wf1, bf1, wf2, bf2, g1, be1, g2, be2, out):
    with ExitStack() as top:
        keep = Memory(nc, top, "")
        t = {
            "ident": keep.sb("ident", [P, P]), "iota": keep.sb("iota", [P, P]),
            "earlier": keep.sb("earlier", [P, P]), "lane": keep.sb("lane", [P, 1]),
            "dump_row": keep.sb("dump_row", [P, 1]),
            "iota16": keep.sb("iota16", [P, P], BF16),
            "source": keep.sb("source", [P, K], I16), "source_or_dump": keep.sb("source_or_dump", [P, K], I16),
            "target": keep.sb("target", [P, K], BF16), "reset": keep.sb("reset", [P, K], BF16),
            "run_end": keep.sb("run_end", [P, K], BF16),
            "window": keep.sb("window", [1, K], I32), "first_edge": keep.sb("first_edge", [1, K], I32),
            "nodes_a": keep.sb("nodes_a", [P, NP]), "big": keep.sb("big", [P, 2 * K * H]),
            "landed": [keep.sem(f"landed{q}") for q in range(SLOTS)],
            "landed_at": [0] * SLOTS,
        }
        t["run_max"] = t["big"][:, 0:K * H]
        t["run_sum"] = t["big"][:, K * H:2 * K * H]
        t["nodes_b"] = t["big"][:, K * H:K * H + NP]
        t["row"] = t["big"][:, 2 * K * H - K:2 * K * H].bitcast(I32)
        d = {
            "xpad": nc.dram_tensor("xpad", (NP + P, D), FP32).ap(),
            "tiles": nc.dram_tensor("tiles", (2, K), I32).ap(),
            "xt": nc.dram_tensor("xt", (NP, R * D), FP32).ap(),
            "q": nc.dram_tensor("q", (NP, D), FP32).ap(),
            "v": nc.dram_tensor("v", (NP, D), FP32).ap(),
            "exp": nc.dram_tensor("exp", (K * H, P), FP32).ap(),
            "xl": nc.dram_tensor("xl", (NP, D), FP32).ap(),
            "out": nc.dram_tensor("out_rows", (NP, D), FP32).ap(),
            "sums": [nc.dram_tensor(f"sums{r}", (NP, D), FP32).ap() for r in range(REP)],
        }

        done = []

        def stage(f, *args):
            done.append(f)
            with ExitStack() as kept:
                with ExitStack() as s:
                    m = Memory(nc, s, f"stage{len(done)}_")
                    m.sem_stack = kept
                    f(nc, m, t, *args)
                for sem in m.sems:
                    nc.gpsimd.sem_clear(sem)
                nc.all_engine_barrier()

        stage(prepare_edges, src, dst, rel, x, d)
        stage(relation_table, d, w1, sl1, b1, True)
        stage(aggregate, d, True)
        stage(relation_table, d, w2, sl1, b1, False)
        stage(aggregate, d, False)
        stage(project, d, sl2, b2, wq, wk, wv, bq, bk, bv, g1, be1)
        stage(score, d, curv, wc, bc)
        stage(combine)
        stage(scatter, d)
        stage(finish, d, wo, bo, g2, be2, wf1, bf1, wf2, bf2, out)


_INS = ["x", "src", "dst", "edge_attr_128", "edge_type_8",
        "L0_gnn_w1", "L0_gnn_sl1", "L0_gnn_b1", "L0_gnn_w2", "L0_gnn_sl2", "L0_gnn_b2",
        "L1_gnn_Wq", "L1_gnn_bq", "L1_gnn_Wk", "L1_gnn_bk", "L1_gnn_Wv", "L1_gnn_bv",
        "L1_gnn_Wo", "L1_gnn_bo", "L1_gnn_Wc", "L1_gnn_bc", "L1_gnn_W1", "L1_gnn_b1",
        "L1_gnn_W2", "L1_gnn_b2", "L1_gnn_g1", "L1_gnn_be1", "L1_gnn_g2", "L1_gnn_be2"]


def kernel(**inputs):
    import numpy as _np
    import concourse.bacc as _bacc
    from concourse import mybir as _mybir
    from concourse.bass_utils import run_bass_kernel_spmd as _run

    nc = _bacc.Bacc("TRN2", target_bir_lowering=False, num_devices=1)
    arrays, args = {}, []
    for name in _INS:
        a = _np.ascontiguousarray(inputs[name])
        arrays[f"in_{name}_dram"] = a
        args.append(nc.dram_tensor(f"in_{name}_dram", a.shape, _mybir.dt.from_np(a.dtype), kind="ExternalInput").ap())
    args.append(nc.dram_tensor("out_0_dram", (N, D), _mybir.dt.float32, kind="ExternalOutput").ap())
    build(nc, *args)
    r = _run(nc, [arrays], core_ids=[0])
    return r.results[0]["out_0_dram"]
```

```python
import concourse.bass as bass
from concourse import mybir
from contextlib import ExitStack

FP32 = mybir.dt.float32
I32 = mybir.dt.int32
I16 = mybir.dt.int16
BF16 = mybir.dt.bfloat16
ALU = mybir.AluOpType
ACT = mybir.ActivationFunctionType
AX = mybir.AxisListType

P = 128
N = 6250
E = 206250
D = 128
R = 8
H = 8
HD = D // H
FF = 4 * D
W = -(-N // P)
BT = 4
BATCHES = -(-W // BT)
NT = BATCHES * BT
NP = NT * P
KC = -(-(E // P + W) // P)
K = KC * P
G = 4
SLOTS = 4
TURNS = K // (SLOTS * G)
GROUPS = K // G
EP = 125
BIG = 1.0e30
REP = 2 * G
EPS = 1e-5
MARKS = 2 * (P + 1) + 3 * P


class Memory:

    def __init__(self, nc, stack, stage):
        self.nc, self.stack, self.stage = nc, stack, stage
        self.sem_stack, self.sems = stack, []

    def sb(self, name, shape, dt=FP32):
        return self.stack.enter_context(self.nc.sbuf_tensor(self.stage + name, shape, dt))

    def ps(self, name, shape, dt=FP32):
        return self.stack.enter_context(self.nc.psum_tensor(self.stage + name, shape, dt))

    def sem(self, name):
        self.sems.append(self.sem_stack.enter_context(self.nc.semaphore(self.stage + name)))
        return self.sems[-1]


def ring_index(pool, sem, value, passed):
    pool.wait_ge(sem, value)
    pool.sem_inc(passed, 1)


def prepare_edges(nc, m, t, src, dst, rel, x, d):
    dst_i = m.sb("dst_i", [EP, E // EP], I32)
    dst_f = m.sb("dst_f", [EP, E // EP])
    below = m.sb("below", [EP, E // EP])
    limit = m.sb("limit", [P, W + 1])
    count = m.sb("count", [EP, W + 1])
    ones = m.sb("ones_col", [P, 1])
    before = m.sb("before", [P, P])
    last_w = m.sb("last_w", [W, 1])
    wend = m.sb("wend", [W, 2])
    wn = m.sb("wn", [W, 1])
    wni = m.sb("wni", [W, 1], I32)
    wtile = m.sb("wtile", [W, 2])
    wval = m.sb("wval", [W, 3])
    tile_no, hot, started = (t["nodes_a"][0:W, a * K:(a + 1) * K] for a in range(3))
    tval = m.sb("tval", [P, KC, 3])
    tno = m.sb("tno", [P, KC])
    raw = m.sb("raw", [P, KC])
    start = m.sb("start", [P, KC])
    start_i = m.sb("start_i", [P, KC], I32)
    win_i = m.sb("win_i", [P, KC], I32)
    lead = m.sb("lead", [P, KC])
    until = m.sb("until", [P, KC])
    rows_i = [t["big"][:, a * K:(a + 1) * K].bitcast(I32) for a in range(3)]
    rows_f = [t["big"][:, a * K:(a + 1) * K].rearrange("p (c e) -> p c e", e=P) for a in range(3, 8)]
    key, first, last, off = (t["big"][:, a * K:(a + 1) * K].rearrange("p (c e) -> p c e", e=P)
                             for a in range(8, 12))
    ends = m.sb("ends", [P, KC, 2])
    marks = m.sb("marks", [P, KC, MARKS], BF16)
    target16 = m.sb("target16", [P, KC, P], BF16)
    valid = t["nodes_a"][:, 0:K].rearrange("p (c e) -> p c e", e=P)
    dump = m.sb("dump", [P, P])
    zero_rows = m.sb("zero_rows", [P, D])
    cnt_ps = m.ps("cnt_ps", [P, 512])
    tr_ps = [m.ps(f"tr_ps{b}", [P, 512]) for b in range(2)]
    s_dst, s_pool, s_v, s_pe, s_tab, s_tab2, s_tr, s_cp, s_pad = (
        m.sem(n) for n in ("p_dst", "p_const", "p_vector", "p_tensor", "p_table",
                           "p_table_back", "p_transposed", "p_copied", "p_pad"))
    s_rows = t["landed"][0]
    add_landed(t, [3 * KC * 16, 0, 0, 0])
    s_cnt = m.sem("p_count")
    s_tile = m.sem("p_tile_rows")
    s_link = m.sem("p_link")
    CH = [(c0, min(G, KC - c0)) for c0 in range(0, KC, G)]
    CONV, COUNTED, WEND, WN, WVAL, TVAL, START, SIX = range(1, 9)

    block = m.stack.enter_context(nc.Block())

    @block.sync
    def _(sp):
        sp.dma_start(dst_i[:, :], dst.rearrange("(p n) -> p n", p=EP)).then_inc(s_dst, 16)
        sp.dma_start(d["xpad"][0:N, :], x).then_inc(s_pad, 16)
        sp.wait_ge(s_pool, 2)
        for n0 in range(N, NP, P):
            n1 = min(n0 + P, NP)
            sp.dma_start(d["xpad"][n0:n1, :], zero_rows[0:n1 - n0, :]).then_inc(s_pad, 16)
        sp.wait_ge(s_v, START)
        with nc.allow_non_contiguous_dma(reason="a few thousand words, once"):
            sp.dma_start(d["tiles"][0].rearrange("(c p) -> p c", p=P), start_i[:, :]).then_inc(s_tab, 16)
            sp.dma_start(d["tiles"][1].rearrange("(c p) -> p c", p=P), win_i[:, :]).then_inc(s_tab, 16)
        sp.wait_ge(s_tab, 32)
        sp.dma_start(t["first_edge"][:, :], d["tiles"][0:1, :]).then_inc(s_tab2, 16)
        sp.dma_start(t["window"][:, :], d["tiles"][1:2, :]).then_inc(s_tab2, 16)
        sp.wait_ge(s_tab2, 32)
        sp.wait_ge(s_pad, 16 * (1 + len(range(N, NP, P))))
        sp.wait_ge(s_v, SIX)
        sp.dma_start(d["targets"].rearrange("(c p e) -> p c e", p=P, e=P), target16[:, :, :]).then_inc(s_tile, 16)
        sp.dma_start(d["tile_marks"].rearrange("(c p) e -> p c e", p=P), marks[:, :, :]).then_inc(s_tile, 16)
        with nc.allow_non_contiguous_dma(reason="a few thousand words, once"):
            sp.dma_start(d["keys"].rearrange("(c p e) -> p c e", p=P, e=2), ends[:, :, :]).then_inc(s_tile, 16)
        sp.wait_ge(s_tile, 48)

    @block.gpsimd
    def _(pool):
        pool.memset(zero_rows[:, :], 0.0).then_inc(s_pool, 1)
        pool.memset(ones[:, :], 1.0).then_inc(s_pool, 1)
        pool.memset(t["ident"][:, :], 0.0).then_inc(s_pool, 1)
        pool.memset(before[:, :], 1.0).then_inc(s_pool, 1)
        pool.memset(t["earlier"][:, :], 1.0).then_inc(s_pool, 1)
        pool.memset(last_w[:, :], 0.0).then_inc(s_pool, 1)
        pool.wait_ge(s_pool, 6)
        pool.affine_select(out=t["ident"][:, :], in_=t["ident"][:, :], compare_op=ALU.not_equal, fill=1.0,
                           base=0, pattern=[[-1, P]], channel_multiplier=1).then_inc(s_pool, 1)
        pool.affine_select(out=before[:, :], in_=before[:, :], compare_op=ALU.is_gt, fill=0.0,
                           base=0, pattern=[[1, P]], channel_multiplier=-1).then_inc(s_pool, 1)
        pool.affine_select(out=t["earlier"][:, :], in_=t["earlier"][:, :], compare_op=ALU.is_gt, fill=0.0,
                           base=0, pattern=[[-1, P]], channel_multiplier=1).then_inc(s_pool, 1)
        pool.affine_select(out=last_w[:, :], in_=last_w[:, :], compare_op=ALU.not_equal, fill=float(K * P),
                           base=-(W - 1), pattern=[[0, 1]], channel_multiplier=1).then_inc(s_pool, 1)
        f = dict(allow_small_or_imprecise_dtypes=True)
        pool.iota(limit[:, :], pattern=[[P, W + 1]], base=0, channel_multiplier=0, **f).then_inc(s_pool, 1)
        pool.iota(tile_no[:, :], pattern=[[1, K]], base=0, channel_multiplier=0, **f).then_inc(s_pool, 1)
        pool.iota(tno[:, :], pattern=[[P * P, KC]], base=0, channel_multiplier=P, **f).then_inc(s_pool, 1)
        pool.iota(t["iota"][:, :], pattern=[[1, P]], base=0, channel_multiplier=0, **f).then_inc(s_pool, 1)
        pool.iota(t["iota16"][:, :], pattern=[[1, P]], base=0, channel_multiplier=0, **f).then_inc(s_pool, 1)
        pool.iota(t["lane"][:, :], pattern=[[0, 1]], base=0, channel_multiplier=1, **f).then_inc(s_pool, 1)
        pool.iota(dump[:, :], pattern=[[1, P]], base=N, channel_multiplier=0, **f).then_inc(s_pool, 1)
        pool.iota(t["dump_row"][:, :], pattern=[[0, 1]], base=N, channel_multiplier=1, **f).then_inc(s_pool, 1)
        pool.iota(wval[:, 2:3], pattern=[[0, 1]], base=0, channel_multiplier=1, **f).then_inc(s_pool, 1)
        pool.wait_ge(s_v, START)
        for a, v in enumerate((src, dst, rel)):
            for c in range(KC):
                pool.indirect_dma_start(
                    rows_i[a][:, c * P:(c + 1) * P], None, v.rearrange("(e a) -> e a", a=1),
                    bass.IndirectOffsetOnAxis(ap=start_i[:, c:c + 1], axis=0)).then_inc(s_rows, 16)

    POOL_DONE = 19

    @block.tensor
    def _(pe):
        pe.wait_ge(s_v, COUNTED)
        pe.wait_ge(s_pool, POOL_DONE)
        for j in range(2):
            nc.tensor.matmul(cnt_ps[0:W, j:j + 1], count[:, j:j + W], ones[0:EP, :],
                             start=True, stop=True).then_inc(s_pe, 1)
        pe.wait_ge(s_v, WN)
        nc.tensor.matmul(cnt_ps[0:W, 2:3], before[0:W, 0:W], wn[:, :], start=True, stop=True).then_inc(s_pe, 1)
        pe.wait_ge(s_v, WVAL)
        for c in range(KC):
            last = nc.tensor.matmul(cnt_ps[:, 16 + 3 * c:19 + 3 * c], hot[:, c * P:(c + 1) * P], wval[:, :],
                                    start=True, stop=True)
        last.then_inc(s_pe, 1)
        pe.wait_ge(s_v, SIX)
        n = 0
        for a in range(5):
            for c0, cn in CH:
                if n >= 2:
                    pe.wait_ge(s_cp, n - 1)
                for j in range(cn):
                    last = nc.tensor.transpose(tr_ps[n % 2][:, j * P:(j + 1) * P], rows_f[a][:, c0 + j, :],
                                               t["ident"][:, :])
                last.then_inc(s_tr, 1)
                n += 1

    @block.scalar
    def _(act):
        n = 0
        for a, name in enumerate(("row", "source", "source_or_dump", "target", "penalty")):
            for c0, cn in CH:
                act.wait_ge(s_tr, n + 1)
                nc.scalar.activation(t[name][:, c0 * P:(c0 + cn) * P], tr_ps[n % 2][:, 0:cn * P],
                                     ACT.Copy).then_inc(s_cp, 1)
                n += 1

    @block.vector
    def _(v):
        v.wait_ge(s_dst, 16)
        nc.vector.tensor_copy(dst_f[:, :], dst_i[:, :]).then_inc(s_v, 1)
        v.wait_ge(s_v, CONV)
        v.wait_ge(s_pool, POOL_DONE)
        with v.Fori(0, W + 1) as w:
            nc.vector.tensor_scalar(below[:, :], dst_f[:, :], limit[0:EP, bass.ds(w, 1)], 0.0, ALU.is_lt,
                                    ALU.add, accum_out=count[:, bass.ds(w, 1)]).then_inc(s_cnt, 1)
            v.wait_ge(s_cnt, w + 1)
        nc.vector.memset(below[:, 0:1], 0.0).then_inc(s_v, 1)
        v.wait_ge(s_pe, 2)
        nc.vector.tensor_copy(wend[:, :], cnt_ps[0:W, 0:2]).then_inc(s_v, 1)
        v.wait_ge(s_v, WEND)
        n = [0]

        def link(ins):
            n[0] += 1
            ins.then_inc(s_link, 1)
            v.wait_ge(s_link, n[0])

        link(nc.vector.scalar_tensor_tensor(wn[:, :], wend[:, 1:2], float(P - 1), wend[:, 0:1],
                                            ALU.add, ALU.subtract))
        link(nc.vector.tensor_copy(wni[:, :], wn[:, :]))
        link(nc.vector.tensor_scalar(wni[:, :], wni[:, :], 7, None, ALU.arith_shift_right))
        nc.vector.tensor_copy(wn[:, :], wni[:, :]).then_inc(s_v, 1)
        v.wait_ge(s_pe, 3)
        link(nc.vector.tensor_copy(wtile[:, 0:1], cnt_ps[0:W, 2:3]))
        link(nc.vector.tensor_tensor(wtile[:, 1:2], wtile[:, 0:1], wn[:, :], ALU.add))
        link(nc.vector.tensor_tensor(wtile[:, 1:2], wtile[:, 1:2], last_w[:, :], ALU.add))
        link(nc.vector.scalar_tensor_tensor(wval[:, 0:1], wtile[:, 0:1], -float(P), wend[:, 0:1],
                                            ALU.mult, ALU.add))
        link(nc.vector.tensor_copy(wval[:, 1:2], wend[:, 1:2]))
        link(nc.vector.tensor_scalar(started[:, :], tile_no[0:W, :], wtile[:, 0:1], None, ALU.is_ge))
        nc.vector.scalar_tensor_tensor(hot[:, :], tile_no[0:W, :], wtile[:, 1:2], started[:, :],
                                       ALU.is_lt, ALU.mult).then_inc(s_v, 1)
        v.wait_ge(s_pe, 4)
        nc.vector.tensor_copy(tval[:, :, :], cnt_ps[:, 16:16 + 3 * KC].rearrange("p (c v) -> p c v", v=3))\
            .then_inc(s_v, 1)
        v.wait_ge(s_v, TVAL)
        link(nc.vector.tensor_tensor(raw[:, :], tval[:, :, 0], tno[:, :], ALU.add))
        link(nc.vector.tensor_scalar(start[:, :], raw[:, :], float(E - P), None, ALU.min))
        link(nc.vector.tensor_tensor(lead[:, :], raw[:, :], start[:, :], ALU.subtract))
        link(nc.vector.tensor_tensor(until[:, :], tval[:, :, 1], start[:, :], ALU.subtract))
        link(nc.vector.tensor_copy(win_i[:, :], tval[:, :, 2]))
        nc.vector.tensor_copy(start_i[:, :], start[:, :]).then_inc(s_v, 1)

        def over_tiles(a):
            return a.unsqueeze(1).to_broadcast([P, KC, P])

        def over_edges(a):
            return a.unsqueeze(2).to_broadcast([P, KC, P])

        pos = over_tiles(t["iota"][:, :])
        link(nc.vector.tensor_tensor(rows_f[0][:, :, :], pos, over_edges(lead[:, :]), ALU.is_ge))
        link(nc.vector.tensor_tensor(valid[:, :, :], pos, over_edges(until[:, :]), ALU.is_lt))
        link(nc.vector.tensor_tensor(valid[:, :, :], valid[:, :, :], rows_f[0][:, :, :], ALU.mult))
        v.wait_ge(s_rows, 3 * KC * 16)
        srow, drow, trow = (r[:, :].rearrange("p (c e) -> p c e", e=P) for r in rows_i)
        row, source, sod, target, penalty = rows_f
        link(nc.vector.tensor_copy(source[:, :, :], srow))
        link(nc.vector.tensor_copy(target[:, :, :], drow))
        link(nc.vector.tensor_copy(row[:, :, :], trow))
        link(nc.vector.scalar_tensor_tensor(row[:, :, :], source[:, :, :], float(R), row[:, :, :],
                                            ALU.mult, ALU.add))
        link(nc.vector.tensor_scalar(lead[:, :], tval[:, :, 2], float(P), None, ALU.mult))
        link(nc.vector.tensor_tensor(target[:, :, :], target[:, :, :], over_edges(lead[:, :]), ALU.subtract))
        link(nc.vector.scalar_tensor_tensor(target[:, :, :], target[:, :, :], 1.0, valid[:, :, :],
                                            ALU.add, ALU.mult))
        link(nc.vector.tensor_scalar(target[:, :, :], target[:, :, :], -1.0, None, ALU.add))
        link(nc.vector.tensor_tensor(sod[:, :, :], source[:, :, :], over_tiles(dump[:, :]), ALU.subtract))
        link(nc.vector.tensor_tensor(sod[:, :, :], sod[:, :, :], valid[:, :, :], ALU.mult))
        link(nc.vector.tensor_tensor(sod[:, :, :], sod[:, :, :], over_tiles(dump[:, :]), ALU.add))
        link(nc.vector.tensor_scalar(penalty[:, :, :], valid[:, :, :], BIG, -BIG, ALU.mult, ALU.add))
        link(nc.vector.tensor_copy(target16[:, :, :], target[:, :, :]))
        link(nc.vector.tensor_scalar(off[:, :, :], valid[:, :, :], -2.0 * NP, 2.0 * NP, ALU.mult, ALU.add))
        link(nc.vector.tensor_copy(key[:, :, :], drow))
        link(nc.vector.tensor_tensor(first[:, :, :], key[:, :, :], off[:, :, :], ALU.add))
        link(nc.vector.tensor_reduce(ends[:, :, 0], first[:, :, :], AX.X, ALU.min))
        link(nc.vector.scalar_tensor_tensor(last[:, :, :], key[:, :, :], 1.0, valid[:, :, :], ALU.add, ALU.mult))
        link(nc.vector.tensor_scalar(last[:, :, :], last[:, :, :], -1.0, None, ALU.add))
        link(nc.vector.tensor_reduce(ends[:, :, 1], last[:, :, :], AX.X, ALU.max))
        link(nc.vector.tensor_tensor(key[:, :, :], key[:, :, :], over_edges(ends[:, :, 0]), ALU.max))
        link(nc.vector.tensor_tensor(key[:, :, :], key[:, :, :], over_edges(ends[:, :, 1]), ALU.min))
        link(nc.vector.tensor_copy(ends[:, :, :], key[:, :, 0:P:P - 1]))
        link(nc.vector.tensor_tensor(first[:, :, :], key[:, :, :], over_edges(ends[:, :, 0]), ALU.is_equal))
        link(nc.vector.tensor_tensor(last[:, :, :], key[:, :, :], over_edges(ends[:, :, 1]), ALU.is_equal))
        link(nc.vector.tensor_tensor(last[:, :, :], last[:, :, :], first[:, :, :], ALU.is_gt))
        starts, goes_on = marks[:, :, 0:P + 1], marks[:, :, P + 1:2 * P + 2]
        own = marks[:, :, 2 * P + 2:MARKS].rearrange("p c (a e) -> p c a e", e=P)
        link(nc.vector.tensor_copy(own[:, :, 0, :], first[:, :, :]))
        link(nc.vector.tensor_copy(own[:, :, 1, :], last[:, :, :]))
        link(nc.vector.tensor_tensor(own[:, :, 2, :], first[:, :, :], last[:, :, :], ALU.is_equal))
        link(nc.vector.memset(goes_on, 0.0))
        link(nc.vector.tensor_tensor(goes_on[:, :, 1:P], key[:, :, 1:P], key[:, :, 0:P - 1], ALU.is_equal))
        nc.vector.tensor_scalar(starts, goes_on, BIG, -BIG, ALU.mult, ALU.add).then_inc(s_v, 1)


def batch_rows(table, x, k=0):
    return table[bass.ds(x.at(k) * (BT * P), BT * P), :].rearrange("(a p) e -> p a e", p=P)


def relation_table(nc, m, t, d, w_all, self_w, bias, first):
    wrel = m.sb("wrel", [D, R * D])
    wself = m.sb("wself", [D, D])
    bcol = m.sb("bcol", [D, 1])
    xin = [m.sb(f"xin{h}", [P, BT, D]) for h in range(2)] if first else None
    xts = [m.sb(f"xts{h}", [D, BT * P]) for h in range(2)]
    summed = m.sb("summed", [D, BT * P])
    xo = [t["big"][:, h * BT * R * D:(h + 1) * BT * R * D].rearrange("p (a e) -> p a e", a=BT) for h in range(2)]
    ps_t = m.ps("ps_t", [P, BT * P])
    ps_x = [[m.ps(f"ps_x{half}{b}", [P, 512]) for b in range(2)] for half in range(2)]
    HALF = R * D // 2
    s_w, s_t, s_sum, s_xts, s_keep, s_zero = (
        m.sem(n) for n in ("r_weights", "r_transposed", "r_summed", "r_slot", "r_kept", "r_zeroed"))
    s_in, s_x, s_out, s_st = ([m.sem(f"{n}{h}") for h in range(2)] for n in (
        "r_in", "r_product", "r_out", "r_stored"))
    block = m.stack.enter_context(nc.Block())

    @block.sync
    def _(sp):
        sp.dma_start(wrel[:, :].rearrange("d (r e) -> d r e", r=R), w_all.rearrange("r d e -> d r e"))\
            .then_inc(s_w, 16)
        sp.dma_start(wself[:, :], self_w).then_inc(s_w, 16)
        with nc.allow_non_contiguous_dma(reason="a bias as a column"):
            sp.dma_start(bcol[:, :], bias.rearrange("(d a) -> d a", a=1)).then_inc(s_w, 16)

        def batch(x):
            if first and x.live(2):
                if x.live():
                    sp.wait_ge(s_t, x.at() + 1)
                sp.dma_start(xin[x.slot(2, 2)][:, :, :], batch_rows(d["xpad"], x, 2)).then_inc(s_in[x.slot(2, 2)], 16)
            if x.live():
                for half in range(2):
                    sp.wait_ge(s_out[half], x.at() * BT + BT)
                sp.dma_start(batch_rows(d["xt"], x), xo[x.slot(0, 2)]).then_inc(s_st[x.slot(0, 2)], 16)

        walk(sp, batch, 2, 0, 2, BATCHES)
        for h in range(2):
            sp.wait_ge(s_st[h], (BATCHES + 1 - h) // 2 * 16)
        sp.wait_ge(s_w, 48)

    @block.tensor
    def _(pe):
        pe.wait_ge(s_w, 48)

        def batch(x):
            if x.live(1):
                h = x.slot(1, 2)
                if x.live():
                    pe.wait_ge(s_xts if first else s_sum, x.at() + 1)
                if first:
                    pe.wait_ge(s_in[h], x.turn(1) * 16 + 16)
                    for j in range(BT):
                        last = nc.tensor.transpose(ps_t[:, j * P:(j + 1) * P], xin[h][:, j, :], t["ident"][:, :])
                else:
                    last = nc.tensor.matmul(ps_t[:, :], wself[:, :], batch_of(t["nodes_a"], x, 1),
                                            start=True, stop=True)
                last.then_inc(s_t, 1)
            if x.live():
                pe.wait_ge(s_xts, x.at() + 1)
                for j in range(BT):
                    for half in range(2):
                        if x.live(-1) or j >= 2:
                            pe.wait_ge(s_out[half], x.at() * BT + j - 1)
                        nc.tensor.matmul(ps_x[half][j % 2][:, :], xts[x.slot(0, 2)][:, j * P:(j + 1) * P],
                                         wrel[:, half * HALF:(half + 1) * HALF], start=True, stop=True)\
                            .then_inc(s_x[half], 1)

        walk(pe, batch, 1, 0, 2, BATCHES)

    def evacuate(engine, copy, x, half):
        h = x.slot(0, 2)
        if x.live(-2):
            engine.wait_ge(s_st[h], x.turn(-2) * 16 + 16)
        for j in range(BT):
            engine.wait_ge(s_x[half], x.at() * BT + j + 1)
            copy(xo[h][:, j, half * HALF:(half + 1) * HALF], ps_x[half][j % 2][:, :]).then_inc(s_out[half], 1)

    @block.scalar
    def _(act):
        act.wait_ge(s_w, 48)

        def batch(x):
            if x.live(1):
                h = x.slot(1, 2)
                if x.live(-1):
                    for half in range(2):
                        act.wait_ge(s_x[half], x.at(-1) * BT + BT)
                    act.wait_ge(s_keep, x.at(-1) + 1)
                if first:
                    act.wait_ge(s_t, x.at(1) + 1)
                    nc.scalar.activation(xts[h][:, :], ps_t[:, :], ACT.Copy).then_inc(s_xts, 1)
                else:
                    act.wait_ge(s_sum, x.at(1) + 1)
                    nc.scalar.activation(xts[h][:, :], summed[:, :], ACT.Relu, bias=bcol[:, :]).then_inc(s_xts, 1)
            if x.live():
                evacuate(act, lambda out, in_: nc.scalar.activation(out, in_, ACT.Copy), x, 0)

        walk(act, batch, 1, 0, 2, BATCHES)

    @block.vector
    def _(v):
        def batch(x):
            if x.live(1) and not first:
                v.wait_ge(s_t, x.at(1) + 1)
                if x.live():
                    v.wait_ge(s_xts, x.at() + 1)
                nc.vector.tensor_tensor(summed[:, :], ps_t[:, :], batch_of(t["nodes_b"], x, 1), ALU.add)\
                    .then_inc(s_sum, 1)
            if x.live():
                evacuate(v, nc.vector.tensor_copy, x, 1)
            if x.live(1):
                v.wait_ge(s_xts, x.at(1) + 1)
                nc.vector.tensor_copy(batch_of(t["nodes_a"], x, 1), xts[x.slot(1, 2)][:, :]).then_inc(s_keep, 1)

        walk(v, batch, 1, 0, 2, BATCHES)
        v.wait_ge(s_keep, BATCHES)
        if not first:
            v.wait_ge(s_sum, BATCHES)
        nc.vector.memset(t["nodes_b"], 0.0).then_inc(s_zero, 1)
        v.wait_ge(s_zero, 1)


def batch_of(nodes, x, k=0):
    return nodes[:, bass.ds(x.at(k) * (BT * P), BT * P)]


class Group:

    def __init__(self, i, q, slots, groups):
        self.i, self.q, self.slots, self.groups = i, q, slots, groups

    def at(self, k=0):
        return self.i * self.slots + (self.q + k)

    def turn(self, k=0):
        return self.i + (self.q + k) // self.slots

    def slot(self, k=0, n=SLOTS):
        return (self.q + k) % n

    def half(self, k=0):
        return self.i * (self.slots // 2) + (self.q + k) // 2

    def live(self, k=0):
        return not isinstance(self.i, int) or 0 <= self.at(k) < self.groups


def walk(engine, body, before, after, slots=SLOTS, groups=GROUPS, peeled=1):
    end = (groups - before) // slots
    for g in range(-before, peeled * slots):
        body(Group(g // slots, g % slots, slots, groups))
    with engine.Fori(peeled, end) as i:
        for q in range(slots):
            body(Group(i, q, slots, groups))
    for g in range(end * slots, groups + after):
        body(Group(g // slots, g % slots, slots, groups))


def aggregate(nc, m, t, d, zero_sums):
    index = [m.sb(f"index{q}", [P, G], I32) for q in range(SLOTS)]
    msg = [m.sb(f"msg{q}", [P, G, D]) for q in range(SLOTS)]
    hot = [m.sb(f"hot{q}", [P, G, P]) for q in range(2)]
    zero = m.sb("zero", [P, BT * D]) if zero_sums else None
    ps = [m.ps(f"ps_agg{q}", [D, G, P]) for q in range(2)]
    s_index, s_hot, s_freed, s_acc, s_read, passed, s_z, s_zd = (
        m.sem(n) for n in ("a_index", "a_hot", "a_msg_free", "a_added", "a_ps_read",
                           "a_passed", "a_zero", "a_zeroed"))
    s_msg = t["landed"]
    at = add_landed(t, [TURNS * G * 16] * SLOTS)
    block = m.stack.enter_context(nc.Block())
    xt = d["xt"].rearrange("n (r e) -> (n r) e", r=R)

    if zero_sums:
        @block.sync
        def _(sp):
            sp.wait_ge(s_z, 1)
            n = 0
            for r in range(REP):
                for a in range(BATCHES):
                    sp.dma_start(d["sums"][r][a * BT * P:(a + 1) * BT * P, :].rearrange("(p j) e -> p (j e)", p=P),
                                 zero[:, :]).then_inc(s_zd, 16)
                    n += 1
            for h in range(H):
                sp.dma_start(d["marks"].rearrange("(k h) e -> k h e", h=H)[:, h, :], d["tile_marks"])\
                    .then_inc(s_zd, 16)
            sp.wait_ge(s_zd, 16 * (n + H))

    @block.scalar
    def _(act):
        with act.Fori(0, TURNS) as i:
            for q in range(SLOTS):
                g = i * SLOTS + q
                act.wait_ge(s_freed, g + 1)
                nc.scalar.activation(index[q][:, :], t["row"][:, bass.ds(g * G, G)], ACT.Copy)\
                    .then_inc(s_index, 1)

    @block.gpsimd
    def _(pool):
        with pool.Fori(0, TURNS) as i:
            for q in range(SLOTS):
                g = i * SLOTS + q
                ring_index(pool, s_index, g + 1, passed)
                for j in range(G):
                    pool.indirect_dma_start(msg[q][:, j, :], None, xt,
                                            bass.IndirectOffsetOnAxis(ap=index[q][:, j:j + 1], axis=0))\
                        .then_inc(s_msg[q], 16)

    @block.tensor
    def _(pe):
        pe.sem_inc(s_freed, SLOTS)
        with pe.Fori(0, TURNS) as i:
            for q in range(SLOTS):
                g = i * SLOTS + q
                pe.wait_ge(s_hot, g + 1)
                pe.wait_ge(s_read, g + 1)
                pe.wait_ge(s_msg[q], i * (16 * G) + (16 * G + at[q]))
                for j in range(G):
                    last = nc.tensor.matmul(ps[q % 2][:, j, :], msg[q][:, j, :], hot[q % 2][:, j, :],
                                            start=True, stop=True)
                last.then_inc(s_freed, 1)

    @block.vector
    def _(v):
        v.sem_inc(s_read, 2)
        if zero_sums:
            nc.vector.memset(zero[:, :], 0.0).then_inc(s_z, 1)

        def group(x):
            if x.live(1):
                v.wait_ge(s_freed, x.at(1) + SLOTS - 1)
                nc.vector.tensor_tensor(
                    hot[x.slot(1, 2)][:, :, :], t["iota16"][:, :].unsqueeze(1).to_broadcast([P, G, P]),
                    t["target"][:, bass.ds(x.at(1) * G, G)].unsqueeze(2).to_broadcast([P, G, P]),
                    ALU.is_equal).then_inc(s_hot, 1)
            if x.live():
                w = windows(nc, mybir.EngineType.DVE, t, x.at() * G, G)
                v.wait_ge(s_freed, x.at() + SLOTS + 1)
                for j in range(G):
                    into = t["nodes_b"][:, bass.ds(w[j] * P, P)]
                    nc.vector.tensor_tensor(into, into, ps[x.slot(0, 2)][:, j, :], ALU.add).then_inc(s_acc, 1)
                    v.wait_ge(s_acc, x.at() * G + j + 1)
                v.sem_inc(s_read, 1)

        walk(v, group, 1, 0)


def windows(nc, engine, t, tile, n):
    _, w = nc.values_load_multi_w_load_instructions(t["window"][0:1, bass.ds(tile, n)], engines=(engine,),
                                                    min_val=0, max_val=W - 1)
    return w


class Steps:

    def __init__(self, engine, sem, base, stood=None):
        self.engine, self.sem, self.base, self.stood, self.n = engine, sem, base, stood, 0

    def stand(self):
        self.engine.sem_inc(self.stood, 1)

    def __call__(self, instruction):
        self.n += 1
        instruction.then_inc(self.sem, 1)
        self.engine.wait_ge(self.sem, self.base + self.n)


def normalize(nc, v, step, out, in_, stats, moments, s_var, s_std, turn):
    for j in range(BT):
        last = nc.vector.bn_stats(stats[:, j, :], in_[:, j, :])
    step(last)
    step.stand()
    for j in range(BT):
        last = nc.vector.bn_aggr(moments[:, j, :], stats[:, j, :])
    last.then_inc(s_var, 1)
    v.wait_ge(s_std, turn)
    step(nc.vector.reciprocal(moments[:, :, 1:2], moments[:, :, 1:2]))
    for j in range(BT):
        last = nc.vector.tensor_scalar(out[:, j, :], in_[:, j, :], moments[:, j, 0:1], moments[:, j, 1:2],
                                       ALU.subtract, ALU.mult)
    return last


def deviation(nc, act, moments, eps, s_var, s_std, turn):
    act.wait_ge(s_var, turn)
    nc.scalar.activation(moments[:, :, 1:2], moments[:, :, 1:2], ACT.Sqrt, bias=eps).then_inc(s_std, 1)


def add_landed(t, counts):
    before = list(t["landed_at"])
    t["landed_at"] = [a + b for a, b in zip(before, counts)]
    return before


def rows_of(v):
    return v.partition_broadcast(P)


def over_batch(row):
    return row[:, :].unsqueeze(1).to_broadcast([P, BT, D])


def tiles(a):
    return a[:, :].rearrange("p (a e) -> p a e", a=BT)


def project(nc, m, t, d, self_w, bias, wq, wk, wv, bq, bk, bv, g1, be1):
    wself = m.sb("wself", [D, D])
    wqkv = m.sb("wqkv", [D, 3 * D])
    bcol = m.sb("bcol", [D, 1])
    bqkv = m.sb("bqkv", [P, 3 * D])
    gain = m.sb("gain", [P, D])
    shift = m.sb("shift", [P, D])
    free = [0]

    def one(name, shape=(P, BT, D)):
        n = int(shape[1]) * int(shape[2])
        free[0] += n
        return t["big"][:, free[0] - n:free[0]].rearrange("p (a e) -> p a e", e=shape[2])

    xin, xl, n1 = ([one(f"{n}{h}") for h in range(2)] for n in ("xin", "xl", "n1"))
    qo, vo = one("qo"), one("vo")
    y = one("y")
    summed, ht = m.sb("summed", [D, BT * P]), m.sb("ht", [D, BT * P])
    n1t = m.sb("n1t", [D, BT * P])
    stats, moments = m.sb("stats", [P, BT, 6]), m.sb("moments", [P, BT, 2])
    ps_a, ps_b, ps_c = (m.ps(n, [P, 512]) for n in ("ps_self", "ps_rows", "ps_normed"))
    ps_d = m.ps("ps_qkv", [P, BT, 512])
    s_w, s_scaled, s_self, s_sum, s_ht, s_rows, s_norm, s_nt, s_n1t, s_qkv, s_q, s_k, s_v, s_xl, s_step = (
        m.sem(n) for n in ("q_weights", "q_scaled", "q_self", "q_summed", "q_relu", "q_rows", "q_normed",
                           "q_normed_t", "q_slot", "q_product", "q_q", "q_k", "q_v", "q_x", "q_step"))
    s_in = [m.sem(f"q_in{h}") for h in range(2)]
    s_sx = [m.sem(f"q_x_stored{h}") for h in range(2)]
    s_sq, s_sv = m.sem("q_q_stored"), m.sem("q_v_stored")
    s_stood = m.sem("q_stood")
    s_var, s_std, s_eps = m.sem("q_variance"), m.sem("q_deviation"), m.sem("q_eps")
    eps = m.sb("eps", [P, 1])
    STEPS = 7
    block = m.stack.enter_context(nc.Block())

    @block.sync
    def _(sp):
        n = 0
        for out, in_ in ((wself[:, :], self_w), (wqkv[:, 0:D], wq), (wqkv[:, D:2 * D], wk),
                         (wqkv[:, 2 * D:3 * D], wv), (bqkv[:, 0:D], rows_of(bq)),
                         (bqkv[:, D:2 * D], rows_of(bk)), (bqkv[:, 2 * D:3 * D], rows_of(bv)),
                         (gain[:, :], rows_of(g1)), (shift[:, :], rows_of(be1))):
            sp.dma_start(out, in_).then_inc(s_w, 16)
            n += 1
        with nc.allow_non_contiguous_dma(reason="a bias as a column"):
            sp.dma_start(bcol[:, :], bias.rearrange("(d a) -> d a", a=1)).then_inc(s_w, 16)
        sp.wait_ge(s_w, 16 * (n + 1))

        def batch(x):
            if x.live(2):
                if x.live():
                    sp.wait_ge(s_step, x.at() * STEPS + 1)
                sp.dma_start(xin[x.slot(2, 2)], batch_rows(d["xpad"], x, 2)).then_inc(s_in[x.slot(2, 2)], 16)
            if x.live():
                sp.wait_ge(s_xl, x.at() + 1)
                sp.dma_start(batch_rows(d["xl"], x), xl[x.slot(0, 2)]).then_inc(s_sx[x.slot(0, 2)], 16)
                sp.wait_ge(s_q, x.at() + 1)
                sp.dma_start(batch_rows(d["q"], x), qo).then_inc(s_sq, 16)
                sp.wait_ge(s_v, x.at() + 1)
                sp.dma_start(batch_rows(d["v"], x), vo).then_inc(s_sv, 16)

        walk(sp, batch, 2, 0, 2, BATCHES)
        for h in range(2):
            sp.wait_ge(s_sx[h], (BATCHES + 1 - h) // 2 * 16)
        sp.wait_ge(s_sq, BATCHES * 16)
        sp.wait_ge(s_sv, BATCHES * 16)

    @block.tensor
    def _(pe):
        pe.wait_ge(s_w, 160)
        pe.wait_ge(s_scaled, 2)

        def batch(x):
            if x.live(1):
                if x.live():
                    pe.wait_ge(s_sum, x.at() + 1)
                nc.tensor.matmul(ps_a[:, :], wself[:, :], batch_of(t["nodes_a"], x, 1),
                                 start=True, stop=True).then_inc(s_self, 1)
            if x.live():
                pe.wait_ge(s_norm, x.at() + 1)
                if x.live(-1):
                    pe.wait_ge(s_n1t, x.at(-1) + 1)
                for j in range(BT):
                    last = nc.tensor.transpose(ps_c[:, j * P:(j + 1) * P], n1[x.slot(0, 2)][:, j, :],
                                               t["ident"][:, :])
                last.then_inc(s_nt, 1)
            if x.live(1):
                pe.wait_ge(s_ht, x.at(1) + 1)
                if x.live():
                    pe.wait_ge(s_step, x.at() * STEPS + 1)
                for j in range(BT):
                    last = nc.tensor.transpose(ps_b[:, j * P:(j + 1) * P], ht[:, j * P:(j + 1) * P],
                                               t["ident"][:, :])
                last.then_inc(s_rows, 1)
            if x.live():
                pe.wait_ge(s_n1t, x.at() + 1)
                if x.live(-1):
                    pe.wait_ge(s_v, x.at(-1) + 1)
                for j in range(BT):
                    last = nc.tensor.matmul(ps_d[:, j, 0:3 * D], n1t[:, j * P:(j + 1) * P], wqkv[:, :],
                                            start=True, stop=True)
                last.then_inc(s_qkv, 1)

        walk(pe, batch, 1, 0, 2, BATCHES)

    @block.gpsimd
    def _(pool):
        pool.memset(eps[:, :], EPS).then_inc(s_eps, 1)

    @block.scalar
    def _(act):
        act.wait_ge(s_eps, 1)
        act.wait_ge(s_w, 160)

        def batch(x):
            if x.live(1):
                act.wait_ge(s_sum, x.at(1) + 1)
                if x.live():
                    act.wait_ge(s_rows, x.at() + 1)
                nc.scalar.activation(ht[:, :], summed[:, :], ACT.Relu, bias=bcol[:, :]).then_inc(s_ht, 1)
            if x.live():
                act.wait_ge(s_nt, x.at() + 1)
                if x.live(-1):
                    act.wait_ge(s_qkv, x.at(-1) + 1)
                nc.scalar.activation(n1t[:, :], ps_c[:, :], ACT.Copy).then_inc(s_n1t, 1)
            if x.live(1):
                for a in range(2):
                    deviation(nc, act, moments, eps[:, :], s_var, s_std, x.at(1) * 2 + 1 + a)

        walk(act, batch, 1, 0, 2, BATCHES)

    @block.vector
    def _(v):
        v.wait_ge(s_w, 160)
        nc.vector.tensor_scalar(wqkv[:, 0:D], wqkv[:, 0:D], HD ** -0.5, None, ALU.mult).then_inc(s_scaled, 1)
        nc.vector.tensor_scalar(bqkv[:, 0:D], bqkv[:, 0:D], HD ** -0.5, None, ALU.mult).then_inc(s_scaled, 1)
        v.wait_ge(s_scaled, 2)

        def batch(x):
            if x.live(1):
                v.wait_ge(s_self, x.at(1) + 1)
                if x.live():
                    v.wait_ge(s_ht, x.at() + 1)
                nc.vector.tensor_tensor(summed[:, :], ps_a[:, :], batch_of(t["nodes_b"], x, 1), ALU.add)\
                    .then_inc(s_sum, 1)
            if x.live():
                v.wait_ge(s_qkv, x.at() + 1)
                if x.live(-1):
                    v.wait_ge(s_sq, x.at() * 16)
                nc.vector.tensor_tensor(qo, ps_d[:, :, 0:D], over_batch(bqkv[:, 0:D]), ALU.add).then_inc(s_q, 1)
                nc.vector.tensor_tensor(tiles(batch_of(t["nodes_a"], x)), ps_d[:, :, D:2 * D],
                                        over_batch(bqkv[:, D:2 * D]), ALU.add).then_inc(s_k, 1)
                if x.live(-1):
                    v.wait_ge(s_sv, x.at() * 16)
                nc.vector.tensor_tensor(vo, ps_d[:, :, 2 * D:3 * D], over_batch(bqkv[:, 2 * D:3 * D]),
                                        ALU.add).then_inc(s_v, 1)
            if x.live(1):
                h = x.slot(1, 2)
                step = Steps(v, s_step, x.at(1) * STEPS, s_stood)
                v.wait_ge(s_in[h], x.turn(1) * 16 + 16)
                v.wait_ge(s_rows, x.at(1) + 1)
                step(nc.vector.tensor_tensor(y, tiles(ps_b), xin[h], ALU.add))
                last = normalize(nc, v, step, xl[h], y, stats, moments, s_var, s_std, x.at(1) * 2 + 1)
                last.then_inc(s_xl, 1)
                v.wait_ge(s_xl, x.at(1) + 1)
                step(normalize(nc, v, step, n1[h], xl[h], stats, moments, s_var, s_std, x.at(1) * 2 + 2))
                step(nc.vector.tensor_tensor(n1[h], n1[h], over_batch(gain), ALU.mult))
                nc.vector.tensor_tensor(n1[h], n1[h], over_batch(shift), ALU.add).then_inc(s_norm, 1)
                assert step.n == STEPS

        walk(v, batch, 1, 0, 2, BATCHES)


def score(nc, m, t, d, curv, wc, bc):
    slots = lambda n, k, shape, dt=FP32: [m.sb(f"{n}{q}", shape, dt) for q in range(k)]
    GH = G * H
    free = [0]

    def room(cols):
        free[0] += cols
        return t["big"][:, free[0] - cols:free[0]]

    index = slots("index", SLOTS, [P, G], I32)
    qrow = [room(G * D) for q in range(SLOTS)]
    cur = [room(G * D).rearrange("p (j e) -> p j e", j=G) for q in range(SLOTS)]
    of_node = [room(G * P) for h in range(2)]
    cur_t = [room(G * P) for h in range(2)]
    prod = room(G * D)
    trow = slots("trow", SLOTS, [P, G * P], BF16)
    far = m.sb("far", [P, G * P], BF16)
    mark = slots("mark", SLOTS, [GH, 2 * (P + 1)], BF16)
    curved = slots("curved", 2, [P, G, H])
    qk = slots("qk", 2, [P, GH])
    sc = slots("sc", 2, [P, GH])
    sc_t, run, top, less, ex, part, tot, rec, prob = (slots(n, 2, [GH, P]) for n in (
        "sc_t", "run", "top", "less", "ex", "part", "tot", "rec", "prob"))
    wc_sb = m.sb("wc_sb", [D, H])
    bias = m.sb("bias", [GH, 1])
    minus = m.sb("minus_lane", [P, 1])
    ps_m = m.ps("ps_runs", [P, 512])
    ps_c, ps_s, ps_k = ([m.ps(f"{n}{h}", [P, 512]) for h in range(2)] for n in ("ps_cur", "ps_score", "ps_key"))
    (s_w, s_index, s_freed, s_pc, s_far, s_node, s_ct, s_k, s_s, s_curved, s_prod, s_qk, s_sc, passed,
     s_pm, s_sct, s_run, s_top, s_less, s_ex, s_part, s_tot, s_rec, s_prob, s_link, s_minus) = (
        m.sem("s_" + n) for n in (
            "weights", "index", "slot_free", "curv_t", "far", "of_node", "curv_slot",
            "key", "curv_score", "curved", "products", "qk", "scores", "passed", "runs_t", "scores_slot",
            "run", "top", "less", "exp", "part_sum", "sum", "reciprocal", "prob", "link", "minus"))
    s_c = [m.sem(f"s_c{q}") for q in range(SLOTS)]
    s_tr = [m.sem(f"s_targets{q}") for q in range(SLOTS)]
    s_mk = [m.sem(f"s_marks{q}") for q in range(SLOTS)]
    s_st = [m.sem(f"s_st{h}") for h in range(2)]
    s_q = t["landed"]
    at = add_landed(t, [TURNS * G * 16] * SLOTS)
    block = m.stack.enter_context(nc.Block())

    @block.sync
    def _(sp):
        sp.dma_start(wc_sb[:, :], wc).then_inc(s_w, 16)
        with nc.allow_non_contiguous_dma(reason="a bias as a column"):
            for j in range(G):
                sp.dma_start(bias[j * H:(j + 1) * H, :], bc.rearrange("(h a) -> h a", a=1)).then_inc(s_w, 16)

        def group(x):
            if x.live(-4):
                q = x.slot(-4)
                if x.live(-4 - SLOTS):
                    sp.wait_ge(s_tot, x.at(-4 - SLOTS) + 1)
                sp.dma_start(mark[q][:, :], d["marks"][bass.ds(x.at(-4) * GH, GH), 0:2 * (P + 1)])\
                    .then_inc(s_mk[q], 16)
            if x.live():
                q = x.slot()
                _, first = nc.values_load_multi_w_load_instructions(
                    t["first_edge"][0:1, bass.ds(x.at() * G, G)], engines=(mybir.EngineType.SP,), min_val=0,
                    max_val=E - P)
                if x.live(-SLOTS):
                    sp.wait_ge(s_pc, x.at(-SLOTS) + 1)
                for j in range(G):
                    sp.dma_start(cur[q][:, j, :], curv[bass.ds(first[j], P), :]).then_inc(s_c[q], 16)

        walk(sp, group, 0, 4, peeled=2)

    @block.gpsimd
    def _(pool):
        with pool.Fori(0, TURNS) as i:
            for q in range(SLOTS):
                g = i * SLOTS + q
                ring_index(pool, s_index, g + 1, passed)
                for j in range(G):
                    pool.indirect_dma_start(qrow[q][:, j * D:(j + 1) * D], None, d["q"],
                                            bass.IndirectOffsetOnAxis(ap=index[q][:, j:j + 1], axis=0))\
                        .then_inc(s_q[q], 16)

    @block.scalar
    def _(act):
        act.wait_ge(s_w, 16 * (G + 1))
        nc.scalar.activation(minus[:, :], t["lane"][:, :], ACT.Copy, scale=-1.0).then_inc(s_minus, 1)
        act.wait_ge(s_minus, 1)

        def group(x):
            if x.live(1):
                h, q = x.slot(1, 2), x.slot(1)
                act.wait_ge(s_tr[q], x.turn(1) * 16 + 16)
                if x.live():
                    act.wait_ge(s_node, x.at() + 1)
                nc.scalar.activation(far[:, :], trow[q][:, :], ACT.Abs, bias=minus[:, :]).then_inc(s_far, 1)
                act.wait_ge(s_far, x.at(1) + 1)
                if x.live(-1):
                    act.wait_ge(s_k, x.at(-1) + 1)
                nc.scalar.activation(of_node[h], far[:, :], ACT.Relu, bias=1.0, scale=-1.0)\
                    .then_inc(s_node, 1)
            if x.live(1 + SLOTS):
                q = x.slot(1)
                act.dma_start(trow[q][:, :],
                              d["targets"][bass.ds(x.at(1 + SLOTS) * (G * P), G * P)].partition_broadcast(P))\
                    .then_inc(s_tr[q], 16)
            if x.live(3):
                if x.live(3 - SLOTS):
                    act.wait_ge(s_freed, x.at(3 - SLOTS) + 1)
                nc.scalar.activation(index[x.slot(3)][:, :], t["source"][:, bass.ds(x.at(3) * G, G)],
                                     ACT.Copy).then_inc(s_index, 1)
            if x.live(-1):
                h = x.slot(-1, 2)
                act.wait_ge(s_pm, x.at(-1) + 1)
                if x.live(-3):
                    act.wait_ge(s_less, x.at(-3) + 1)
                nc.scalar.activation(sc_t[h][:, :], ps_m[0:GH, 0:P], ACT.Identity, bias=bias[:, :])\
                    .then_inc(s_sct, 1)
            if x.live(1):
                h = x.slot(1, 2)
                act.wait_ge(s_pc, x.at(1) + 1)
                if x.live(-1):
                    act.wait_ge(s_s, x.at(-1) + 1)
                nc.scalar.activation(cur_t[h], ps_c[h][:, :], ACT.Copy).then_inc(s_ct, 1)
            if x.live(-2):
                h = x.slot(-2, 2)
                act.wait_ge(s_less, x.at(-2) + 1)
                if x.live(-4):
                    act.wait_ge(s_prob, x.at(-4) + 1)
                nc.scalar.activation(ex[h][:, :], less[h][:, :], ACT.Exp).then_inc(s_ex, 1)
            if x.live(-4):
                h = x.slot(-4, 2)
                act.wait_ge(s_prob, x.at(-4) + 1)
                act.dma_start(d["exp"][bass.ds(x.at(-4) * GH, GH), :], prob[h][:, :]).then_inc(s_st[h], 16)

        walk(act, group, 1 + SLOTS, 4)
        for h in range(2):
            act.wait_ge(s_st[h], GROUPS // 2 * 16)

    @block.tensor
    def _(pe):
        pe.wait_ge(s_w, 16 * (G + 1))

        def group(x):
            if x.live():
                h = x.slot(0, 2)
                w = windows(nc, mybir.EngineType.PE, t, x.at() * G, G)
                pe.wait_ge(s_node, x.at() + 1)
                if x.live(-2):
                    pe.wait_ge(s_prod, x.at(-2) + 1)
                for j in range(G):
                    last = nc.tensor.matmul(ps_k[h][:, j * D:(j + 1) * D], of_node[h][:, j * P:(j + 1) * P],
                                            t["nodes_a"][:, bass.ds(w[j] * P, P)], start=True, stop=True)
                last.then_inc(s_k, 1)
            if x.live(-1):
                h = x.slot(-1, 2)
                pe.wait_ge(s_sc, x.at(-1) + 1)
                if x.live(-2):
                    pe.wait_ge(s_sct, x.at(-2) + 1)
                nc.tensor.transpose(ps_m[0:GH, 0:P], sc[h][:, :], t["ident"][:, :]).then_inc(s_pm, 1)
            if x.live(1):
                pe.wait_ge(s_c[x.slot(1)], x.turn(1) * (16 * G) + 16 * G)
                h = x.slot(1, 2)
                if x.live(-1):
                    pe.wait_ge(s_ct, x.at(-1) + 1)
                for j in range(G):
                    last = nc.tensor.transpose(ps_c[h][:, j * P:(j + 1) * P], cur[x.slot(1)][:, j, :],
                                               t["ident"][:, :])
                last.then_inc(s_pc, 1)
            if x.live():
                h = x.slot(0, 2)
                pe.wait_ge(s_ct, x.at() + 1)
                if x.live(-2):
                    pe.wait_ge(s_curved, x.at(-2) + 1)
                for j in range(G):
                    last = nc.tensor.matmul(ps_s[h][:, j * H:(j + 1) * H], cur_t[h][:, j * P:(j + 1) * P],
                                            wc_sb[:, :], start=True, stop=True)
                last.then_inc(s_s, 1)

        walk(pe, group, 1, 1)

    @block.vector
    def _(v):
        link_m, link_s = (t[n].rearrange("p (g a) -> p g a", a=2) for n in ("link_m", "link_s"))

        def group(x):
            if x.live(-2):
                h, q = x.slot(-2, 2), x.slot(-2)
                v.wait_ge(s_mk[q], x.turn(-2) * 16 + 16)
                v.wait_ge(s_sct, x.at(-2) + 1)
                nc.vector.tensor_tensor_scan(run[h][:, :], mark[q][:, 0:P], sc_t[h][:, :], -BIG, ALU.add,
                                             ALU.max).then_inc(s_run, 1)
            if x.live(-3):
                h, q = x.slot(-3, 2), x.slot(-3)
                v.wait_ge(s_ex, x.at(-3) + 1)
                nc.vector.tensor_tensor_scan(part[h][:, :], mark[q][:, P + 1:2 * P + 1], ex[h][:, :], 0.0,
                                             ALU.mult, ALU.add).then_inc(s_part, 1)
            if x.live(-2):
                h, q = x.slot(-2, 2), x.slot(-2)
                v.wait_ge(s_run, x.at(-2) + 1)
                nc.vector.tensor_tensor_scan(top[h][:, ::-1], mark[q][:, P:0:-1], run[h][:, ::-1], -BIG,
                                             ALU.add, ALU.max).then_inc(s_top, 1)
            if x.live(-3):
                h, q = x.slot(-3, 2), x.slot(-3)
                v.wait_ge(s_part, x.at(-3) + 1)
                nc.vector.tensor_tensor_scan(tot[h][:, ::-1], mark[q][:, 2 * P + 1:P + 1:-1],
                                             part[h][:, ::-1], 0.0, ALU.mult, ALU.max).then_inc(s_tot, 1)
            if x.live(-2):
                h = x.slot(-2, 2)
                v.wait_ge(s_top, x.at(-2) + 1)
                nc.vector.tensor_tensor(less[h][:, :], sc_t[h][:, :], top[h][:, :], ALU.subtract)\
                    .then_inc(s_less, 1)
                nc.vector.tensor_copy(link_m[:, bass.ds(x.at(-2), 1), :], top[h][:, 0:P:P - 1].unsqueeze(1))\
                    .then_inc(s_link, 1)
            if x.live(-3):
                h = x.slot(-3, 2)
                v.wait_ge(s_tot, x.at(-3) + 1)
                nc.vector.tensor_copy(link_s[:, bass.ds(x.at(-3), 1), :], tot[h][:, 0:P:P - 1].unsqueeze(1))\
                    .then_inc(s_link, 1)
                nc.vector.reciprocal(rec[h][:, :], tot[h][:, :]).then_inc(s_rec, 1)
            if x.live():
                h, q = x.slot(0, 2), x.slot()
                v.wait_ge(s_k, x.at() + 1)
                v.wait_ge(s_q[q], x.turn() * (16 * G) + (16 * G + at[q]))
                if x.live(-1):
                    v.wait_ge(s_qk, x.at(-1) + 1)
                nc.vector.tensor_tensor(prod, ps_k[h][:, :], qrow[q], ALU.mult).then_inc(s_prod, 1)
                v.wait_ge(s_s, x.at() + 1)
                nc.vector.tensor_tensor(curved[h][:, :, :], ps_s[h][:, 0:GH].rearrange("p (j a) -> p j a", a=H),
                                        t["penalty"][:, bass.ds(x.at() * G, G)].unsqueeze(2)
                                        .to_broadcast([P, G, H]), ALU.add).then_inc(s_curved, 1)
                v.wait_ge(s_prod, x.at() + 1)
                nc.vector.tensor_reduce(qk[h][:, :], prod.rearrange("p (a e) -> p a e", e=HD),
                                        AX.X, ALU.add).then_inc(s_qk, 1)
                v.wait_ge(s_qk, x.at() + 1)
                v.wait_ge(s_curved, x.at() + 1)
                if x.live(-2):
                    v.wait_ge(s_pm, x.at(-2) + 1)
                nc.vector.tensor_tensor(sc[h][:, :], qk[h][:, :],
                                        curved[h][:, :, :].rearrange("p j a -> p (j a)"), ALU.add)\
                    .then_inc(s_sc, 1)
                v.sem_inc(s_freed, 1)
            if x.live(-3):
                h = x.slot(-3, 2)
                v.wait_ge(s_rec, x.at(-3) + 1)
                if x.live(-5):
                    v.wait_ge(s_st[h], x.half(-5) * 16 + 16)
                nc.vector.tensor_tensor(prob[h][:, :], ex[h][:, :], rec[h][:, :], ALU.mult).then_inc(s_prob, 1)

        walk(v, group, 0, 3, peeled=2)


def combine(nc, m, t, d):
    L = 2 * K
    cols = L // G
    seq_m, seq_s, key, a, b, f = (t["big"][0:H, n * L:(n + 1) * L] for n in range(6))
    z = t["nodes_a"][0:H, 0:L]
    split = [m.sb(f"split{j}", [H, cols]) for j in range(2 * G)]
    reset, go_on = m.sb("reset", [H, L + 1], BF16), m.sb("go_on", [H, L + 1], BF16)
    s_in, s_v, s_exp, s_back = m.sem("b_in"), m.sem("b_step"), m.sem("b_exp"), m.sem("b_back")
    block = m.stack.enter_context(nc.Block())
    links = (t["link_m"], t["link_s"])
    BEFORE_EXP = 2 * G + 9
    ALL = BEFORE_EXP + 6 + G

    def place(seq, j):
        return seq.rearrange("p (g j a) -> p g j a", j=G, a=2)[:, :, j, :]

    @block.sync
    def _(sp):
        for n in range(2 * G):
            j = n % G
            sp.dma_start(split[n][:, :], links[n // G][j * H:(j + 1) * H, :]).then_inc(s_in, 16)
        sp.dma_start(key, d["keys"].partition_broadcast(H)).then_inc(s_in, 16)
        sp.wait_ge(s_v, ALL)
        for j in range(G):
            sp.dma_start(t["link_m"][j * H:(j + 1) * H, :], split[j][:, :]).then_inc(s_back, 16)
        sp.wait_ge(s_back, 16 * G)

    @block.vector
    def _(v):
        n = [0]

        def link(ins):
            n[0] += 1
            ins.then_inc(s_v, 1)
            v.wait_ge(s_v, n[0])

        v.wait_ge(s_in, 16 * (2 * G + 1))
        for j in range(2 * G):
            link(nc.vector.tensor_copy(place((seq_m, seq_s)[j // G], j % G),
                                       split[j][:, :].rearrange("p (g a) -> p g a", a=2)))
        link(nc.vector.memset(go_on[:, :], 0.0))
        link(nc.vector.tensor_tensor(go_on[:, 1:L], key[:, 1:L], key[:, 0:L - 1], ALU.is_equal))
        link(nc.vector.tensor_scalar(reset[:, :], go_on[:, :], BIG, -BIG, ALU.mult, ALU.add))
        link(nc.vector.tensor_tensor_scan(a, reset[:, 0:L], seq_m, -BIG, ALU.add, ALU.max))
        link(nc.vector.tensor_tensor_scan(b[:, ::-1], reset[:, L:0:-1], a[:, ::-1], -BIG, ALU.add, ALU.max))
        link(nc.vector.tensor_tensor(a, seq_m, b, ALU.subtract))
        link(nc.vector.tensor_copy(z, seq_s))
        odd = z.rearrange("p (k a) -> p k a", a=2)[:, :, 1:2]
        same = go_on[:, 0:L].rearrange("p (k a) -> p k a", a=2)[:, :, 1:2]
        link(nc.vector.tensor_scalar(key[:, 0:K].unsqueeze(2), same, -1.0, 1.0, ALU.mult, ALU.add))
        link(nc.vector.tensor_tensor(odd, odd, key[:, 0:K].unsqueeze(2), ALU.mult))
        assert n[0] == BEFORE_EXP
        v.wait_ge(s_exp, 1)
        link(nc.vector.tensor_tensor(z, z, f, ALU.mult))
        link(nc.vector.tensor_tensor_scan(a, go_on[:, 0:L], z, 0.0, ALU.mult, ALU.add))
        link(nc.vector.tensor_tensor_scan(b[:, ::-1], go_on[:, L:0:-1], a[:, ::-1], 0.0, ALU.mult, ALU.max))
        link(nc.vector.reciprocal(a, b))
        link(nc.vector.tensor_tensor(f, f, seq_s, ALU.mult))
        link(nc.vector.tensor_tensor(f, f, a, ALU.mult))
        for j in range(G):
            link(nc.vector.tensor_copy(split[j][:, :].rearrange("p (g a) -> p g a", a=2), place(f, j)))
        assert n[0] == ALL

    @block.scalar
    def _(act):
        act.wait_ge(s_v, BEFORE_EXP)
        nc.scalar.activation(f, a, ACT.Exp).then_inc(s_exp, 1)


def scatter(nc, m, t, d):
    slots = lambda n, k, shape, dt=FP32: [m.sb(f"{n}{q}", shape, dt) for q in range(k)]
    GH = G * H
    values = t["nodes_a"]
    free = [0]

    def room(cols):
        free[0] += cols
        return t["big"][:, free[0] - cols:free[0]]

    def of_tiles(a):
        return a.rearrange("p (j e) -> p j e", j=G)

    index = slots("index", SLOTS, [P, G], I32)
    dest = slots("dest", SLOTS, [P, G], I32)
    total = [room(G * D) for q in range(SLOTS)]
    of_node, msg = ([room(G * P) for h in range(2)] for n in range(2))
    same = [of_tiles(room(G * P)) for h in range(SLOTS)]
    dup = of_tiles(room(G * P))
    trow = slots("trow", SLOTS, [P, G * P], BF16)
    far = m.sb("far", [P, G * P], BF16)
    prob_t = slots("prob_t", SLOTS, [GH, P])
    mark = slots("mark", SLOTS, [GH, 3 * P], BF16)
    scale1, scale2, scaled = (slots(n, 2, [GH, P]) for n in ("scale1", "scale2", "scaled"))
    prob = slots("prob", 2, [P, GH])
    srcs, dups, away, moved = (slots(n, 2, [P, G]) for n in ("srcs", "dups", "away", "moved"))
    minus = m.sb("minus_lane", [P, 1])
    ps_q, ps_p, ps_v, ps_o = ([m.ps(f"{n}{h}", [P, 512]) for h in range(2)] for n in (
        "ps_src", "ps_prob", "ps_val", "ps_tot"))
    (s_val, s_slot, s_ps, s_far, s_node, s_scale1, s_scale2, s_scaled, s_pp, s_prob, s_same, s_dup, s_dups,
     s_away, s_moved, s_dest, s_index, s_v, s_msg, s_o, s_tot, s_free, passed, s_minus) = (
        m.sem("c_" + n) for n in (
            "v_table", "slots", "source_t", "far", "of_node", "scale1", "scale2", "scaled", "prob_back",
            "prob", "same", "dup", "dups", "away", "moved", "dest", "index", "values", "msg", "product", "total",
            "total_free", "passed", "minus"))
    s_pr, s_mk, s_tr = ([m.sem(f"c_{n}{q}") for q in range(SLOTS)] for n in ("prob", "marks", "targets"))
    s_sc = t["landed"]
    at = add_landed(t, [TURNS * 2 * G * 16] * 2 + [0, 0])
    block = m.stack.enter_context(nc.Block())

    @block.sync
    def _(sp):
        sp.dma_start(values.rearrange("p (a e) -> p a e", e=D), d["v"].rearrange("(a p) e -> p a e", p=P))\
            .then_inc(s_val, 16)

        def group(x):
            q = x.slot()
            if x.live(-SLOTS):
                sp.wait_ge(s_far, x.at(-SLOTS) + 1)
                sp.wait_ge(s_scaled, x.at(-SLOTS) + 1)
            sp.dma_start(trow[q][:, :], d["targets"][bass.ds(x.at() * (G * P), G * P)].partition_broadcast(P))\
                .then_inc(s_tr[q], 16)
            sp.dma_start(prob_t[q][:, :], d["exp"][bass.ds(x.at() * GH, GH), :]).then_inc(s_pr[q], 16)
            sp.dma_start(mark[q][:, :], d["marks"][bass.ds(x.at() * GH, GH), 2 * (P + 1):MARKS])\
                .then_inc(s_mk[q], 16)

        walk(sp, group, 0, 0)

    @block.scalar
    def _(act):
        nc.scalar.activation(minus[:, :], t["lane"][:, :], ACT.Copy, scale=-1.0).then_inc(s_minus, 1)
        act.wait_ge(s_minus, 1)

        def group(x):
            if x.live(-2):
                h, q = x.slot(-2, 2), x.slot(-2)
                act.wait_ge(s_free, x.at(-2) + 1)
                act.wait_ge(s_dest, x.at(-2) + 1)
                nc.scalar.activation(index[q][:, :], dest[q][:, :], ACT.Copy).then_inc(s_index, 1)
                act.wait_ge(s_o, x.at(-2) + 1)
                nc.scalar.activation(total[q], ps_o[h][:, :], ACT.Copy).then_inc(s_tot, 1)
            if x.live(2):
                h = x.slot(2, 2)
                if x.live():
                    act.wait_ge(s_dest, x.at() + 1)
                nc.scalar.activation(srcs[h][:, :], t["source_or_dump"][:, bass.ds(x.at(2) * G, G)],
                                     ACT.Copy).then_inc(s_slot, 1)
            if x.live(1):
                h, q = x.slot(1, 2), x.slot(1)
                act.wait_ge(s_tr[q], x.turn(1) * 16 + 16)
                if x.live():
                    act.wait_ge(s_node, x.at() + 1)
                nc.scalar.activation(far[:, :], trow[q][:, :], ACT.Abs, bias=minus[:, :]).then_inc(s_far, 1)
                act.wait_ge(s_far, x.at(1) + 1)
                if x.live(-1):
                    act.wait_ge(s_v, x.at(-1) + 1)
                nc.scalar.activation(of_node[h], far[:, :], ACT.Relu, bias=1.0, scale=-1.0)\
                    .then_inc(s_node, 1)
                act.wait_ge(s_pp, x.at(1) + 1)
                if x.live(-1):
                    act.wait_ge(s_msg, x.at(-1) + 1)
                nc.scalar.activation(prob[h][:, :], ps_p[h][:, 0:GH], ACT.Copy).then_inc(s_prob, 1)

        walk(act, group, 2, 2)

    @block.gpsimd
    def _(pool):
        pool.sem_inc(s_free, SLOTS)

        def group(x):
            h, q = x.slot(0, 2), x.slot()
            pool.wait_ge(s_index, x.at() + 1)
            ring_index(pool, s_tot, x.at() + 1, passed)
            for j in range(G):
                pool.indirect_dma_start(d["sums"][h * G + j],
                                        bass.IndirectOffsetOnAxis(ap=index[q][:, j:j + 1], axis=0),
                                        total[q][:, j * D:(j + 1) * D], None, compute_op=ALU.add)\
                    .then_inc(s_sc[h], 16)
            if x.live(-1):
                ring_index(pool, s_sc[1 - h], x.half(-1) * (16 * G) + (16 * G + at[1 - h]), s_free)

        walk(pool, group, 0, 0)
        for h in range(2):
            pool.wait_ge(s_sc[h], TURNS * 2 * 16 * G + at[h])

    @block.tensor
    def _(pe):
        pe.wait_ge(s_val, 16)

        def group(x):
            if x.live(1):
                h = x.slot(1, 2)
                pe.wait_ge(s_slot, x.at(1) + 1)
                if x.live(-1):
                    pe.wait_ge(s_same, x.at(-1) + 1)
                    pe.wait_ge(s_prob, x.at(-1) + 1)
                pe.wait_ge(s_scaled, x.at(1) + 1)
                for j in range(G):
                    last = nc.tensor.transpose(ps_q[h][:, j * P:(j + 1) * P],
                                               srcs[h][:, j:j + 1].to_broadcast([P, P]), t["ident"][:, :])
                last.then_inc(s_ps, 1)
                nc.tensor.transpose(ps_p[h][:, 0:GH], scaled[h][:, :], t["ident"][0:GH, 0:GH]).then_inc(s_pp, 1)
            if x.live():
                h = x.slot(0, 2)
                w = windows(nc, mybir.EngineType.PE, t, x.at() * G, G)
                pe.wait_ge(s_node, x.at() + 1)
                if x.live(-2):
                    pe.wait_ge(s_msg, x.at(-2) + 1)
                for j in range(G):
                    last = nc.tensor.matmul(ps_v[h][:, j * D:(j + 1) * D], of_node[h][:, j * P:(j + 1) * P],
                                            values[:, bass.ds(w[j] * P, P)], start=True, stop=True)
                last.then_inc(s_v, 1)
            if x.live(-1):
                h = x.slot(-1, 2)
                pe.wait_ge(s_msg, x.at(-1) + 1)
                if x.live(-3):
                    pe.wait_ge(s_tot, x.at(-3) + 1)
                for j in range(G):
                    last = nc.tensor.matmul(ps_o[h][:, j * D:(j + 1) * D], same[x.slot(-1)][:, j, :],
                                            msg[h][:, j * D:(j + 1) * D], start=True, stop=True)
                last.then_inc(s_o, 1)

        walk(pe, group, 1, 1)

    @block.vector
    def _(v):
        def group(x):
            if x.live(2):
                h, q = x.slot(2, 2), x.slot(2)
                of_first, of_last = (t["link_m"][:, bass.ds(x.at(2) * 2 + a, 1)] for a in range(2))
                v.wait_ge(s_mk[q], x.turn(2) * 16 + 16)
                nc.vector.scalar_tensor_tensor(scale1[h][:, :], mark[q][:, 0:P], of_first, mark[q][:, 2 * P:3 * P],
                                               ALU.mult, ALU.add).then_inc(s_scale1, 1)
                v.wait_ge(s_scale1, x.at(2) + 1)
                nc.vector.scalar_tensor_tensor(scale2[h][:, :], mark[q][:, P:2 * P], of_last, scale1[h][:, :],
                                               ALU.mult, ALU.add).then_inc(s_scale2, 1)
            if x.live():
                h = x.slot(0, 2)
                v.wait_ge(s_prob, x.at() + 1)
                v.wait_ge(s_v, x.at() + 1)
                if x.live(-2):
                    v.wait_ge(s_o, x.at(-2) + 1)
                nc.vector.tensor_tensor(
                    msg[h][:, :].rearrange("p (a e) -> p a e", e=HD),
                    ps_v[h][:, :].rearrange("p (a e) -> p a e", e=HD),
                    prob[h][:, :].unsqueeze(2).to_broadcast([P, GH, HD]), ALU.mult).then_inc(s_msg, 1)
            if x.live(2):
                h, q = x.slot(2, 2), x.slot(2)
                v.wait_ge(s_pr[q], x.turn(2) * 16 + 16)
                v.wait_ge(s_scale2, x.at(2) + 1)
                if x.live():
                    v.wait_ge(s_pp, x.at() + 1)
                nc.vector.tensor_tensor(scaled[h][:, :], prob_t[q][:, :], scale2[h][:, :], ALU.mult)\
                    .then_inc(s_scaled, 1)
            if x.live(1):
                h = x.slot(1, 2)
                v.wait_ge(s_ps, x.at(1) + 1)
                if x.live(1 - SLOTS):
                    v.wait_ge(s_o, x.at(1 - SLOTS) + 1)
                nc.vector.tensor_tensor(same[x.slot(1)], of_tiles(ps_q[h][:, :]),
                                        srcs[h][:, :].unsqueeze(2).to_broadcast([P, G, P]), ALU.is_equal)\
                    .then_inc(s_same, 1)
                nc.vector.tensor_scalar(away[h][:, :], srcs[h][:, :], -1.0, t["dump_row"][:, :], ALU.mult,
                                        ALU.add).then_inc(s_away, 1)
                v.wait_ge(s_same, x.at(1) + 1)
                nc.vector.tensor_tensor(dup, same[x.slot(1)], t["earlier"][:, :].unsqueeze(1).to_broadcast([P, G, P]),
                                        ALU.mult).then_inc(s_dup, 1)
                v.wait_ge(s_dup, x.at(1) + 1)
                nc.vector.tensor_reduce(dups[h][:, :], dup, AX.X, ALU.add).then_inc(s_dups, 1)
                v.wait_ge(s_dups, x.at(1) + 1)
                v.wait_ge(s_away, x.at(1) + 1)
                nc.vector.scalar_tensor_tensor(moved[h][:, :], dups[h][:, :], 1.0, away[h][:, :], ALU.min,
                                               ALU.mult).then_inc(s_moved, 1)
                v.wait_ge(s_moved, x.at(1) + 1)
                if x.live(1 - SLOTS):
                    v.wait_ge(s_index, x.at(1 - SLOTS) + 1)
                nc.vector.tensor_tensor(dest[x.slot(1)][:, :], moved[h][:, :], srcs[h][:, :], ALU.add)\
                    .then_inc(s_dest, 1)

        walk(v, group, 2, 0)


def finish(nc, m, t, d, wo, bo, g2, be2, wf1, bf1, wf2, bf2, out):
    NF = FF // P
    wo_sb = m.sb("wo_sb", [D, D])
    w1_sb = m.sb("w1_sb", [D, FF])
    w2_sb = m.sb("w2_sb", [P, NF, D])
    b1_sb = m.sb("b1_sb", [P, NF])
    bo_sb, b2_sb, gain, shift = (m.sb(n, [P, D]) for n in ("bo_sb", "b2_sb", "gain", "shift"))
    free = [0]

    def one(name, shape=(P, BT, D)):
        n = int(shape[1]) * int(shape[2])
        free[0] += n
        return t["big"][:, free[0] - n:free[0]].rearrange("p (a e) -> p a e", e=shape[2])

    parts = [one(f"parts{h}", (P, BT * REP, D)).rearrange("p (a r) e -> p a r e", r=REP) for h in range(2)]
    xl, o, n2, x2, yo = ([one(f"{n}{h}") for h in range(2)] for n in ("xl", "o", "n2", "x2", "yo"))
    x1, y = one("x1"), one("y")
    ot, n2t = one("ot", (D, BT, P)), one("n2t", (D, BT, P))
    hid = one("hid", (P, NF * BT, P)).rearrange("p (c a) e -> p c a e", c=NF)
    stats = [m.sb(f"stats{a}", [P, BT, 6]) for a in range(2)]
    moments = [m.sb(f"moments{a}", [P, BT, 2]) for a in range(2)]
    ps_o, ps_a, ps_n, ps_y = (m.ps(n, [P, 512]) for n in ("ps_sum", "ps_att", "ps_normed", "ps_ffn"))
    ps_f = [m.ps(f"ps_hid{c}", [P, 512]) for c in range(NF)]
    s_w, s_o, s_ot, s_otc, s_att, s_n2, s_nt, s_n2t, s_f, s_hid, s_y, s_out, s_step1, s_step2, s_x2 = (
        m.sem(n) for n in ("f_weights", "f_sum", "f_sum_t", "f_sum_slot", "f_attention", "f_normed",
                           "f_normed_t", "f_slot", "f_hidden", "f_relu", "f_ffn", "f_out", "f_step",
                           "f_step_out", "f_residual"))
    s_in, s_xl, s_st = ([m.sem(f"{n}{h}") for h in range(2)] for n in ("f_in", "f_x", "f_stored"))
    s_stood = m.sem("f_stood")
    s_var, s_std, s_var2, s_std2, s_eps = (m.sem(n) for n in (
        "f_variance", "f_deviation", "f_variance_out", "f_deviation_out", "f_eps"))
    eps = m.sb("eps", [P, 1])
    STEPS1, STEPS2 = 6, 3
    block = m.stack.enter_context(nc.Block())

    @block.sync
    def _(sp):
        n = 0
        for to, of in ((wo_sb[:, :], wo), (w1_sb[:, :], wf1), (w2_sb[:, :, :], wf2.rearrange("(c p) e -> p c e", p=P)),
                       (bo_sb[:, :], rows_of(bo)), (b2_sb[:, :], rows_of(bf2)),
                       (gain[:, :], rows_of(g2)), (shift[:, :], rows_of(be2))):
            sp.dma_start(to, of).then_inc(s_w, 16)
            n += 1
        with nc.allow_non_contiguous_dma(reason="a bias as columns"):
            sp.dma_start(b1_sb[:, :], bf1.rearrange("(c p) -> p c", p=P)).then_inc(s_w, 16)
        sp.wait_ge(s_w, 16 * (n + 1))

        def batch(x):
            if x.live(3):
                h = x.slot(3, 2)
                if x.live(1):
                    sp.wait_ge(s_o, x.at(1) + 1)
                for r in range(REP):
                    sp.dma_start(parts[h][:, :, r, :], batch_rows(d["sums"][r], x, 3)).then_inc(s_in[h], 16)
            if x.live(2):
                h = x.slot(2, 2)
                if x.live():
                    sp.wait_ge(s_x2, x.at() * 2 + 2)
                sp.dma_start(xl[h], batch_rows(d["xl"], x, 2)).then_inc(s_xl[h], 16)
            if x.live():
                h = x.slot(0, 2)
                sp.wait_ge(s_out, x.at() + 1)
                n0 = x.at() * BT * P
                if not isinstance(n0, int) or n0 + BT * P <= N:
                    sp.dma_start(batch_rows(out, x), yo[h]).then_inc(s_st[h], 16)
                else:
                    assert n0 < N <= n0 + P
                    sp.dma_start(out[n0:N, :], yo[h][0:N - n0, 0, :]).then_inc(s_st[h], 16)

        walk(sp, batch, 3, 0, 2, BATCHES)
        for h in range(2):
            sp.wait_ge(s_st[h], (BATCHES + 1 - h) // 2 * 16)

    @block.tensor
    def _(pe):
        pe.wait_ge(s_w, 128)

        def batch(x):
            if x.live(1):
                pe.wait_ge(s_o, x.at(1) + 1)
                if x.live():
                    pe.wait_ge(s_otc, x.at() + 1)
                for j in range(BT):
                    last = nc.tensor.transpose(ps_o[:, j * P:(j + 1) * P], o[x.slot(1, 2)][:, j, :], t["ident"][:, :])
                last.then_inc(s_ot, 1)
            if x.live():
                pe.wait_ge(s_n2, x.at() + 1)
                if x.live(-1):
                    pe.wait_ge(s_n2t, x.at(-1) + 1)
                for j in range(BT):
                    last = nc.tensor.transpose(ps_n[:, j * P:(j + 1) * P], n2[x.slot(0, 2)][:, j, :], t["ident"][:, :])
                last.then_inc(s_nt, 1)
            if x.live(1):
                pe.wait_ge(s_otc, x.at(1) + 1)
                if x.live():
                    pe.wait_ge(s_step1, x.at() * STEPS1 + 1)
                for j in range(BT):
                    last = nc.tensor.matmul(ps_a[:, j * D:(j + 1) * D], ot[:, j, :], wo_sb[:, :], start=True, stop=True)
                last.then_inc(s_att, 1)
            if x.live():
                pe.wait_ge(s_n2t, x.at() + 1)
                for c in range(NF):
                    if x.live(-1):
                        pe.wait_ge(s_hid, x.at(-1) * NF + (c + 1))
                    nc.tensor.matmul(ps_f[c][:, :], w1_sb[:, c * P:(c + 1) * P],
                                     n2t.rearrange("p a e -> p (a e)"), start=True, stop=True).then_inc(s_f, 1)
                pe.wait_ge(s_hid, x.at() * NF + NF)
                if x.live(-1):
                    pe.wait_ge(s_step2, x.at(-1) * STEPS2 + 1)
                for j in range(BT):
                    for c in range(NF):
                        last = nc.tensor.matmul(ps_y[:, j * D:(j + 1) * D], hid[:, c, j, :], w2_sb[:, c, :],
                                                start=(c == 0), stop=(c == NF - 1))
                last.then_inc(s_y, 1)

        walk(pe, batch, 1, 0, 2, BATCHES)

    @block.gpsimd
    def _(pool):
        pool.memset(eps[:, :], EPS).then_inc(s_eps, 1)

    @block.scalar
    def _(act):
        act.wait_ge(s_eps, 1)
        act.wait_ge(s_w, 128)

        def batch(x):
            if x.live(1):
                act.wait_ge(s_ot, x.at(1) + 1)
                if x.live():
                    act.wait_ge(s_att, x.at() + 1)
                nc.scalar.activation(ot, tiles(ps_o), ACT.Copy).then_inc(s_otc, 1)
            if x.live():
                act.wait_ge(s_nt, x.at() + 1)
                if x.live(-1):
                    act.wait_ge(s_f, x.at(-1) * NF + NF)
                nc.scalar.activation(n2t, tiles(ps_n), ACT.Copy).then_inc(s_n2t, 1)
            if x.live(1):
                deviation(nc, act, moments[0], eps[:, :], s_var, s_std, x.at(1) + 1)
            if x.live():
                if x.live(-1):
                    act.wait_ge(s_y, x.at(-1) + 1)
                for c in range(NF):
                    act.wait_ge(s_f, x.at() * NF + (c + 1))
                    nc.scalar.activation(hid[:, c, :, :], tiles(ps_f[c]), ACT.Relu,
                                         bias=b1_sb[:, c:c + 1]).then_inc(s_hid, 1)
                deviation(nc, act, moments[1], eps[:, :], s_var2, s_std2, x.at() + 1)

        walk(act, batch, 1, 0, 2, BATCHES)

    @block.vector
    def _(v):
        v.wait_ge(s_w, 128)
        NIN = 16 * REP

        def batch(x):
            if x.live(1):
                h = x.slot(1, 2)
                step = Steps(v, s_step1, x.at(1) * STEPS1, s_stood)
                v.wait_ge(s_att, x.at(1) + 1)
                step(nc.vector.tensor_tensor(x1, tiles(ps_a), over_batch(bo_sb), ALU.add))
                v.wait_ge(s_xl[h], x.turn(1) * 16 + 16)
                step(nc.vector.tensor_tensor(x1, x1, xl[h], ALU.add))
                step(normalize(nc, v, step, n2[h], x1, stats[0], moments[0], s_var, s_std, x.at(1) + 1))
                step(nc.vector.tensor_tensor(n2[h], n2[h], over_batch(gain), ALU.mult))
                assert step.n == STEPS1
                nc.vector.tensor_tensor(n2[h], n2[h], over_batch(shift), ALU.add).then_inc(s_n2, 1)
            if x.live(2):
                h = x.slot(2, 2)
                v.wait_ge(s_in[h], x.turn(2) * NIN + NIN)
                if x.live():
                    v.wait_ge(s_ot, x.at() + 1)
                for j in range(BT):
                    last = nc.vector.tensor_reduce(o[h][:, j, :], parts[h][:, j, :, :].rearrange("p r e -> p e r"),
                                                   AX.X, ALU.add)
                last.then_inc(s_o, 1)
            if x.live():
                h = x.slot(0, 2)
                step = Steps(v, s_step2, x.at() * STEPS2, s_stood)
                v.wait_ge(s_x2, x.at() * 2 + 2)
                v.wait_ge(s_y, x.at() + 1)
                step(nc.vector.tensor_tensor(y, tiles(ps_y), x2[h], ALU.add))
                if x.live(-2):
                    v.wait_ge(s_st[h], x.turn(-2) * 16 + 16)
                normalize(nc, v, step, yo[h], y, stats[1], moments[1], s_var2, s_std2, x.at() + 1)\
                    .then_inc(s_out, 1)
                assert step.n == STEPS2
            if x.live(1):
                h = x.slot(1, 2)
                nc.vector.tensor_tensor(x2[h], x1, xl[h], ALU.add).then_inc(s_x2, 1)
                v.wait_ge(s_x2, x.at(1) * 2 + 1)
                nc.vector.tensor_tensor(x2[h], x2[h], over_batch(b2_sb), ALU.add).then_inc(s_x2, 1)

        walk(v, batch, 2, 0, 2, BATCHES)


def build(nc, x, src, dst, curv, rel, w1, sl1, b1, w2, sl2, b2, wq, bq, wk, bk, wv, bv, wo, bo, wc, bc,
          wf1, bf1, wf2, bf2, g1, be1, g2, be2, out):
    with ExitStack() as top:
        keep = Memory(nc, top, "")
        t = {
            "ident": keep.sb("ident", [P, P]), "iota": keep.sb("iota", [P, P]),
            "earlier": keep.sb("earlier", [P, P]), "lane": keep.sb("lane", [P, 1]),
            "dump_row": keep.sb("dump_row", [P, 1]),
            "iota16": keep.sb("iota16", [P, P], BF16),
            "source": keep.sb("source", [P, K], I16), "source_or_dump": keep.sb("source_or_dump", [P, K], I16),
            "target": keep.sb("target", [P, K], BF16), "penalty": keep.sb("penalty", [P, K], BF16),
            "window": keep.sb("window", [1, K], I32), "first_edge": keep.sb("first_edge", [1, K], I32),
            "nodes_a": keep.sb("nodes_a", [P, NP]), "big": keep.sb("big", [P, 14 * K]),
            "landed": [keep.sem(f"landed{q}") for q in range(SLOTS)],
            "landed_at": [0] * SLOTS,
        }
        t["nodes_b"] = t["big"][:, 13 * K - NP:13 * K]
        t["row"] = t["big"][:, 13 * K:14 * K].bitcast(I32)
        t["link_m"], t["link_s"] = (t["big"][0:G * H, 13 * K + a * K // 2:13 * K + (a + 1) * K // 2]
                                    for a in range(2))
        d = {
            "xpad": nc.dram_tensor("xpad", (NP, D), FP32).ap(),
            "tiles": nc.dram_tensor("tiles", (2, K), I32).ap(),
            "xt": nc.dram_tensor("xt", (NP, R * D), FP32).ap(),
            "q": nc.dram_tensor("q", (NP, D), FP32).ap(),
            "v": nc.dram_tensor("v", (NP, D), FP32).ap(),
            "exp": nc.dram_tensor("exp", (K * H, P), FP32).ap(),
            "targets": nc.dram_tensor("targets", (K * P,), BF16).ap(),
            "tile_marks": nc.dram_tensor("tile_marks", (K, MARKS), BF16).ap(),
            "marks": nc.dram_tensor("marks", (K * H, MARKS), BF16).ap(),
            "keys": nc.dram_tensor("keys", (K * 2,), FP32).ap(),
            "xl": nc.dram_tensor("xl", (NP, D), FP32).ap(),
            "sums": [nc.dram_tensor(f"sums{r}", (NP, D), FP32).ap() for r in range(REP)],
        }

        done = []

        def stage(f, *args):
            done.append(f)
            with ExitStack() as kept:
                with ExitStack() as s:
                    m = Memory(nc, s, f"stage{len(done)}_")
                    m.sem_stack = kept
                    f(nc, m, t, *args)
                for sem in m.sems:
                    nc.gpsimd.sem_clear(sem)
                nc.all_engine_barrier()

        stage(prepare_edges, src, dst, rel, x, d)
        stage(relation_table, d, w1, sl1, b1, True)
        stage(aggregate, d, True)
        stage(relation_table, d, w2, sl1, b1, False)
        stage(aggregate, d, False)
        stage(project, d, sl2, b2, wq, wk, wv, bq, bk, bv, g1, be1)
        stage(score, d, curv, wc, bc)
        stage(combine, d)
        stage(scatter, d)
        stage(finish, d, wo, bo, g2, be2, wf1, bf1, wf2, bf2, out)


_INS = ["x", "src", "dst", "edge_attr_128", "edge_type_8",
        "L0_gnn_w1", "L0_gnn_sl1", "L0_gnn_b1", "L0_gnn_w2", "L0_gnn_sl2", "L0_gnn_b2",
        "L1_gnn_Wq", "L1_gnn_bq", "L1_gnn_Wk", "L1_gnn_bk", "L1_gnn_Wv", "L1_gnn_bv",
        "L1_gnn_Wo", "L1_gnn_bo", "L1_gnn_Wc", "L1_gnn_bc", "L1_gnn_W1", "L1_gnn_b1",
        "L1_gnn_W2", "L1_gnn_b2", "L1_gnn_g1", "L1_gnn_be1", "L1_gnn_g2", "L1_gnn_be2"]


def kernel(**inputs):
    import numpy as _np
    import concourse.bacc as _bacc
    from concourse import mybir as _mybir
    from concourse.bass_utils import run_bass_kernel_spmd as _run

    nc = _bacc.Bacc("TRN2", target_bir_lowering=False, num_devices=1)
    arrays, args = {}, []
    for name in _INS:
        a = _np.ascontiguousarray(inputs[name])
        arrays[f"in_{name}_dram"] = a
        args.append(nc.dram_tensor(f"in_{name}_dram", a.shape, _mybir.dt.from_np(a.dtype), kind="ExternalInput").ap())
    args.append(nc.dram_tensor("out_0_dram", (N, D), _mybir.dt.float32, kind="ExternalOutput").ap())
    build(nc, *args)
    r = _run(nc, [arrays], core_ids=[0])
    return r.results[0]["out_0_dram"]
```
